# Optimizing a Trainium2 kernel written in Bass

```python
import numpy as np
import jax
import jax.numpy as jnp

def _softmax(x, axis=-1):
    return jax.nn.softmax(x, axis=axis)

def _gelu(x):
    return jax.nn.gelu(x, approximate=True)

def _silu(x):
    return jax.nn.silu(x)

def _sigmoid(x):
    return jax.nn.sigmoid(x)

def _layernorm(x, axis=-1, eps=1e-05):
    m = jnp.mean(x, axis=axis, keepdims=True)
    v = jnp.var(x, axis=axis, keepdims=True)
    return (x - m) / jnp.sqrt(v + eps)

def _scatter_add(tgt, idx, src, axis=0):
    return tgt.at[idx].add(src)

def _segment_sum(src, seg, n):
    return jax.ops.segment_sum(src, seg, n)
kernel_name = 'mk_adaln_d1_jaxref_r4_b22d1f'

def setup_inputs(seed: int=0):
    np.random.seed(seed)
    _w = jnp.asarray

    def _L0_attn_setup():
        import jax, jax.numpy as jnp
        import numpy as np
        IGNORE = -100000.0
        key = jax.random.key(seed)
        ks = jax.random.split(key, 5)
        b, s, d_model = (4, 512, 512)
        n_q, n_kv, d_head = (32, 8, 64)
        std = 0.02
        return {'normalized_resid_pre': jax.random.normal(ks[0], (b, s, d_model), jnp.float32), 'W_Q': jax.random.normal(ks[1], (n_q, d_model, d_head), jnp.float32) * std, 'W_K': jax.random.normal(ks[2], (n_kv, d_model, d_head), jnp.float32) * std, 'W_V': jax.random.normal(ks[3], (n_kv, d_model, d_head), jnp.float32) * std, 'W_O': jax.random.normal(ks[4], (n_kv, d_head, d_model), jnp.float32) * std}
    _L0_attn_in = _L0_attn_setup()

    def _L0_ffn_setup():
        import jax, jax.numpy as jnp
        import numpy as np
        B, S, H, E, D, K = (2, 512, 512, 8, 512, 2)
        key = jax.random.key(seed)
        ks = jax.random.split(key, 4)
        return {'x': jax.random.normal(ks[0], (B, S, H), jnp.float32), 'router_w': jax.random.normal(ks[1], (H, E), jnp.float32) / np.sqrt(H).astype(np.float32), 'router_b': jnp.zeros((E,), jnp.float32), 'expert_w': jax.random.normal(ks[2], (E, H, D), jnp.float32) / np.sqrt(H).astype(np.float32), 'expert_b': jnp.zeros((E, D), jnp.float32), 'out_w': jax.random.normal(ks[3], (D, D), jnp.float32) / np.sqrt(D).astype(np.float32), 'out_b': jnp.zeros((D,), jnp.float32)}
    _L0_ffn_in = _L0_ffn_setup()
    _L0_c = _w((lambda *s: np.random.randn(*s).astype(np.float32) * 0.05)(1, 512))
    _L0_wmod = _w((lambda *s: np.random.randn(*s).astype(np.float32) * 0.05)(512, 6 * 512) * 512 ** (-0.5))
    _d = {'L0_attn_normalized_resid_pre': _L0_attn_in['normalized_resid_pre'], 'L0_attn_W_Q': _L0_attn_in['W_Q'], 'L0_attn_W_K': _L0_attn_in['W_K'], 'L0_attn_W_V': _L0_attn_in['W_V'], 'L0_attn_W_O': _L0_attn_in['W_O'], 'L0_ffn_router_w': _L0_ffn_in['router_w'], 'L0_ffn_router_b': _L0_ffn_in['router_b'], 'L0_ffn_expert_w': _L0_ffn_in['expert_w'], 'L0_ffn_expert_b': _L0_ffn_in['expert_b'], 'L0_ffn_out_w': _L0_ffn_in['out_w'], 'L0_ffn_out_b': _L0_ffn_in['out_b'], 'L0_c': _L0_c, 'L0_wmod': _L0_wmod}
    _x0 = _d['L0_attn_normalized_resid_pre']
    _d['L0_attn_normalized_resid_pre'] = jax.random.normal(jax.random.fold_in(jax.random.key(seed), 1), (1, 4096, 512), dtype=_x0.dtype)
    del _x0
    return _d

def reference(L0_attn_normalized_resid_pre, L0_attn_W_Q, L0_attn_W_K, L0_attn_W_V, L0_attn_W_O, L0_ffn_router_w, L0_ffn_router_b, L0_ffn_expert_w, L0_ffn_expert_b, L0_ffn_out_w, L0_ffn_out_b, L0_c, L0_wmod):

    def _L0_attn_ref(normalized_resid_pre, W_Q, W_K, W_V, W_O):
        import jax, jax.numpy as jnp
        import numpy as np
        IGNORE = -100000.0
        x = normalized_resid_pre
        b, s, _ = x.shape
        n_kv, d_head = (W_K.shape[0], W_K.shape[2])
        n_q = W_Q.shape[0]
        g = n_q // n_kv
        q = jnp.einsum('bpd,hdk->bphk', x, W_Q)
        k = jnp.einsum('bpd,ndk->bpnk', x, W_K)
        v = jnp.einsum('bpd,ndk->bpnk', x, W_V)
        gq = q.reshape(b, s, n_kv, g, d_head).transpose(0, 1, 3, 2, 4)
        scores = jnp.einsum('bqgnh,bknh->bnqk', gq, k) / jnp.sqrt(jnp.float32(d_head))
        causal = jnp.triu(jnp.ones((s, s), dtype=bool), k=1)
        scores = jnp.where(causal, IGNORE, scores)
        pattern = jax.nn.softmax(scores, axis=-1)
        z = jnp.einsum('bknh,bnqk->bqnh', v, pattern)
        attn_out = jnp.einsum('bqnh,nhd->bqd', z, W_O)
        return attn_out

    def _L0_ffn_ref(x, router_w, router_b, expert_w, expert_b, out_w, out_b):
        import jax, jax.numpy as jnp
        import numpy as np
        B, S, H, E, D, K = (2, 512, 512, 8, 512, 2)
        num_experts = expert_w.shape[0]
        router_logits = jnp.einsum('bsh,he->bse', x, router_w) + router_b
        router_probs = jax.nn.softmax(router_logits, axis=-1)
        top_k_probs, top_k_indices = jax.lax.top_k(router_probs, K)
        top_k_probs = top_k_probs / jnp.sum(top_k_probs, axis=-1, keepdims=True)
        onehot = jax.nn.one_hot(top_k_indices, num_experts, dtype=x.dtype)
        gates = jnp.einsum('bsk,bske->bse', top_k_probs, onehot)
        expert_out = jax.nn.gelu(jnp.einsum('bsh,ehd->ebsd', x, expert_w) + expert_b[:, None, None, :])
        combined = jnp.einsum('bse,ebsd->bsd', gates, expert_out)
        return jnp.einsum('bsd,df->bsf', combined, out_w) + out_b
    x = L0_attn_normalized_resid_pre
    mod = (_silu(L0_c) @ L0_wmod).reshape(L0_c.shape[0], 6, 1, -1)
    sa, ca, ga, sb, cb, gb = (mod[:, 0], mod[:, 1], mod[:, 2], mod[:, 3], mod[:, 4], mod[:, 5])
    ga = (2 * (ga >= 0) - 1) * jnp.maximum(jnp.abs(ga), 0.25)
    gb = (2 * (gb >= 0) - 1) * jnp.maximum(jnp.abs(gb), 0.25)
    h = _layernorm(x, axis=-1) * (1 + ca) + sa
    x = x + ga * _L0_attn_ref(h, L0_attn_W_Q, L0_attn_W_K, L0_attn_W_V, L0_attn_W_O)
    h = _layernorm(x, axis=-1) * (1 + cb) + sb
    x = x + gb * _L0_ffn_ref(h, L0_ffn_router_w, L0_ffn_router_b, L0_ffn_expert_w, L0_ffn_expert_b, L0_ffn_out_w, L0_ffn_out_b)
    return x

_drawn_inputs = setup_inputs


def setup_inputs(seed=0):
    import zlib

    import numpy as np

    out = dict(_drawn_inputs(seed))
    spreads = {'L0_ffn_router_b': (0.0, 1.677),
     'L0_ffn_expert_b': (0.0, 2.0),
     'L0_ffn_out_b': (0.0, 1.078)}
    factors = {'L0_attn_W_Q': 8.0, 'L0_attn_W_K': 8.0, 'L0_attn_W_V': 8.0, 'L0_attn_W_O': 8.0}
    for name, (base, spread) in spreads.items():
        noise = np.random.default_rng([zlib.crc32(name.encode()), seed]).standard_normal(out[name].shape)
        drawn = base * np.exp(spread * noise) if base else spread * noise
        out[name] = jnp.asarray(drawn.astype(out[name].dtype))
    for name, factor in factors.items():
        out[name] = (out[name] * factor).astype(out[name].dtype)
    return out
```

```python
import math
from contextlib import ExitStack

import concourse.bass as bass
from concourse import mybir

F32 = mybir.dt.float32
F32R = mybir.dt.float32r
BF16 = mybir.dt.bfloat16
FP16 = mybir.dt.float16
ALU = mybir.AluOpType
ACT = mybir.ActivationFunctionType
AX = mybir.AxisListType

P = 128
S = 4096
D = 512
C = D // P
BLK = 512
NB = S // BLK
TPB = BLK // P
HEADS = 8
GROUP = 4
DH = 64
PAIRS = HEADS // 2
KT = S // P
E = 8
EPS = 1e-5
VHI, VMID, VONE, VLO = 0, DH, 2 * DH, 2 * DH + 1
VW = 3 * DH + 2
NEG = -1e30
SCALE = 1.0 / math.sqrt(DH)
P_SHIFT = 4 * math.log(2.0) / SCALE


def three_terms(pe, out, s_hi, s_lo, m_hi, m_lo):
    for c in range(C):
        for n, (s, m) in enumerate(((s_hi, m_hi), (s_hi, m_lo), (s_lo, m_hi))):
            last = pe.matmul(out, s(c), m(c), start=(c == 0 and n == 0),
                             stop=(c == C - 1 and n == 2))
    return last


def project_phase(nc, io, sh):
    with ExitStack() as ctx:
        def sb(name, shape, dt):
            return ctx.enter_context(nc.sbuf_tensor(name, shape, dt))

        def sem(name):
            return ctx.enter_context(nc.semaphore(name))

        RAW = 4
        raw = [sb(f"raw{i}", [P, C, 512], F32) for i in range(RAW)]
        wqh, wql, wkh, wkl, wvh, wvl = (sb(n, [P, C, 512], F32R)
                                        for n in ("wqh", "wql", "wkh", "wkl", "wvh", "wvl"))
        wsum = [sb(f"wsum{i}", [P, 512], F32) for i in range(4)]
        craw = sb("craw", [P, C], F32)
        cexp = sb("cexp", [P, C], F32)
        cden = sb("cden", [P, C], F32)
        cinv = sb("cinv", [P, C], F32)
        csilu = sb("csilu", [P, C], F32)
        cwide = sb("cwide", [P, C, P], F32)
        mrow = [sb(f"mrow{i}", [P, 512], F32) for i in range(4)]
        gneg, gabs, gsgn = (sb(n, [P, 512], F32) for n in ("gneg", "gabs", "gsgn"))
        sa = sb("sa", [P, C], F32)
        ca1 = sb("ca1", [P, C], F32)
        xb = [sb(f"xb{i}", [P, TPB, D], F32) for i in range(2)]
        bst = sb("bst", [P, TPB, 6], F32)
        mv = sb("mv", [P, TPB, 2], F32)
        sd = sb("sd", [P, TPB], F32)
        rstd = sb("rstd", [P, TPB], F32)
        xhat = sb("xhat", [P, TPB, D], F32)
        hf = [sb(f"hf{i}", [P, BLK], F32) for i in range(2)]
        hh = [sb(f"hh{i}", [P, C, BLK], F32R) for i in range(2)]
        hl = [sb(f"hl{i}", [P, C, BLK], F32R) for i in range(2)]
        QR = 4
        qh = [sb(f"qh{i}", [P, BLK], F32R) for i in range(QR)]
        ql = [sb(f"ql{i}", [P, BLK], F32R) for i in range(QR)]
        VR = 2
        vt = [sb(f"vt{i}", [P, HEADS, VW], BF16) for i in range(VR)]
        vr = [sb(f"vr{i}", [P, HEADS, DH], F32) for i in range(VR)]
        tp = [ctx.enter_context(nc.psum_tensor(f"tp{i}", [P, 512], F32)) for i in range(2)]
        NACC = 6
        acc = [ctx.enter_context(nc.psum_tensor(f"acc{i}", [P, 512], F32)) for i in range(NACC)]

        c_in = sem("c_in")
        x_in = [sem(f"x_in{i}") for i in range(2)]
        raw_in = [sem(f"raw_in{i}") for i in range(RAW)]
        raw_free = [sem(f"raw_free{i}") for i in range(RAW)]
        const_done = sem("const_done")
        c_exp = sem("c_exp")
        c_chain = sem("c_chain")
        cwide_done = sem("cwide_done")
        mod_mm = sem("mod_mm")
        mod_row = sem("mod_row")
        col_mm = sem("col_mm")
        col_done = sem("col_done")
        w_hi = sem("w_hi")
        w_lo = sem("w_lo")
        w_half = sem("w_half")
        w_sum = sem("w_sum")
        bn_done = sem("bn_done")
        bn_seen = sem("bn_seen")
        mv_done = sem("mv_done")
        sd_done = sem("sd_done")
        rstd_done = sem("rstd_done")
        xhat_done = sem("xhat_done")
        tp_done = sem("tp_done")
        h_high = sem("h_high")
        h_low = sem("h_low")
        acc_done = sem("acc_done")
        hi_out = sem("hi_out")
        acc_read = sem("acc_read")
        v_mid = sem("v_mid")
        v_ready = sem("v_ready")
        qk_sent = [sem(f"qk_sent{i}") for i in range(QR)]
        v_sent = [sem(f"v_sent{i}") for i in range(VR)]
        g_chain = sem("g_chain")

        NQK = 2 * PAIRS
        NIT = NQK + TPB
        HALF = NIT // 2
        PIECES = ([("mod", 0), ("mod", 1), ("wk", 0), ("wv", 0)]
                  + [("wq", c) for c in range(C)] + [("mod", m) for m in range(2, 6)])
        AT = {p: n for n, p in enumerate(PIECES)}

        def slot(kind, i=0):
            n = AT[kind, i]
            return n % RAW, 16 * (n // RAW + 1)

        block = ctx.enter_context(nc.Block())

        @block.sync
        def _(sp):
            sp.dma_start(craw[:, :], io.c).then_inc(c_in, 16)
            sp.dma_start(xb[0][:, :, :], io.x[0]).then_inc(x_in[0], 16)
            for n, (kind, i) in enumerate(PIECES):
                if n >= RAW:
                    sp.wait_ge(raw_free[n % RAW], n // RAW)
                src = {"mod": io.wmod, "wk": io.wk, "wv": io.wv, "wq": io.wq}[kind][i]
                sp.dma_start(raw[n % RAW][:, :, :], src).then_inc(raw_in[n % RAW], 16)
                if n == 3:
                    sp.dma_start(xb[1][:, :, :], io.x[1]).then_inc(x_in[1], 16)

            def stores(b, s, ahead):
                if ahead:
                    sp.wait_ge(xhat_done, b + 1)
                    sp.dma_start(xb[s][:, :, :], io.x[b + 2]).then_inc(x_in[s], 16)
                for n in range(NQK):
                    dst = io.q_scr if n < PAIRS else io.k_scr
                    sp.wait_ge(acc_read, NACC + b * NIT + n + 1)
                    for part, t in enumerate((qh, ql)):
                        sp.dma_start(dst[part, n % PAIRS, :, bass.ds(b * BLK, BLK)],
                                     t[n % QR][:, :].bitcast(F32)).then_inc(qk_sent[n % QR], 16)
                for t in range(TPB):
                    sp.wait_ge(v_ready, b * TPB + t + 1)
                    sp.dma_start(io.v_scr[:, :, b * TPB + t, :], vt[t % VR][:, :, :])\
                      .then_inc(v_sent[t % VR], 16)

            with sp.Fori(0, NB // 2 - 1) as it:
                for s in range(2):
                    stores(2 * it + s, s, True)
            for s in range(2):
                stores(NB - 2 + s, s, False)
            for i in range(QR):
                sp.wait_ge(qk_sent[i], 32 + NB * (NQK // QR) * 32)
            for i in range(VR):
                sp.wait_ge(v_sent[i], 16 + NB * (TPB // VR) * 16)

        @block.gpsimd
        def _(pool):
            for m in (sh.identf, sh.identb, sh.mask_qk, sh.mask_kq):
                pool.memset(m[:, :], 0.0).then_inc(const_done, 1)
            pool.memset(sh.eps[:, :], EPS).then_inc(const_done, 1)
            for t in vt:
                pool.memset(t[:, :, :], 1.0).then_inc(const_done, 1)
            pool.wait_ge(const_done, 5 + VR)
            for m in (sh.identf, sh.identb):
                pool.affine_select(out=m[:, :], in_=m[:, :], compare_op=ALU.not_equal, fill=1.0,
                                   base=0, pattern=[[-1, P]], channel_multiplier=1)\
                    .then_inc(const_done, 1)
            pool.affine_select(out=sh.mask_qk[:, :], in_=sh.mask_qk[:, :], compare_op=ALU.is_ge,
                               fill=NEG, base=0, pattern=[[-1, P]], channel_multiplier=1)\
                .then_inc(const_done, 1)
            pool.affine_select(out=sh.mask_kq[:, :], in_=sh.mask_kq[:, :], compare_op=ALU.is_ge,
                               fill=NEG, base=0, pattern=[[1, P]], channel_multiplier=-1)\
                .then_inc(const_done, 1)

        CONST = 9 + VR

        @block.scalar
        def _(act):
            act.sem_inc(h_high, 2)
            for i in range(QR):
                act.sem_inc(qk_sent[i], 32)
            for i in range(VR):
                act.sem_inc(v_sent[i], 16)
            act.wait_ge(c_in, 16)
            act.activation(cexp[:, :], craw[:, :], ACT.Exp, scale=-1.0).then_inc(c_exp, 1)
            act.wait_ge(const_done, CONST)

            def std_dev(b):
                act.wait_ge(mv_done, b + 1)
                act.activation(sd[:, :], mv[:, :, 1], ACT.Sqrt, bias=sh.eps[:, 0:1])\
                   .then_inc(sd_done, 1)

            def modulate(b, s):
                for c in range(C):
                    act.wait_ge(tp_done, b * C + c + 1)
                    act.wait_ge(h_low, b * C + c + 1)
                    act.activation(hf[c % 2][:, :], tp[c % 2][:, :], ACT.Identity,
                                   scale=ca1[:, c:c + 1], bias=sa[:, c:c + 1])
                    act.activation(hh[s][:, c, :], tp[c % 2][:, :], ACT.Identity,
                                   scale=ca1[:, c:c + 1], bias=sa[:, c:c + 1]).then_inc(h_high, 1)

            def high_parts(b, lo, hi):
                for n in range(lo, hi):
                    act.wait_ge(acc_done, b * NIT + n + 1)
                    if n < NQK:
                        k = n % QR
                        act.wait_ge(qk_sent[k], (b * (NQK // QR) + n // QR) * 32 + 32)
                        act.activation(qh[k][:, :], acc[n % NACC][:, :], ACT.Copy)\
                           .then_inc(hi_out, 1)
                    else:
                        t = n - NQK
                        k = t % VR
                        act.wait_ge(v_sent[k], (b * (TPB // VR) + t // VR) * 16 + 16)
                        act.activation(vt[k][:, :, VHI:VHI + DH],
                                       acc[n % NACC][:, :].rearrange("p (h d) -> p h d", h=HEADS),
                                       ACT.Copy).then_inc(hi_out, 1)
                        act.wait_ge(acc_read, NACC + b * NIT + n + 1)
                        act.activation(vt[k][:, :, VMID:VMID + DH], vr[k][:, :, :], ACT.Copy)\
                           .then_inc(v_mid, 1)

            std_dev(0)
            act.wait_ge(col_done, 2)
            modulate(0, 0)
            for w, kind in ((wkh, "wk"), (wvh, "wv")):
                k, n = slot(kind)
                act.wait_ge(raw_in[k], n)
                act.activation(w[:, :, :], raw[k][:, :, :], ACT.Copy).then_inc(w_hi, 1)
            for c in range(C):
                act.wait_ge(w_sum, c + 1)
                act.activation(wqh[:, c, :], wsum[2 + c % 2][:, :], ACT.Copy).then_inc(w_hi, 1)

            def step(b, s, ahead):
                if ahead:
                    std_dev(b + 1)
                high_parts(b, 0, HALF)
                if ahead:
                    modulate(b + 1, 1 - s)
                high_parts(b, HALF, NIT)

            with act.Fori(0, NB // 2 - 1) as it:
                for s in range(2):
                    step(2 * it + s, s, True)
            for s in range(2):
                step(NB - 2 + s, s, s == 0)

        @block.vector
        def _(dve):
            dve.sem_inc(acc_read, NACC)
            dve.sem_inc(h_low, 2)

            def layer_norm(b, s, x_count):
                dve.wait_ge(x_in[s], x_count)
                for t in range(TPB):
                    dve.bn_stats(bst[:, t, :], xb[s][:, t, :]).then_inc(bn_done, 1)
                dve.wait_ge(bn_done, b * TPB + TPB)
                dve.sem_inc(bn_seen, 1)
                for t in range(TPB):
                    last = dve.bn_aggr(mv[:, t, :], bst[:, t, :])
                last.then_inc(mv_done, 1)
                dve.wait_ge(sd_done, b + 1)
                dve.reciprocal(rstd[:, :], sd[:, :]).then_inc(rstd_done, 1)
                dve.wait_ge(rstd_done, b + 1)
                if not isinstance(b, int) or b > 0:
                    dve.wait_ge(tp_done, b * C)
                for t in range(TPB):
                    last = dve.tensor_scalar(xhat[:, t, :], xb[s][:, t, :], mv[:, t, 0:1],
                                             rstd[:, t:t + 1], ALU.subtract, ALU.mult)
                last.then_inc(xhat_done, 1)

            def low_h(b, s):
                for c in range(C):
                    dve.wait_ge(h_high, 2 + b * C + c + 1)
                    dve.tensor_tensor(hl[s][:, c, :], hf[c % 2][:, :],
                                      hh[s][:, c, :].bitcast(F32), ALU.subtract)\
                       .then_inc(h_low, 1)

            def low_parts(b, lo, hi):
                for n in range(lo, hi):
                    dve.wait_ge(hi_out, b * NIT + n + 1)
                    if n < NQK:
                        k = n % QR
                        dve.tensor_tensor(ql[k][:, :], acc[n % NACC][:, :],
                                          qh[k][:, :].bitcast(F32), ALU.subtract)\
                           .then_inc(acc_read, 1)
                    else:
                        t = n - NQK
                        k = t % VR
                        dve.tensor_tensor(vr[k][:, :, :],
                                          acc[n % NACC][:, :].rearrange("p (h d) -> p h d",
                                                                        h=HEADS),
                                          vt[k][:, :, VHI:VHI + DH], ALU.subtract)\
                           .then_inc(acc_read, 1)
                        dve.wait_ge(v_mid, b * TPB + t + 1)
                        dve.tensor_tensor(vt[k][:, :, VLO:VLO + DH], vr[k][:, :, :],
                                          vt[k][:, :, VMID:VMID + DH], ALU.subtract)\
                           .then_inc(v_ready, 1)

            dve.wait_ge(c_exp, 1)
            dve.tensor_scalar_add(cden[:, :], cexp[:, :], 1.0).then_inc(c_chain, 1)
            dve.wait_ge(c_chain, 1)
            dve.reciprocal(cinv[:, :], cden[:, :]).then_inc(c_chain, 1)
            dve.wait_ge(c_chain, 2)
            dve.tensor_tensor(csilu[:, :], craw[:, :], cinv[:, :], ALU.mult).then_inc(c_chain, 1)
            dve.wait_ge(c_chain, 3)
            for c in range(C):
                last = dve.tensor_copy(cwide[:, c, :], csilu[:, c:c + 1].broadcast_to([P, P]))
            last.then_inc(cwide_done, 1)
            layer_norm(0, 0, 16)

            def mod_sections(ms, bank0, cols):
                for i, m in enumerate(ms):
                    dve.wait_ge(mod_mm, m + 1)
                    dve.tensor_copy(mrow[i][:, :], acc[bank0 + i][:, :]).then_inc(mod_row, 1)
                for i, (col, dst, add) in enumerate(cols):
                    dve.wait_ge(col_mm, col + 1)
                    dve.tensor_scalar_add(dst[:, :], acc[bank0 + len(ms) + i][:, ::P], add)\
                       .then_inc(col_done, 1)

            mod_sections([0, 1], 0, [(0, sa, 0.0), (1, ca1, 1.0)])
            low_h(0, 0)
            for w, wh, kind in ((wkl, wkh, "wk"), (wvl, wvh, "wv")):
                k, n = slot(kind)
                dve.wait_ge(raw_in[k], n)
                dve.wait_ge(w_hi, 1 if kind == "wk" else 2)
                dve.tensor_tensor(w[:, :, :], raw[k][:, :, :], wh[:, :, :].bitcast(F32),
                                  ALU.subtract).then_inc(raw_free[k], 1)
            for c in range(C):
                k, n = slot("wq", c)
                dve.wait_ge(raw_in[k], n)
                g = raw[k][:, :, :].rearrange("p a (b g d) -> p (a b) g d", g=GROUP, d=DH)

                def out(t):
                    return t[:, :].rearrange("p (n d) -> p n d", d=DH)

                dve.tensor_tensor(out(wsum[0]), g[:, :, 0, :], g[:, :, 1, :], ALU.add)\
                   .then_inc(w_half, 1)
                dve.tensor_tensor(out(wsum[1]), g[:, :, 2, :], g[:, :, 3, :], ALU.add)\
                   .then_inc(raw_free[k], 1)
                dve.wait_ge(w_half, c + 1)
                dve.wait_ge(raw_free[k], n // 16)
                dve.tensor_tensor(wsum[2 + c % 2][:, :], wsum[0][:, :], wsum[1][:, :], ALU.add)\
                   .then_inc(w_sum, 1)
                dve.wait_ge(w_sum, c + 1)
                dve.wait_ge(w_hi, 3 + c)
                dve.tensor_tensor(wql[:, c, :], wsum[2 + c % 2][:, :],
                                  wqh[:, c, :].bitcast(F32), ALU.subtract).then_inc(w_lo, 1)

            def step(b, s, ahead, x_count):
                if ahead:
                    layer_norm(b + 1, 1 - s, x_count)
                low_parts(b, 0, HALF)
                if ahead:
                    low_h(b + 1, 1 - s)
                low_parts(b, HALF, NIT)

            with dve.Fori(0, NB // 2 - 1) as it:
                step(2 * it, 0, True, it * 16 + 16)
                step(2 * it + 1, 1, True, it * 16 + 32)
            step(NB - 2, 0, True, NB // 2 * 16)
            step(NB - 1, 1, False, 0)

            mod_sections([2, 3, 4, 5], 0, [(2, sh.sb, 0.0), (3, sh.cb1, 1.0)])
            n = 0
            for i, dst in ((0, sh.ga), (3, sh.gb)):
                g = mrow[i]
                dve.wait_ge(mod_row, 3 + i)
                dve.tensor_scalar(gneg[:, :], g[:, :], -1.0, None, ALU.mult).then_inc(g_chain, 1)
                dve.tensor_scalar(gsgn[:, :], g[:, :], 0.0, 2.0, ALU.is_ge, ALU.mult)\
                   .then_inc(g_chain, 1)
                dve.wait_ge(g_chain, n + 2)
                dve.tensor_tensor(gabs[:, :], g[:, :], gneg[:, :], ALU.max).then_inc(g_chain, 1)
                dve.wait_ge(g_chain, n + 3)
                dve.tensor_scalar(gneg[:, :], gabs[:, :], 0.25, None, ALU.max)\
                   .then_inc(g_chain, 1)
                dve.wait_ge(g_chain, n + 4)
                dve.scalar_tensor_tensor(dst[:, :], gsgn[:, :], -1.0, gneg[:, :], ALU.add,
                                         ALU.mult).then_inc(g_chain, 1)
                n += 5
                dve.wait_ge(g_chain, n)

        @block.tensor
        def _(pe):
            def mod_section(m, bank):
                k, n = slot("mod", m)
                pe.wait_ge(raw_in[k], n)
                for c in range(C):
                    last = pe.matmul(acc[bank][:, :], cwide[:, c, :], raw[k][:, c, :],
                                     start=(c == 0), stop=(c == C - 1))
                last.then_inc(mod_mm, 1)
                pe.wait_ge(mod_mm, m + 1)
                pe.sem_inc(raw_free[k], 1)

            def column(row, bank, row_count):
                pe.wait_ge(mod_row, row_count)
                for c in range(C):
                    last = pe.transpose(acc[bank][:, c * P:(c + 1) * P],
                                        mrow[row][:, c * P:(c + 1) * P], sh.identf[:, :])
                last.then_inc(col_mm, 1)

            def transposes(b):
                pe.wait_ge(xhat_done, b + 1)
                for c in range(C):
                    pe.wait_ge(h_high, b * C + c + 1)
                    for t in range(TPB):
                        last = pe.transpose(tp[c % 2][:, t * P:(t + 1) * P],
                                            xhat[:, t, c * P:(c + 1) * P], sh.identf[:, :])
                    last.then_inc(tp_done, 1)

            def products(b, s, lo, hi):
                pe.wait_ge(h_low, 2 + (b + 1) * C)
                for n in range(lo, hi):
                    pe.wait_ge(acc_read, b * NIT + n + 1)
                    if n < NQK:
                        wh, wl = (wqh, wql) if n < PAIRS else (wkh, wkl)
                        j = n % PAIRS * P
                        last = three_terms(pe, acc[n % NACC][:, :],
                                           lambda c: wh[:, c, j:j + P], lambda c: wl[:, c, j:j + P],
                                           lambda c: hh[s][:, c, :], lambda c: hl[s][:, c, :])
                    else:
                        j = (n - NQK) * P
                        last = three_terms(pe, acc[n % NACC][:, :],
                                           lambda c: hh[s][:, c, j:j + P],
                                           lambda c: hl[s][:, c, j:j + P],
                                           lambda c: wvh[:, c, :], lambda c: wvl[:, c, :])
                    last.then_inc(acc_done, 1)

            def step(b, s, ahead):
                products(b, s, 0, HALF)
                if ahead:
                    transposes(b + 1)
                products(b, s, HALF, NIT)

            pe.wait_ge(const_done, CONST)
            pe.wait_ge(cwide_done, 1)
            for m in range(2):
                mod_section(m, m)
            for m in range(2):
                column(m, 2 + m, m + 1)
            transposes(0)
            pe.wait_ge(col_done, 2)
            for kind in ("wk", "wv"):
                k, n = slot(kind)
                pe.wait_ge(raw_free[k], n // 16)
            pe.wait_ge(w_lo, C)
            with pe.Fori(0, NB // 2 - 1) as it:
                for s in range(2):
                    step(2 * it + s, s, True)
            for s in range(2):
                step(NB - 2 + s, s, s == 0)
            pe.wait_ge(acc_read, NACC + NB * NIT)
            for m in range(2, 6):
                mod_section(m, m - 2)
            column(1, 4, 4)
            column(2, 5, 5)


def attention_schedule():
    steps, first, last = [], [], []
    for head in range(2):
        for j in range(NB):
            u = head * NB + j
            first.append(len(steps))
            for g in range(2 * j):
                steps.append((u, head, j, [(2 * g, 0, 0), (2 * g + 1, BLK, 0)], 2 * BLK))
            steps.append((u, head, j, [(4 * j, 0, 0), (4 * j + 1, 4 * P, 1)], 7 * P))
            steps.append((u, head, j, [(4 * j + 2, 0, 2), (4 * j + 3, 2 * P, 3)], 3 * P))
            last.append(len(steps) - 1)
    units = len(first)

    def items(u):
        j = u % NB
        return [("max", u, q, kb) for q in range(TPB) for kb in range(j + 1)] + [("row", u)]

    ahead = items(0)
    todo = [(first[u] - 2, it) for u in range(1, units) for it in items(u)]
    todo = [(max(0, by), it) for by, it in todo]
    carried = [[] for _ in steps]
    for g in reversed(range(len(steps))):
        while todo and todo[-1][0] >= g and (len(carried[g]) < CAP or g == 0):
            carried[g].insert(0, todo.pop()[1])
    assert not todo
    return steps, first, last, ahead, carried


CAP = 3


def attend_phase(nc, io, sh):
    STEPS, FIRST, LAST, AHEAD, CARRIED = attention_schedule()
    NG = len(STEPS)
    NU = len(FIRST)
    NI = len(AHEAD) + sum(map(len, CARRIED))
    LAG = 2
    with ExitStack() as ctx:
        def sb(name, shape, dt):
            return ctx.enter_context(nc.sbuf_tensor(name, shape, dt))

        def sem(name):
            return ctx.enter_context(nc.semaphore(name))

        kk, k1, qq, q1 = ([sb(f"{n}{i}", [P, S], F32R) for i in range(2)]
                          for n in ("kk", "k1_", "qq", "q1_"))
        v = [sb(f"v{i}", [P, KT, VW], BF16) for i in range(2)]
        PR = 3
        p32 = [sb(f"p32_{i}", [P, 2 * BLK], F32) for i in range(PR)]
        phi = [sb(f"phi{i}", [P, 2 * BLK], FP16) for i in range(PR)]
        plo = [sb(f"plo{i}", [P, 2 * BLK], FP16) for i in range(PR)]
        mpart = [sb(f"mpart{i}", [P, TPB, NB], F32) for i in range(2)]
        m4 = [sb(f"m4_{i}", [P, TPB], F32) for i in range(2)]
        zs = [sb(f"zs{i}", [P, TPB, VW], F32) for i in range(2)]
        rl = [sb(f"rl{i}", [P, TPB], F32) for i in range(2)]
        zt = [sb(f"zt{i}", [P, TPB, DH], F32) for i in range(2)]
        zo = [sb(f"zo{i}", [P, TPB, DH], F32) for i in range(2)]
        st = [ctx.enter_context(nc.psum_tensor(f"st{i}", [P, 2 * BLK], F32)) for i in range(2)]
        zp = ctx.enter_context(nc.psum_tensor("zp", [P, TPB, 256], F32))
        sq = [ctx.enter_context(nc.psum_tensor(f"sq{i}", [P, BLK], F32)) for i in range(2)]

        kqv_in = [sem(f"kqv_in{i}") for i in range(2)]
        fill_done = sem("fill_done")
        sq_done = sem("sq_done")
        sq_read = sem("sq_read")
        m4_done = sem("m4_done")
        st_done = sem("st_done")
        exp_done = sem("exp_done")
        plo_done = sem("plo_done")
        pv_done = sem("pv_done")
        z_copied = sem("z_copied")
        r_done = sem("r_done")
        z_chain = sem("z_chain")
        z_ready = sem("z_ready")
        z_sent = [sem(f"z_sent{i}") for i in range(2)]
        LOADS = 7

        block = ctx.enter_context(nc.Block())

        @block.sync
        def _(sp):
            def load(pair, i):
                rows = slice(i * DH, (i + 1) * DH)
                for dst, lo, src, part in ((kk, 0, io.k_scr, 0), (kk, DH, io.k_scr, 1),
                                           (qq, 0, io.q_scr, 0), (qq, DH, io.q_scr, 0),
                                           (k1, 0, io.k_scr, 0), (q1, 0, io.q_scr, 1)):
                    sp.dma_start(dst[i][lo:lo + DH, :].bitcast(F32), src[part, pair, rows, :])\
                      .then_inc(kqv_in[i], 16)
                sp.dma_start(v[i][:, :, :], io.v_scr[:, 2 * pair + i, :, :])\
                  .then_inc(kqv_in[i], 16)

            def store(pair, u):
                i, j = divmod(u, NB)
                sp.wait_ge(z_ready, 2 + pair * NU + u + 1)
                sp.dma_start(io.z_scr[j, :, :, bass.ds((2 * pair + i) * DH, DH)],
                             zo[u % 2][:, :, :]).then_inc(z_sent[u % 2], 16)

            for i in range(2):
                load(0, i)
            with sp.Fori(0, PAIRS - 1) as pair:
                for i in range(2):
                    for j in range(NB):
                        store(pair, i * NB + j)
                    load(pair + 1, i)
            for u in range(NU):
                store(PAIRS - 1, u)
            for i in range(2):
                sp.wait_ge(z_sent[i], 16 + PAIRS * NU // 2 * 16)

        @block.gpsimd
        def _(pool):
            pool.sem_inc(z_ready, 2)
            for i in range(2):
                pool.sem_inc(z_sent[i], 16)
                pool.memset(k1[i][DH:P, :].bitcast(F32), 0.0).then_inc(fill_done, 1)
                pool.memset(q1[i][DH:P, :].bitcast(F32), 0.0).then_inc(fill_done, 1)
            pool.wait_ge(fill_done, 4)
            for i in range(2):
                pool.memset(k1[i][DH:DH + 1, :].bitcast(F32), 1.0).then_inc(fill_done, 1)

            with pool.Fori(0, PAIRS) as pair:
                for u in range(NU):
                    k = u % 2
                    n = pair * NU + u
                    pool.wait_ge(z_copied, 1 + n + 1)
                    pool.tensor_tensor(zt[0][:, :, :], zs[k][:, :, VHI:VHI + DH],
                                       zs[k][:, :, VMID:VMID + DH], ALU.add).then_inc(z_chain, 1)
                    pool.wait_ge(z_chain, n * 2 + 1)
                    pool.tensor_tensor(zt[1][:, :, :], zt[0][:, :, :],
                                       zs[k][:, :, VLO:VLO + DH], ALU.add).then_inc(z_chain, 1)
                    pool.wait_ge(z_chain, n * 2 + 2)
                    pool.wait_ge(r_done, n + 1)
                    pool.wait_ge(z_sent[k], 16 * (pair * (NU // 2) + u // 2) + 16)
                    pool.tensor_tensor(zo[k][:, :, :], zt[1][:, :, :],
                                       rl[k][:, :].unsqueeze(2).broadcast_to([P, TPB, DH]),
                                       ALU.mult).then_inc(z_ready, 1)

        @block.scalar
        def _(act):
            act.sem_inc(exp_done, 2)
            act.sem_inc(z_copied, 1)
            with act.Fori(0, PAIRS) as pair:
                def copy_z(u):
                    act.wait_ge(pv_done, PR + pair * NG + LAST[u] + 1)
                    act.wait_ge(z_ready, pair * NU + u + 1)
                    act.activation(zs[u % 2][:, :, 0:VW - 1], zp[:, :, 0:VW - 1], ACT.Copy)\
                       .then_inc(z_copied, 1)

                for g, (u, head, j, tiles, width) in enumerate(STEPS):
                    act.wait_ge(st_done, pair * NG + g + 1)
                    act.wait_ge(pv_done, pair * NG + g + 1)
                    act.activation(phi[g % PR][:, 0:width], st[g % 2][:, 0:width], ACT.Exp,
                                   scale=SCALE)
                    act.activation(p32[g % PR][:, 0:width], st[g % 2][:, 0:width], ACT.Exp,
                                   scale=SCALE).then_inc(exp_done, 1)
                    if g - LAG in LAST:
                        copy_z(LAST.index(g - LAG))
                copy_z(NU - 1)

        @block.vector
        def _(dve):
            dve.sem_inc(sq_read, 2)
            dve.wait_ge(fill_done, 6)
            with dve.Fori(0, PAIRS) as pair:
                done = [0]

                def item(it):
                    n = done[0]
                    done[0] += 1
                    u = it[1]
                    head, j = divmod(u, NB)
                    dve.wait_ge(sq_done, pair * NI + n + 1)
                    if it[0] == "max":
                        q, kb = it[2:]
                        dve.reduce_max(mpart[u % 2][:, q, kb:kb + 1],
                                       sq[n % 2][:, 0:BLK if kb < j else (q + 1) * P],
                                       AX.X).then_inc(sq_read, 1)
                        if (q, kb) == (TPB - 1, j):
                            dve.wait_ge(sq_read, 2 + pair * NI + n + 1)
                            dve.reduce_max(m4[u % 2][:, :], mpart[u % 2][:, :, 0:j + 1], AX.X)\
                               .then_inc(m4_done, 1)
                    else:
                        dve.tensor_scalar(q1[head][DH:DH + 1, j * BLK:(j + 1) * BLK],
                                          sq[n % 2][0:1, :], -1.0, P_SHIFT, ALU.mult, ALU.add)\
                           .then_inc(sq_read, 1)

                def low_p(g):
                    width = STEPS[g][4]
                    dve.wait_ge(exp_done, 2 + pair * NG + g + 1)
                    dve.tensor_tensor(plo[g % PR][:, 0:width], p32[g % PR][:, 0:width],
                                      phi[g % PR][:, 0:width], ALU.subtract).then_inc(plo_done, 1)

                def inverse_sums(u):
                    dve.wait_ge(z_copied, 1 + pair * NU + u + 1)
                    dve.reciprocal(rl[u % 2][:, :], zs[u % 2][:, :, VONE]).then_inc(r_done, 1)

                for it in AHEAD:
                    item(it)
                for g in range(NG):
                    cut = (len(CARRIED[g]) + 1) // 2
                    for it in CARRIED[g][:cut]:
                        item(it)
                    if g > 0:
                        low_p(g - 1)
                    for it in CARRIED[g][cut:]:
                        item(it)
                    if g - LAG - 1 in LAST:
                        inverse_sums(LAST.index(g - LAG - 1))
                low_p(NG - 1)
                inverse_sums(NU - 1)

        @block.tensor
        def _(pe):
            pe.sem_inc(pv_done, PR)
            pe.wait_ge(fill_done, 6)
            with pe.Fori(0, PAIRS) as pair:
                done = [0]

                def item(it):
                    n = done[0]
                    done[0] += 1
                    u = it[1]
                    head, j = divmod(u, NB)
                    if it == ("max", head * NB, 0, 0):
                        pe.wait_ge(kqv_in[head], (pair + 1) * (LOADS * 16))
                    pe.wait_ge(sq_read, pair * NI + n + 1)
                    if it[0] == "max":
                        q, kb = it[2:]
                        width = BLK if kb < j else (q + 1) * P
                        last = pe.matmul(sq[n % 2][:, 0:width],
                                         qq[head][:, j * BLK + q * P:j * BLK + (q + 1) * P],
                                         kk[head][:, kb * BLK:kb * BLK + width],
                                         start=True, stop=kb < j)
                        if kb == j:
                            last = pe.matmul(sq[n % 2][:, width - P:width], sh.identb[:, :],
                                             sh.mask_qk[:, :], start=False, stop=True)
                    else:
                        pe.wait_ge(m4_done, pair * NU + u + 1)
                        for q in range(TPB):
                            last = pe.transpose(sq[n % 2][0:1, q * P:(q + 1) * P],
                                                m4[u % 2][:, q:q + 1], sh.identf[:, :])
                    last.then_inc(sq_done, 1)

                def scores(g, tile):
                    u, head, j, tiles, width = STEPS[g]
                    kt, col, q0 = tile
                    w = BLK - q0 * P
                    out = st[g % 2][:, col:col + w]
                    keys = slice(kt * P, (kt + 1) * P)
                    queries = slice(j * BLK + q0 * P, (j + 1) * BLK)
                    pe.matmul(out, kk[head][:, keys], qq[head][:, queries], start=True, stop=False)
                    last = pe.matmul(out, k1[head][:, keys], q1[head][:, queries],
                                     start=False, stop=kt < 4 * j)
                    if kt >= 4 * j:
                        last = pe.matmul(st[g % 2][:, col:col + P], sh.identb[:, :],
                                         sh.mask_kq[:, :], start=False, stop=True)
                    return last

                def p_v(g, tile):
                    u, head, j, tiles, width = STEPS[g]
                    kt, col, q0 = tile
                    for q in range(q0, TPB):
                        c = col + (q - q0) * P
                        pe.matmul(zp[:, q, 0:VW - 1], phi[g % PR][:, c:c + P],
                                  v[head][:, kt, 0:VW - 1], start=(kt == 0 and q % 2 == 0),
                                  stop=False, skip_group_check=True)
                        last = pe.matmul(zp[:, q, 0:VONE + 1], plo[g % PR][:, c:c + P],
                                         v[head][:, kt, 0:VONE + 1], start=False,
                                         stop=(kt == 4 * j + q), skip_group_check=True)
                    return last

                def p_v_waits(g):
                    u = STEPS[g][0]
                    pe.wait_ge(plo_done, pair * NG + g + 1)
                    if g == FIRST[u]:
                        pe.wait_ge(z_copied, pair * NU + u + 1)

                for it in AHEAD:
                    item(it)
                for g in range(NG):
                    u, head, j, tiles, width = STEPS[g]
                    carried = list(CARRIED[g])
                    if g == FIRST[u]:
                        row = AHEAD + [x for c in CARRIED for x in c]
                        pe.wait_ge(sq_read, 2 + pair * NI + row.index(("row", u)) + 1)
                    pe.wait_ge(exp_done, pair * NG + g + 1)
                    for n, tile in enumerate(tiles):
                        last = scores(g, tile)
                        if n == len(tiles) - 1:
                            last.then_inc(st_done, 1)
                        if carried:
                            item(carried.pop(0))
                    if g >= LAG:
                        p_v_waits(g - LAG)
                        for n, tile in enumerate(STEPS[g - LAG][3]):
                            last = p_v(g - LAG, tile)
                            if n == len(STEPS[g - LAG][3]) - 1:
                                last.then_inc(pv_done, 1)
                            if carried:
                                item(carried.pop(0))
                    while carried:
                        item(carried.pop(0))
                for g in range(NG - LAG, NG):
                    p_v_waits(g)
                    for tile in STEPS[g][3]:
                        last = p_v(g, tile)
                    last.then_inc(pv_done, 1)


def mix_phase(nc, io, sh):
    with ExitStack() as ctx:
        def sb(name, shape, dt):
            return ctx.enter_context(nc.sbuf_tensor(name, shape, dt))

        def sem(name):
            return ctx.enter_context(nc.semaphore(name))

        def bank(name, shape=(P, 512)):
            return ctx.enter_context(nc.psum_tensor(name, list(shape), F32))

        raw = sb("mraw", [P, C, 512], F32)
        woh, wol = (sb(n, [P, C, D], F32R) for n in ("woh", "wol"))
        rw = sb("rw", [P, C, E], F32)
        rwh, rwl = (sb(n, [P, C, E], F32R) for n in ("rwh", "rwl"))
        rb = sb("rb", [E, 1], F32)
        ob = sb("ob", [P, D], F32)
        obg = sb("obg", [P, D], F32)
        z = sb("z", [P, TPB, D], F32)
        zh, zl = (sb(n, [P, C, BLK], F32R) for n in ("zh", "zl"))
        xt = [sb(f"xt{i}", [P, TPB, D], F32) for i in range(2)]
        bst = sb("bst2", [P, TPB, 6], F32)
        mv = sb("mv2", [P, TPB, 2], F32)
        sd = sb("sd2", [P, TPB], F32)
        rstd = sb("rstd2", [P, TPB], F32)
        xhat = sb("xhat2", [P, TPB, D], F32)
        hf = [sb(f"hf2_{i}", [P, BLK], F32) for i in range(2)]
        hh, hl = (sb(n, [P, C, BLK], F32R) for n in ("hh2", "hl2"))
        lgt = sb("lgt", [E, S], F32)
        rank = sb("rank", [P, E], F32)
        big = [sb(f"big{i}", [P, KT, E], F32) for i in range(5)]
        row = [sb(f"row{i}", [P, KT], F32) for i in range(6)]
        tz = [bank(f"tz{i}") for i in range(2)]
        th = [bank(f"th{i}") for i in range(2)]
        acc = [bank(f"macc{i}") for i in range(2)]
        lg = bank("lg")
        lt = bank("lt")

        w_in = [sem(f"mw_in{i}") for i in range(3)]
        small_in = sem("small_in")
        z_in = sem("z_in")
        x_in = [sem(f"mx_in{i}") for i in range(2)]
        we_in = sem("we_in")
        w_scaled = sem("w_scaled")
        w_hi = sem("mw_hi")
        w_lo = sem("mw_lo")
        rank_done = sem("rank_done")
        obg_done = sem("obg_done")
        tz_done = sem("tz_done")
        z_high = sem("z_high")
        z_low = sem("z_low")
        acc_done = sem("macc_done")
        x1_done = sem("x1_done")
        bn_done = sem("bn_done2")
        bn_seen = sem("bn_seen2")
        mv_done = sem("mv_done2")
        sd_done = sem("sd_done2")
        rstd_done = sem("rstd_done2")
        xhat_done = sem("xhat_done2")
        x1o_done = sem("x1o_done")
        x1_sent = sem("x1_sent")
        th_done = sem("th_done")
        h_high = sem("h_high2")
        h_low = sem("h_low2")
        h_sent = sem("h_sent")
        lg_done = sem("lg_done")
        lg_read = sem("lg_read")
        lt_done = sem("lt_done")
        g_chain = sem("g_chain2")
        g_exp = sem("g_exp")
        gt_done = sem("gt_done")
        gt_read = sem("gt_read")
        g_sent = sem("g_sent")

        GATE_LINKS = 21

        block = ctx.enter_context(nc.Block())

        @block.sync
        def _(sp):
            sp.dma_start(raw[:, :, :], io.wo).then_inc(w_in[0], 16)
            sp.dma_start(z[:, :, :], io.z_scr[0]).then_inc(z_in, 16)
            sp.dma_start(xt[0][:, :, :], io.x[0]).then_inc(x_in[0], 16)
            sp.dma_start(rw[:, :, :], io.rw).then_inc(w_in[2], 16)
            sp.dma_start(rb[:, :], io.rb).then_inc(small_in, 16)
            sp.dma_start(ob[:, :], io.ob.broadcast_to([P, D])).then_inc(small_in, 16)
            sp.dma_start(xt[1][:, :, :], io.x[1]).then_inc(x_in[1], 16)
            sp.wait_ge(w_lo, 1)
            sp.dma_start(raw[:, :, :], io.ow).then_inc(w_in[1], 16)

            def step(b, s, ahead, ahead2):
                if ahead:
                    sp.wait_ge(tz_done, (b + 1) * C)
                    sp.dma_start(z[:, :, :], io.z_scr[b + 1]).then_inc(z_in, 16)
                sp.dma_start(sh.weraw[:, b, :, :], io.we[b]).then_inc(we_in, 16)
                sp.wait_ge(x1o_done, b + 1)
                sp.dma_start(io.x1_scr[b], xt[s][:, :, :]).then_inc(x1_sent, 16)
                if ahead2:
                    sp.wait_ge(x1_sent, (b + 1) * 16)
                    sp.dma_start(xt[s][:, :, :], io.x[b + 2]).then_inc(x_in[s], 16)
                sp.wait_ge(h_low, 2 + (b + 1) * C)
                for part, t in enumerate((hh, hl)):
                    sp.dma_start(io.h_scr[part, b], t[:, :, :].bitcast(F32))\
                      .then_inc(h_sent, 16)

            with sp.Fori(0, NB // 2 - 1) as it:
                for s in range(2):
                    step(2 * it + s, s, True, True)
            for s in range(2):
                step(NB - 2 + s, s, s == 0, False)
            sp.wait_ge(gt_read, NB)
            sp.dma_start(io.g_scr, lgt[:, :]).then_inc(g_sent, 16)
            sp.wait_ge(we_in, NB * 16)
            sp.wait_ge(x1_sent, NB * 16)
            sp.wait_ge(h_sent, 32 + NB * 32)
            sp.wait_ge(g_sent, 16)

        @block.gpsimd
        def _(pool):
            for e in range(E):
                pool.memset(rank[:, e:e + 1], float(E - e)).then_inc(rank_done, 1)
            pool.wait_ge(small_in, 32)
            pool.tensor_tensor(obg[:, :], ob[:, :], sh.gb[:, :], ALU.mult).then_inc(obg_done, 1)
            pool.wait_ge(obg_done, 1)

            def residual(b, s):
                pool.wait_ge(xhat_done, b + 1)
                for t in range(TPB):
                    last = pool.tensor_tensor(xt[s][:, t, :], xt[s][:, t, :], obg[:, :], ALU.add)
                last.then_inc(x1o_done, 1)

            with pool.Fori(0, NB // 2) as it:
                for s in range(2):
                    residual(2 * it + s, s)

        @block.scalar
        def _(act):
            act.sem_inc(h_high, 2)
            act.sem_inc(h_sent, 32)
            act.sem_inc(lg_read, 1)

            act.wait_ge(w_scaled, 1)
            act.activation(woh[:, :, :], raw[:, :, :], ACT.Copy).then_inc(w_hi, 1)

            def z_stage(b):
                for c in range(C):
                    act.wait_ge(tz_done, b * C + c + 1)
                    act.activation(zh[:, c, :], tz[c % 2][:, :], ACT.Copy).then_inc(z_high, 1)

            def o_stage(b):
                act.wait_ge(mv_done, b + 1)
                act.activation(sd[:, :], mv[:, :, 1], ACT.Sqrt, bias=sh.eps[:, 0:1])\
                   .then_inc(sd_done, 1)

            def h_stage(b):
                act.wait_ge(h_sent, b * 32 + 32)
                for c in range(C):
                    act.wait_ge(th_done, b * C + c + 1)
                    act.wait_ge(h_low, b * C + c + 1)
                    act.activation(hf[c % 2][:, :], th[c % 2][:, :], ACT.Identity,
                                   scale=sh.cb1[:, c:c + 1], bias=sh.sb[:, c:c + 1])
                    act.activation(hh[:, c, :], th[c % 2][:, :], ACT.Identity,
                                   scale=sh.cb1[:, c:c + 1], bias=sh.sb[:, c:c + 1])\
                       .then_inc(h_high, 1)

            def r_stage(b):
                act.wait_ge(lg_done, b + 1)
                act.activation(lgt[:, bass.ds(b * BLK, BLK)], lg[0:E, :], ACT.Identity,
                               bias=rb[:, 0:1]).then_inc(lg_read, 1)

            z_stage(0)
            act.wait_ge(w_in[2], 16)
            act.activation(rwh[:, :, :], rw[:, :, :], ACT.Copy).then_inc(w_hi, 1)
            act.wait_ge(small_in, 32)
            o_stage(0)
            act.wait_ge(w_scaled, 2)
            act.activation(sh.owh[:, :, :], raw[:, :, :], ACT.Copy).then_inc(w_hi, 1)

            def step(b, ahead):
                if ahead:
                    z_stage(b + 1)
                h_stage(b)
                if ahead:
                    o_stage(b + 1)
                r_stage(b)

            with act.Fori(0, NB // 2 - 1) as it:
                for s in range(2):
                    step(2 * it + s, True)
            for s in range(2):
                step(NB - 2 + s, s == 0)
            act.wait_ge(g_chain, 2)
            act.activation(big[2][:, :, :], big[1][:, :, :], ACT.Exp).then_inc(g_exp, 1)

        @block.vector
        def _(dve):
            dve.sem_inc(z_low, 2)
            dve.sem_inc(x1_done, 2)
            dve.sem_inc(h_low, 2)

            def scaled(k, g):
                dve.wait_ge(w_in[k], 16)
                for c in range(C):
                    last = dve.tensor_tensor(raw[:, c, :], raw[:, c, :], g[:, :], ALU.mult)
                last.then_inc(w_scaled, 1)

            def low(k, wl, wh, n):
                dve.wait_ge(w_hi, n)
                dve.tensor_tensor(wl[:, :, :], raw[:, :, :], wh[:, :, :].bitcast(F32),
                                  ALU.subtract).then_inc(w_lo, 1)

            def z_stage(b):
                for c in range(C):
                    dve.wait_ge(z_high, b * C + c + 1)
                    dve.tensor_tensor(zl[:, c, :], tz[c % 2][:, :], zh[:, c, :].bitcast(F32),
                                      ALU.subtract).then_inc(z_low, 1)

            def o_stage(b, s, x_count):
                dve.wait_ge(x_in[s], x_count)
                for t in range(TPB):
                    dve.wait_ge(acc_done, b * TPB + t + 1)
                    dve.tensor_tensor(xt[s][:, t, :], acc[t % 2][:, :], xt[s][:, t, :], ALU.add)\
                       .then_inc(x1_done, 1)
                    dve.wait_ge(x1_done, 2 + b * TPB + t + 1)
                    dve.bn_stats(bst[:, t, :], xt[s][:, t, :]).then_inc(bn_done, 1)
                dve.wait_ge(bn_done, b * TPB + TPB)
                dve.sem_inc(bn_seen, 1)
                for t in range(TPB):
                    last = dve.bn_aggr(mv[:, t, :], bst[:, t, :])
                last.then_inc(mv_done, 1)
                dve.wait_ge(sd_done, b + 1)
                dve.reciprocal(rstd[:, :], sd[:, :]).then_inc(rstd_done, 1)
                dve.wait_ge(rstd_done, b + 1)
                if not isinstance(b, int) or b > 0:
                    dve.wait_ge(th_done, b * C)
                for t in range(TPB):
                    last = dve.tensor_scalar(xhat[:, t, :], xt[s][:, t, :], mv[:, t, 0:1],
                                             rstd[:, t:t + 1], ALU.subtract, ALU.mult)
                last.then_inc(xhat_done, 1)

            def h_stage(b):
                for c in range(C):
                    dve.wait_ge(h_high, 2 + b * C + c + 1)
                    dve.tensor_tensor(hl[:, c, :], hf[c % 2][:, :], hh[:, c, :].bitcast(F32),
                                      ALU.subtract).then_inc(h_low, 1)

            scaled(0, sh.ga)
            low(0, wol, woh, 1)
            z_stage(0)
            dve.wait_ge(w_hi, 2)
            dve.tensor_tensor(rwl[:, :, :], rw[:, :, :], rwh[:, :, :].bitcast(F32),
                              ALU.subtract).then_inc(w_lo, 1)
            o_stage(0, 0, 16)
            scaled(1, sh.gb)
            low(1, sh.owl, sh.owh, 3)

            def step(b, s, ahead, x_count):
                if ahead:
                    z_stage(b + 1)
                h_stage(b)
                if ahead:
                    o_stage(b + 1, 1 - s, x_count)

            with dve.Fori(0, NB // 2 - 1) as it:
                step(2 * it, 0, True, it * 16 + 16)
                step(2 * it + 1, 1, True, it * 16 + 32)
            step(NB - 2, 0, True, NB // 2 * 16)
            step(NB - 1, 1, False, 0)

            n = [0]

            def link(ins):
                n[0] += 1
                ins.then_inc(g_chain, 1)
                dve.wait_ge(g_chain, n[0])

            def wide(r):
                return r[:, :].unsqueeze(2).broadcast_to([P, KT, E])

            logits = lt[:, 0:KT * E].rearrange("p (t e) -> p t e", e=E)
            dve.wait_ge(lt_done, 1)
            link(dve.reduce_max(row[0][:, :], logits, AX.X))
            link(dve.tensor_tensor(big[1][:, :, :], logits, wide(row[0]), ALU.subtract))
            dve.wait_ge(g_exp, 1)
            link(dve.reduce_sum(row[1][:, :], big[2][:, :, :], AX.X))
            link(dve.reciprocal(row[2][:, :], row[1][:, :]))
            link(dve.tensor_tensor(big[0][:, :, :], big[2][:, :, :], wide(row[2]), ALU.mult))
            ranks = rank[:, :].unsqueeze(1).broadcast_to([P, KT, E])
            dve.wait_ge(rank_done, E)

            def best(probs, value, chosen):
                link(dve.reduce_max(value[:, :], probs, AX.X))
                link(dve.tensor_tensor(big[1][:, :, :], probs, wide(value), ALU.is_equal))
                link(dve.tensor_tensor(big[2][:, :, :], big[1][:, :, :], ranks, ALU.mult))
                link(dve.reduce_max(row[5][:, :], big[2][:, :, :], AX.X))
                link(dve.tensor_tensor(chosen, big[2][:, :, :], wide(row[5]), ALU.is_equal))

            best(big[0][:, :, :], row[0], big[3][:, :, :])
            link(dve.scalar_tensor_tensor(big[4][:, :, :], big[3][:, :, :], -2.0,
                                          big[0][:, :, :], ALU.mult, ALU.add))
            best(big[4][:, :, :], row[1], big[1][:, :, :])
            link(dve.tensor_tensor(big[2][:, :, :], big[3][:, :, :], big[1][:, :, :], ALU.add))
            link(dve.tensor_tensor(big[3][:, :, :], big[2][:, :, :], big[0][:, :, :], ALU.mult))
            link(dve.tensor_tensor(row[2][:, :], row[0][:, :], row[1][:, :], ALU.add))
            link(dve.reciprocal(row[3][:, :], row[2][:, :]))
            link(dve.tensor_tensor(big[4][:, :, :], big[3][:, :, :], wide(row[3]), ALU.mult))
            assert n[0] == GATE_LINKS, n[0]
            for k in range(NB):
                dve.wait_ge(gt_done, k + 1)
                dve.tensor_copy(lgt[:, k * BLK:(k + 1) * BLK], (tz + th)[k % 4][0:E, :])\
                   .then_inc(gt_read, 1)

        @block.tensor
        def _(pe):
            def z_stage(b):
                pe.wait_ge(z_in, b * 16 + 16)
                for c in range(C):
                    pe.wait_ge(z_low, b * C + c + 1)
                    for t in range(TPB):
                        last = pe.transpose(tz[c % 2][:, t * P:(t + 1) * P],
                                            z[:, t, c * P:(c + 1) * P], sh.identf[:, :])
                    last.then_inc(tz_done, 1)

            def h_stage(b):
                pe.wait_ge(xhat_done, b + 1)
                for c in range(C):
                    pe.wait_ge(h_high, b * C + c + 1)
                    for t in range(TPB):
                        last = pe.transpose(th[c % 2][:, t * P:(t + 1) * P],
                                            xhat[:, t, c * P:(c + 1) * P], sh.identf[:, :])
                    last.then_inc(th_done, 1)

            def o_stage(b):
                pe.wait_ge(z_low, 2 + (b + 1) * C)
                for t in range(TPB):
                    pe.wait_ge(x1_done, b * TPB + t + 1)
                    tok = slice(t * P, (t + 1) * P)
                    three_terms(pe, acc[t % 2][:, :], lambda c: zh[:, c, tok],
                                lambda c: zl[:, c, tok], lambda c: woh[:, c, :],
                                lambda c: wol[:, c, :]).then_inc(acc_done, 1)

            def r_stage(b):
                pe.wait_ge(h_low, 2 + (b + 1) * C)
                pe.wait_ge(lg_read, b + 1)
                three_terms(pe, lg[0:E, :], lambda c: rwh[:, c, :], lambda c: rwl[:, c, :],
                            lambda c: hh[:, c, :], lambda c: hl[:, c, :]).then_inc(lg_done, 1)

            def step(b, ahead):
                if ahead:
                    z_stage(b + 1)
                h_stage(b)
                if ahead:
                    o_stage(b + 1)
                r_stage(b)

            z_stage(0)
            pe.wait_ge(w_lo, 1)
            o_stage(0)
            pe.wait_ge(w_lo, 2)
            with pe.Fori(0, NB // 2 - 1) as it:
                for s in range(2):
                    step(2 * it + s, True)
            for s in range(2):
                step(NB - 2 + s, s == 0)
            pe.wait_ge(lg_read, 1 + NB)
            for t in range(KT):
                last = pe.transpose(lt[:, t * E:(t + 1) * E], lgt[:, t * P:(t + 1) * P],
                                    sh.identf[0:E, 0:E])
            last.then_inc(lt_done, 1)
            pe.wait_ge(g_chain, GATE_LINKS)
            for k in range(NB):
                if k >= 4:
                    pe.wait_ge(gt_read, k - 3)
                for t in range(TPB):
                    last = pe.transpose((tz + th)[k % 4][0:E, t * P:(t + 1) * P],
                                        big[4][:, k * TPB + t, :], sh.identf[:, :])
                last.then_inc(gt_done, 1)


def experts_phase(nc, io, sh):
    with ExitStack() as ctx:
        def sb(name, shape, dt):
            return ctx.enter_context(nc.sbuf_tensor(name, shape, dt))

        def sem(name):
            return ctx.enter_context(nc.semaphore(name))

        wel = sb("wel", [P, E, C, D], F32R)
        weh = sb("weh", [P, E, C, D], F32R)
        eb = sb("eb", [P, E * C], F32)
        hh, hl = (sb(n, [P, C, BLK], F32R) for n in ("hh3", "hl3"))
        mix = sb("mix", [P, C, BLK], F32)
        mh, ml = (sb(n, [P, C, BLK], F32R) for n in ("mh", "ml"))
        GR, LR, XR = 2, 4, 2
        ge = [sb(f"ge{i}", [P, BLK], F32) for i in range(GR)]
        gl = [sb(f"gl{i}", [P, BLK], F32) for i in range(LR)]
        x1 = [sb(f"x1_{i}", [P, D], F32) for i in range(XR)]
        NACC = 6
        acc = [ctx.enter_context(nc.psum_tensor(f"eacc{i}", [P, 512], F32)) for i in range(NACC)]

        eb_in = sem("eb_in")
        h_in = sem("h_in")
        ge_in = [sem(f"ge_in{i}") for i in range(GR)]
        x1_in = [sem(f"x1_in{i}") for i in range(XR)]
        out_sent = [sem(f"out_sent{i}") for i in range(XR)]
        we_hi = sem("we_hi")
        we_lo = sem("we_lo")
        acc_done = sem("eacc_done")
        gelu_done = sem("gelu_done")
        gated = sem("gated")
        mixed = sem("mixed")
        mix_hi = sem("mix_hi")
        mix_lo = sem("mix_lo")
        out_done = sem("out_done")

        NE = E * C
        NO = NE + TPB

        block = ctx.enter_context(nc.Block())

        @block.sync
        def _(sp):
            def h_load(b):
                for part, t in enumerate((hh, hl)):
                    sp.dma_start(t[:, :, :].bitcast(F32), io.h_scr[part, b]).then_inc(h_in, 16)

            def gate_load(b, e):
                sp.dma_start(ge[e % GR][:, :],
                             io.g_scr[e:e + 1, bass.ds(b * BLK, BLK)].broadcast_to([P, BLK]))\
                  .then_inc(ge_in[e % GR], 16)

            def x1_load(b, t):
                sp.dma_start(x1[t % XR][:, :], io.x1_scr[b, :, t, :]).then_inc(x1_in[t % XR], 16)

            def step(b, ahead):
                for e in range(GR, E):
                    sp.wait_ge(mixed, LR + b * NE + (e - GR + 1) * C)
                    gate_load(b, e)
                if ahead:
                    sp.wait_ge(acc_done, b * NO + NE)
                    h_load(b + 1)
                    for e in range(GR):
                        sp.wait_ge(mixed, LR + b * NE + (E - GR + e + 1) * C)
                        gate_load(b + 1, e)
                for t in range(TPB):
                    sp.wait_ge(out_done, TPB + b * TPB + t + 1)
                    sp.dma_start(io.out[b, :, t, :], x1[t % XR][:, :])\
                      .then_inc(out_sent[t % XR], 16)
                    if t < TPB - XR or ahead:
                        sp.wait_ge(out_sent[t % XR], (b * (TPB // XR) + t // XR + 1) * 16)
                        if t < TPB - XR:
                            x1_load(b, t + XR)
                        else:
                            x1_load(b + 1, t + XR - TPB)

            sp.dma_start(eb[:, :], io.eb).then_inc(eb_in, 16)
            h_load(0)
            for e in range(GR):
                gate_load(0, e)
            for t in range(XR):
                x1_load(0, t)
            with sp.Fori(0, NB - 1) as b:
                step(b, True)
            step(NB - 1, False)
            for i in range(XR):
                sp.wait_ge(out_sent[i], NB * (TPB // XR) * 16)

        @block.scalar
        def _(act):
            act.sem_inc(gelu_done, 1)
            for e in range(E):
                act.activation(weh[:, e, :, :], sh.weraw[:, e, :, :], ACT.Copy)\
                   .then_inc(we_hi, 1)
                if e == 0:
                    act.wait_ge(eb_in, 16)
            with act.Fori(0, NB) as b:
                for n in range(NE):
                    act.wait_ge(acc_done, b * NO + n + 1)
                    act.wait_ge(mixed, b * NE + n + 1)
                    act.activation(gl[n % LR][:, :], acc[n % NACC][:, :], ACT.Gelu_apprx_tanh,
                                   bias=eb[:, n:n + 1]).then_inc(gelu_done, 1)
                for c in range(C):
                    act.wait_ge(mixed, LR + b * NE + NE - C + c + 1)
                    act.activation(mh[:, c, :], mix[:, c, :], ACT.Copy).then_inc(mix_hi, 1)

        @block.vector
        def _(dve):
            dve.sem_inc(mixed, LR)
            dve.sem_inc(out_done, TPB)
            for e in range(E):
                dve.wait_ge(we_hi, e + 1)
                dve.tensor_tensor(wel[:, e, :, :], sh.weraw[:, e, :, :],
                                  weh[:, e, :, :].bitcast(F32), ALU.subtract).then_inc(we_lo, 1)

            with dve.Fori(0, NB) as b:
                def add(n):
                    c = n % C
                    if n >= C:
                        dve.wait_ge(gated, b * (NE - C) + n - C + 1)
                        dve.wait_ge(mixed, LR + b * NE + n - C + 1)
                        dve.tensor_tensor(mix[:, c, :], mix[:, c, :], gl[n % LR][:, :], ALU.add)\
                           .then_inc(mixed, 1)

                for n in range(NE):
                    e, c = divmod(n, C)
                    if c == 0:
                        dve.wait_ge(ge_in[e % GR], (b * (E // GR) + e // GR + 1) * 16)
                    dve.wait_ge(gelu_done, 1 + b * NE + n + 1)
                    if e == 0:
                        dve.tensor_tensor(mix[:, c, :], gl[n % LR][:, :], ge[e % GR][:, :],
                                          ALU.mult).then_inc(mixed, 1)
                    else:
                        dve.tensor_tensor(gl[n % LR][:, :], gl[n % LR][:, :], ge[e % GR][:, :],
                                          ALU.mult).then_inc(gated, 1)
                    if n > 0:
                        add(n - 1)
                add(NE - 1)
                for c in range(C):
                    dve.wait_ge(mix_hi, b * C + c + 1)
                    dve.tensor_tensor(ml[:, c, :], mix[:, c, :], mh[:, c, :].bitcast(F32),
                                      ALU.subtract).then_inc(mix_lo, 1)
                for t in range(TPB):
                    dve.wait_ge(acc_done, b * NO + NE + t + 1)
                    dve.wait_ge(x1_in[t % XR], (b * (TPB // XR) + t // XR + 1) * 16)
                    dve.tensor_tensor(x1[t % XR][:, :], acc[(NE + t) % NACC][:, :],
                                      x1[t % XR][:, :], ALU.add).then_inc(out_done, 1)

        @block.tensor
        def _(pe):
            with pe.Fori(0, NB) as b:
                pe.wait_ge(h_in, (b + 1) * 32)
                for n in range(NE):
                    e, c = divmod(n, C)
                    if c == 0:
                        pe.wait_ge(we_lo, e + 1)
                    if n < NACC - TPB:
                        pe.wait_ge(gelu_done, 1 + b * NE)
                    elif n < NACC:
                        pe.wait_ge(out_done, b * TPB + n - (NACC - TPB) + 1)
                    else:
                        pe.wait_ge(gelu_done, 1 + b * NE + n - NACC + 1)
                    cols = slice(c * P, (c + 1) * P)
                    three_terms(pe, acc[n % NACC][:, :], lambda k: weh[:, e, k, cols],
                                lambda k: wel[:, e, k, cols], lambda k: hh[:, k, :],
                                lambda k: hl[:, k, :]).then_inc(acc_done, 1)
                pe.wait_ge(mix_lo, (b + 1) * C)
                for t in range(TPB):
                    pe.wait_ge(gelu_done, 1 + b * NE + NE + t - NACC + 1)
                    tok = slice(t * P, (t + 1) * P)
                    three_terms(pe, acc[(NE + t) % NACC][:, :], lambda k: mh[:, k, tok],
                                lambda k: ml[:, k, tok], lambda k: sh.owh[:, k, :],
                                lambda k: sh.owl[:, k, :]).then_inc(acc_done, 1)


class Holder:
    pass


def adaln_block(nc, arrays, out):
    io, sh = Holder(), Holder()

    def scratch(name, shape, dt=F32):
        return nc.dram_tensor(name, shape, dt, kind="Internal").ap()

    io.x = arrays["x"].rearrange("(b t p) d -> b p t d", t=TPB, p=P)
    io.out = out.rearrange("(b t p) d -> b p t d", t=TPB, p=P)
    io.c = arrays["c"]
    wide = "(c p) n -> p c n"
    io.wmod = [arrays["wmod"][:, m * D:(m + 1) * D].rearrange(wide, p=P) for m in range(6)]
    io.wk = [arrays["wk"].rearrange(wide, p=P)]
    io.wv = [arrays["wv"].rearrange(wide, p=P)]
    io.wq = [arrays["wq"][c * P:(c + 1) * P, :].rearrange("p (a n) -> p a n", a=C)
             for c in range(C)]
    io.wo = arrays["wo"].rearrange(wide, p=P)
    io.ow = arrays["ow"].rearrange(wide, p=P)
    io.we = arrays["we"].rearrange("e (c p) n -> e p c n", p=P)
    io.rw = arrays["rw"].rearrange(wide, p=P)
    io.rb, io.ob, io.eb = arrays["rb"], arrays["ob"], arrays["eb"]
    io.q_scr = scratch("q_scr", [2, PAIRS, P, S])
    io.k_scr = scratch("k_scr", [2, PAIRS, P, S])
    io.v_scr = scratch("v_scr", [P, HEADS, KT, VW], BF16)
    io.z_scr = scratch("z_scr", [NB, P, TPB, D])
    io.x1_scr = scratch("x1_scr", [NB, P, TPB, D])
    io.h_scr = scratch("h_scr", [2, NB, P, C, BLK])
    io.g_scr = scratch("g_scr", [E, S])

    with ExitStack() as ctx:
        def sb(name, shape, dt):
            return ctx.enter_context(nc.sbuf_tensor(name, shape, dt))

        sh.identf = sb("identf", [P, P], F32)
        sh.identb = sb("identb", [P, P], BF16)
        sh.mask_qk = sb("mask_qk", [P, P], BF16)
        sh.mask_kq = sb("mask_kq", [P, P], BF16)
        sh.eps = sb("eps", [P, 1], F32)
        sh.ga = sb("ga", [P, D], F32)
        sh.gb = sb("gb", [P, D], F32)
        sh.sb = sb("sbc", [P, C], F32)
        sh.cb1 = sb("cb1", [P, C], F32)
        project_phase(nc, io, sh)
        attend_phase(nc, io, sh)
        sh.owh, sh.owl = (sb(n, [P, C, D], F32R) for n in ("owh", "owl"))
        with nc.sbuf_tensor("weraw", [P, E, C, D], F32) as sh.weraw:
            mix_phase(nc, io, sh)
        experts_phase(nc, io, sh)


def kernel(**inputs):
    import numpy as np
    import concourse.bacc as bacc
    from concourse.bass_utils import run_bass_kernel_spmd

    f = {n.replace("L0_", ""): np.asarray(a) for n, a in inputs.items()}
    laid = {
        "x": f["attn_normalized_resid_pre"].reshape(S, D),
        "c": f["c"].reshape(C, P).T,
        "wmod": f["wmod"],
        "wq": f["attn_W_Q"].transpose(1, 0, 2).reshape(D, HEADS * GROUP * DH),
        "wk": f["attn_W_K"].transpose(1, 0, 2).reshape(D, HEADS * DH),
        "wv": f["attn_W_V"].transpose(1, 0, 2).reshape(D, HEADS * DH),
        "wo": f["attn_W_O"].reshape(HEADS * DH, D),
        "rw": f["ffn_router_w"],
        "rb": f["ffn_router_b"].reshape(E, 1),
        "we": f["ffn_expert_w"],
        "eb": f["ffn_expert_b"].reshape(E, C, P).transpose(2, 0, 1).reshape(P, E * C),
        "ow": f["ffn_out_w"],
        "ob": f["ffn_out_b"].reshape(1, D),
    }
    laid = {n: np.ascontiguousarray(a) for n, a in laid.items()}
    nc = bacc.Bacc("TRN2", target_bir_lowering=False, num_devices=1)
    aps = {n: nc.dram_tensor(f"in_{n}", a.shape, mybir.dt.from_np(a.dtype),
                             kind="ExternalInput").ap() for n, a in laid.items()}
    out = nc.dram_tensor("out", [S, D], F32, kind="ExternalOutput").ap()
    adaln_block(nc, aps, out)
    r = run_bass_kernel_spmd(nc, [{f"in_{n}": a for n, a in laid.items()}], core_ids=[0])
    return r.results[0]["out"].reshape(1, S, D)
```

```python
import math
from contextlib import ExitStack

import concourse.bass as bass
from concourse import mybir

F32 = mybir.dt.float32
F32R = mybir.dt.float32r
BF16 = mybir.dt.bfloat16
I32 = mybir.dt.int32
U32 = mybir.dt.uint32
FP16 = mybir.dt.float16
ALU = mybir.AluOpType
ACT = mybir.ActivationFunctionType
AX = mybir.AxisListType

P = 128
S = 4096
D = 512
C = D // P
BLK = 512
NB = S // BLK
TPB = BLK // P
HEADS = 8
GROUP = 4
DH = 64
PAIRS = HEADS // 2
KT = S // P
E = 8
NTILE = -(-((2 * S - E) // P + E) // 4) * 4
EPS = 1e-5
VHI, VMID, VONE, VLO = 0, DH, 2 * DH, 2 * DH + 1
VW = 3 * DH + 2
NEG = -1e30
SCALE = 1.0 / math.sqrt(DH)
P_SHIFT = 4 * math.log(2.0) / SCALE


def three_terms(pe, out, s_hi, s_lo, m_hi, m_lo):
    for c in range(C):
        for n, (s, m) in enumerate(((s_hi, m_hi), (s_hi, m_lo), (s_lo, m_hi))):
            last = pe.matmul(out, s(c), m(c), start=(c == 0 and n == 0),
                             stop=(c == C - 1 and n == 2))
    return last


def project_phase(nc, io, sh):
    with ExitStack() as ctx:
        def sb(name, shape, dt):
            return ctx.enter_context(nc.sbuf_tensor(name, shape, dt))

        def sem(name):
            return ctx.enter_context(nc.semaphore(name))

        RAW = 4
        raw = [sb(f"raw{i}", [P, C, 512], F32) for i in range(RAW)]
        wqh, wql, wkh, wkl, wvh, wvl = (sb(n, [P, C, 512], F32R)
                                        for n in ("wqh", "wql", "wkh", "wkl", "wvh", "wvl"))
        wsum = [sb(f"wsum{i}", [P, 512], F32) for i in range(4)]
        craw = sb("craw", [P, C], F32)
        cexp = sb("cexp", [P, C], F32)
        cden = sb("cden", [P, C], F32)
        cinv = sb("cinv", [P, C], F32)
        csilu = sb("csilu", [P, C], F32)
        cwide = sb("cwide", [P, C, P], F32)
        mrow = [sb(f"mrow{i}", [P, 512], F32) for i in range(4)]
        gneg, gabs, gsgn = (sb(n, [P, 512], F32) for n in ("gneg", "gabs", "gsgn"))
        sa = sb("sa", [P, C], F32)
        ca1 = sb("ca1", [P, C], F32)
        xb = [sb(f"xb{i}", [P, TPB, D], F32) for i in range(2)]
        bst = sb("bst", [P, TPB, 6], F32)
        mv = sb("mv", [P, TPB, 2], F32)
        sd = sb("sd", [P, TPB], F32)
        rstd = sb("rstd", [P, TPB], F32)
        xhat = sb("xhat", [P, TPB, D], F32)
        hf = [sb(f"hf{i}", [P, BLK], F32) for i in range(2)]
        hh = [sb(f"hh{i}", [P, C, BLK], F32R) for i in range(2)]
        hl = [sb(f"hl{i}", [P, C, BLK], F32R) for i in range(2)]
        QR = 4
        qh = [sb(f"qh{i}", [P, BLK], F32R) for i in range(QR)]
        ql = [sb(f"ql{i}", [P, BLK], F32R) for i in range(QR)]
        VR = 2
        vt = [sb(f"vt{i}", [P, HEADS, VW], BF16) for i in range(VR)]
        vr = [sb(f"vr{i}", [P, HEADS, DH], F32) for i in range(VR)]
        tp = [ctx.enter_context(nc.psum_tensor(f"tp{i}", [P, 512], F32)) for i in range(2)]
        NACC = 6
        acc = [ctx.enter_context(nc.psum_tensor(f"acc{i}", [P, 512], F32)) for i in range(NACC)]

        c_in = sem("c_in")
        x_in = [sem(f"x_in{i}") for i in range(2)]
        raw_in = [sem(f"raw_in{i}") for i in range(RAW)]
        raw_free = [sem(f"raw_free{i}") for i in range(RAW)]
        const_done = sem("const_done")
        c_exp = sem("c_exp")
        c_chain = sem("c_chain")
        cwide_done = sem("cwide_done")
        mod_mm = sem("mod_mm")
        mod_row = sem("mod_row")
        col_mm = sem("col_mm")
        col_done = sem("col_done")
        w_hi = sem("w_hi")
        w_lo = sem("w_lo")
        w_half = sem("w_half")
        w_sum = sem("w_sum")
        bn_done = sem("bn_done")
        bn_seen = sem("bn_seen")
        mv_done = sem("mv_done")
        sd_done = sem("sd_done")
        rstd_done = sem("rstd_done")
        xhat_done = sem("xhat_done")
        tp_done = sem("tp_done")
        h_high = sem("h_high")
        h_low = sem("h_low")
        acc_done = sem("acc_done")
        hi_out = sem("hi_out")
        acc_read = sem("acc_read")
        v_mid = sem("v_mid")
        v_ready = sem("v_ready")
        qk_sent = [sem(f"qk_sent{i}") for i in range(QR)]
        v_sent = [sem(f"v_sent{i}") for i in range(VR)]
        g_chain = sem("g_chain")

        NQK = 2 * PAIRS
        NIT = NQK + TPB
        HALF = NIT // 2
        PIECES = ([("mod", 0), ("mod", 1), ("wk", 0), ("wv", 0)]
                  + [("wq", c) for c in range(C)] + [("mod", m) for m in range(2, 6)])
        AT = {p: n for n, p in enumerate(PIECES)}

        def slot(kind, i=0):
            n = AT[kind, i]
            return n % RAW, 16 * (n // RAW + 1)

        block = ctx.enter_context(nc.Block())

        @block.sync
        def _(sp):
            sp.dma_start(craw[:, :], io.c).then_inc(c_in, 16)
            sp.dma_start(xb[0][:, :, :], io.x[0]).then_inc(x_in[0], 16)
            for n, (kind, i) in enumerate(PIECES):
                if n >= RAW:
                    sp.wait_ge(raw_free[n % RAW], n // RAW)
                src = {"mod": io.wmod, "wk": io.wk, "wv": io.wv, "wq": io.wq}[kind][i]
                sp.dma_start(raw[n % RAW][:, :, :], src).then_inc(raw_in[n % RAW], 16)
                if n == 3:
                    sp.dma_start(xb[1][:, :, :], io.x[1]).then_inc(x_in[1], 16)

            def stores(b, s, ahead):
                if ahead:
                    sp.wait_ge(xhat_done, b + 1)
                    sp.dma_start(xb[s][:, :, :], io.x[b + 2]).then_inc(x_in[s], 16)
                for n in range(NQK):
                    dst = io.q_scr if n < PAIRS else io.k_scr
                    sp.wait_ge(acc_read, NACC + b * NIT + n + 1)
                    for part, t in enumerate((qh, ql)):
                        sp.dma_start(dst[part, n % PAIRS, :, bass.ds(b * BLK, BLK)],
                                     t[n % QR][:, :].bitcast(F32)).then_inc(qk_sent[n % QR], 16)
                for t in range(TPB):
                    sp.wait_ge(v_ready, b * TPB + t + 1)
                    sp.dma_start(io.v_scr[:, :, b * TPB + t, :], vt[t % VR][:, :, :])\
                      .then_inc(v_sent[t % VR], 16)

            with sp.Fori(0, NB // 2 - 1) as it:
                for s in range(2):
                    stores(2 * it + s, s, True)
            for s in range(2):
                stores(NB - 2 + s, s, False)
            for i in range(QR):
                sp.wait_ge(qk_sent[i], 32 + NB * (NQK // QR) * 32)
            for i in range(VR):
                sp.wait_ge(v_sent[i], 16 + NB * (TPB // VR) * 16)

        @block.gpsimd
        def _(pool):
            for m in (sh.identf, sh.identb, sh.mask_qk, sh.mask_kq):
                pool.memset(m[:, :], 0.0).then_inc(const_done, 1)
            pool.memset(sh.eps[:, :], EPS).then_inc(const_done, 1)
            for t in vt:
                pool.memset(t[:, :, :], 1.0).then_inc(const_done, 1)
            pool.wait_ge(const_done, 5 + VR)
            for m in (sh.identf, sh.identb):
                pool.affine_select(out=m[:, :], in_=m[:, :], compare_op=ALU.not_equal, fill=1.0,
                                   base=0, pattern=[[-1, P]], channel_multiplier=1)\
                    .then_inc(const_done, 1)
            pool.affine_select(out=sh.mask_qk[:, :], in_=sh.mask_qk[:, :], compare_op=ALU.is_ge,
                               fill=NEG, base=0, pattern=[[-1, P]], channel_multiplier=1)\
                .then_inc(const_done, 1)
            pool.affine_select(out=sh.mask_kq[:, :], in_=sh.mask_kq[:, :], compare_op=ALU.is_ge,
                               fill=NEG, base=0, pattern=[[1, P]], channel_multiplier=-1)\
                .then_inc(const_done, 1)

        CONST = 9 + VR

        @block.scalar
        def _(act):
            act.sem_inc(h_high, 2)
            for i in range(QR):
                act.sem_inc(qk_sent[i], 32)
            for i in range(VR):
                act.sem_inc(v_sent[i], 16)
            act.wait_ge(c_in, 16)
            act.activation(cexp[:, :], craw[:, :], ACT.Exp, scale=-1.0).then_inc(c_exp, 1)
            act.wait_ge(const_done, CONST)

            def std_dev(b):
                act.wait_ge(mv_done, b + 1)
                act.activation(sd[:, :], mv[:, :, 1], ACT.Sqrt, bias=sh.eps[:, 0:1])\
                   .then_inc(sd_done, 1)

            def modulate(b, s):
                for c in range(C):
                    act.wait_ge(tp_done, b * C + c + 1)
                    act.wait_ge(h_low, b * C + c + 1)
                    act.activation(hf[c % 2][:, :], tp[c % 2][:, :], ACT.Identity,
                                   scale=ca1[:, c:c + 1], bias=sa[:, c:c + 1])
                    act.activation(hh[s][:, c, :], tp[c % 2][:, :], ACT.Identity,
                                   scale=ca1[:, c:c + 1], bias=sa[:, c:c + 1]).then_inc(h_high, 1)

            def high_parts(b, lo, hi):
                for n in range(lo, hi):
                    act.wait_ge(acc_done, b * NIT + n + 1)
                    if n < NQK:
                        k = n % QR
                        act.wait_ge(qk_sent[k], (b * (NQK // QR) + n // QR) * 32 + 32)
                        act.activation(qh[k][:, :], acc[n % NACC][:, :], ACT.Copy)\
                           .then_inc(hi_out, 1)
                    else:
                        t = n - NQK
                        k = t % VR
                        act.wait_ge(v_sent[k], (b * (TPB // VR) + t // VR) * 16 + 16)
                        act.activation(vt[k][:, :, VHI:VHI + DH],
                                       acc[n % NACC][:, :].rearrange("p (h d) -> p h d", h=HEADS),
                                       ACT.Copy).then_inc(hi_out, 1)
                        act.wait_ge(acc_read, NACC + b * NIT + n + 1)
                        act.activation(vt[k][:, :, VMID:VMID + DH], vr[k][:, :, :], ACT.Copy)\
                           .then_inc(v_mid, 1)

            std_dev(0)
            act.wait_ge(col_done, 2)
            modulate(0, 0)
            for w, kind in ((wkh, "wk"), (wvh, "wv")):
                k, n = slot(kind)
                act.wait_ge(raw_in[k], n)
                act.activation(w[:, :, :], raw[k][:, :, :], ACT.Copy).then_inc(w_hi, 1)
            for c in range(C):
                act.wait_ge(w_sum, c + 1)
                act.activation(wqh[:, c, :], wsum[2 + c % 2][:, :], ACT.Copy).then_inc(w_hi, 1)

            def step(b, s, ahead):
                if ahead:
                    std_dev(b + 1)
                high_parts(b, 0, HALF)
                if ahead:
                    modulate(b + 1, 1 - s)
                high_parts(b, HALF, NIT)

            with act.Fori(0, NB // 2 - 1) as it:
                for s in range(2):
                    step(2 * it + s, s, True)
            for s in range(2):
                step(NB - 2 + s, s, s == 0)

        @block.vector
        def _(dve):
            dve.sem_inc(acc_read, NACC)
            dve.sem_inc(h_low, 2)

            def layer_norm(b, s, x_count):
                dve.wait_ge(x_in[s], x_count)
                for t in range(TPB):
                    dve.bn_stats(bst[:, t, :], xb[s][:, t, :]).then_inc(bn_done, 1)
                dve.wait_ge(bn_done, b * TPB + TPB)
                dve.sem_inc(bn_seen, 1)
                for t in range(TPB):
                    last = dve.bn_aggr(mv[:, t, :], bst[:, t, :])
                last.then_inc(mv_done, 1)
                dve.wait_ge(sd_done, b + 1)
                dve.reciprocal(rstd[:, :], sd[:, :]).then_inc(rstd_done, 1)
                dve.wait_ge(rstd_done, b + 1)
                if not isinstance(b, int) or b > 0:
                    dve.wait_ge(tp_done, b * C)
                for t in range(TPB):
                    last = dve.tensor_scalar(xhat[:, t, :], xb[s][:, t, :], mv[:, t, 0:1],
                                             rstd[:, t:t + 1], ALU.subtract, ALU.mult)
                last.then_inc(xhat_done, 1)

            def low_h(b, s):
                for c in range(C):
                    dve.wait_ge(h_high, 2 + b * C + c + 1)
                    dve.tensor_tensor(hl[s][:, c, :], hf[c % 2][:, :],
                                      hh[s][:, c, :].bitcast(F32), ALU.subtract)\
                       .then_inc(h_low, 1)

            def low_parts(b, lo, hi):
                for n in range(lo, hi):
                    dve.wait_ge(hi_out, b * NIT + n + 1)
                    if n < NQK:
                        k = n % QR
                        dve.tensor_tensor(ql[k][:, :], acc[n % NACC][:, :],
                                          qh[k][:, :].bitcast(F32), ALU.subtract)\
                           .then_inc(acc_read, 1)
                    else:
                        t = n - NQK
                        k = t % VR
                        dve.tensor_tensor(vr[k][:, :, :],
                                          acc[n % NACC][:, :].rearrange("p (h d) -> p h d",
                                                                        h=HEADS),
                                          vt[k][:, :, VHI:VHI + DH], ALU.subtract)\
                           .then_inc(acc_read, 1)
                        dve.wait_ge(v_mid, b * TPB + t + 1)
                        dve.tensor_tensor(vt[k][:, :, VLO:VLO + DH], vr[k][:, :, :],
                                          vt[k][:, :, VMID:VMID + DH], ALU.subtract)\
                           .then_inc(v_ready, 1)

            dve.wait_ge(c_exp, 1)
            dve.tensor_scalar_add(cden[:, :], cexp[:, :], 1.0).then_inc(c_chain, 1)
            dve.wait_ge(c_chain, 1)
            dve.reciprocal(cinv[:, :], cden[:, :]).then_inc(c_chain, 1)
            dve.wait_ge(c_chain, 2)
            dve.tensor_tensor(csilu[:, :], craw[:, :], cinv[:, :], ALU.mult).then_inc(c_chain, 1)
            dve.wait_ge(c_chain, 3)
            for c in range(C):
                last = dve.tensor_copy(cwide[:, c, :], csilu[:, c:c + 1].broadcast_to([P, P]))
            last.then_inc(cwide_done, 1)
            layer_norm(0, 0, 16)

            def mod_sections(ms, bank0, cols):
                for i, m in enumerate(ms):
                    dve.wait_ge(mod_mm, m + 1)
                    dve.tensor_copy(mrow[i][:, :], acc[bank0 + i][:, :]).then_inc(mod_row, 1)
                for i, (col, dst, add) in enumerate(cols):
                    dve.wait_ge(col_mm, col + 1)
                    dve.tensor_scalar_add(dst[:, :], acc[bank0 + len(ms) + i][:, ::P], add)\
                       .then_inc(col_done, 1)

            mod_sections([0, 1], 0, [(0, sa, 0.0), (1, ca1, 1.0)])
            low_h(0, 0)
            for w, wh, kind in ((wkl, wkh, "wk"), (wvl, wvh, "wv")):
                k, n = slot(kind)
                dve.wait_ge(raw_in[k], n)
                dve.wait_ge(w_hi, 1 if kind == "wk" else 2)
                dve.tensor_tensor(w[:, :, :], raw[k][:, :, :], wh[:, :, :].bitcast(F32),
                                  ALU.subtract).then_inc(raw_free[k], 1)
            for c in range(C):
                k, n = slot("wq", c)
                dve.wait_ge(raw_in[k], n)
                g = raw[k][:, :, :].rearrange("p a (b g d) -> p (a b) g d", g=GROUP, d=DH)

                def out(t):
                    return t[:, :].rearrange("p (n d) -> p n d", d=DH)

                dve.tensor_tensor(out(wsum[0]), g[:, :, 0, :], g[:, :, 1, :], ALU.add)\
                   .then_inc(w_half, 1)
                dve.tensor_tensor(out(wsum[1]), g[:, :, 2, :], g[:, :, 3, :], ALU.add)\
                   .then_inc(raw_free[k], 1)
                dve.wait_ge(w_half, c + 1)
                dve.wait_ge(raw_free[k], n // 16)
                dve.tensor_tensor(wsum[2 + c % 2][:, :], wsum[0][:, :], wsum[1][:, :], ALU.add)\
                   .then_inc(w_sum, 1)
                dve.wait_ge(w_sum, c + 1)
                dve.wait_ge(w_hi, 3 + c)
                dve.tensor_tensor(wql[:, c, :], wsum[2 + c % 2][:, :],
                                  wqh[:, c, :].bitcast(F32), ALU.subtract).then_inc(w_lo, 1)

            def step(b, s, ahead, x_count):
                if ahead:
                    layer_norm(b + 1, 1 - s, x_count)
                low_parts(b, 0, HALF)
                if ahead:
                    low_h(b + 1, 1 - s)
                low_parts(b, HALF, NIT)

            with dve.Fori(0, NB // 2 - 1) as it:
                step(2 * it, 0, True, it * 16 + 16)
                step(2 * it + 1, 1, True, it * 16 + 32)
            step(NB - 2, 0, True, NB // 2 * 16)
            step(NB - 1, 1, False, 0)

            mod_sections([2, 3, 4, 5], 0, [])
            dve.wait_ge(mod_row, 6)
            dve.tensor_copy(sh.sb[:, :], mrow[1][:, :]).then_inc(g_chain, 1)
            dve.tensor_scalar_add(sh.cb1[:, :], mrow[2][:, :], 1.0).then_inc(g_chain, 1)
            n = 2
            for i, dst in ((0, sh.ga), (3, sh.gb)):
                g = mrow[i]
                dve.wait_ge(mod_row, 3 + i)
                dve.tensor_scalar(gneg[:, :], g[:, :], -1.0, None, ALU.mult).then_inc(g_chain, 1)
                dve.tensor_scalar(gsgn[:, :], g[:, :], 0.0, 2.0, ALU.is_ge, ALU.mult)\
                   .then_inc(g_chain, 1)
                dve.wait_ge(g_chain, n + 2)
                dve.tensor_tensor(gabs[:, :], g[:, :], gneg[:, :], ALU.max).then_inc(g_chain, 1)
                dve.wait_ge(g_chain, n + 3)
                dve.tensor_scalar(gneg[:, :], gabs[:, :], 0.25, None, ALU.max)\
                   .then_inc(g_chain, 1)
                dve.wait_ge(g_chain, n + 4)
                dve.scalar_tensor_tensor(dst[:, :], gsgn[:, :], -1.0, gneg[:, :], ALU.add,
                                         ALU.mult).then_inc(g_chain, 1)
                n += 5
                dve.wait_ge(g_chain, n)

        @block.tensor
        def _(pe):
            def mod_section(m, bank):
                k, n = slot("mod", m)
                pe.wait_ge(raw_in[k], n)
                for c in range(C):
                    last = pe.matmul(acc[bank][:, :], cwide[:, c, :], raw[k][:, c, :],
                                     start=(c == 0), stop=(c == C - 1))
                last.then_inc(mod_mm, 1)
                pe.wait_ge(mod_mm, m + 1)
                pe.sem_inc(raw_free[k], 1)

            def column(row, bank, row_count):
                pe.wait_ge(mod_row, row_count)
                for c in range(C):
                    last = pe.transpose(acc[bank][:, c * P:(c + 1) * P],
                                        mrow[row][:, c * P:(c + 1) * P], sh.identf[:, :])
                last.then_inc(col_mm, 1)

            def transposes(b):
                pe.wait_ge(xhat_done, b + 1)
                for c in range(C):
                    pe.wait_ge(h_high, b * C + c + 1)
                    for t in range(TPB):
                        last = pe.transpose(tp[c % 2][:, t * P:(t + 1) * P],
                                            xhat[:, t, c * P:(c + 1) * P], sh.identf[:, :])
                    last.then_inc(tp_done, 1)

            def products(b, s, lo, hi):
                pe.wait_ge(h_low, 2 + (b + 1) * C)
                for n in range(lo, hi):
                    pe.wait_ge(acc_read, b * NIT + n + 1)
                    if n < NQK:
                        wh, wl = (wqh, wql) if n < PAIRS else (wkh, wkl)
                        j = n % PAIRS * P
                        last = three_terms(pe, acc[n % NACC][:, :],
                                           lambda c: wh[:, c, j:j + P], lambda c: wl[:, c, j:j + P],
                                           lambda c: hh[s][:, c, :], lambda c: hl[s][:, c, :])
                    else:
                        j = (n - NQK) * P
                        last = three_terms(pe, acc[n % NACC][:, :],
                                           lambda c: hh[s][:, c, j:j + P],
                                           lambda c: hl[s][:, c, j:j + P],
                                           lambda c: wvh[:, c, :], lambda c: wvl[:, c, :])
                    last.then_inc(acc_done, 1)

            def step(b, s, ahead):
                products(b, s, 0, HALF)
                if ahead:
                    transposes(b + 1)
                products(b, s, HALF, NIT)

            pe.wait_ge(const_done, CONST)
            pe.wait_ge(cwide_done, 1)
            for m in range(2):
                mod_section(m, m)
            for m in range(2):
                column(m, 2 + m, m + 1)
            transposes(0)
            pe.wait_ge(col_done, 2)
            for kind in ("wk", "wv"):
                k, n = slot(kind)
                pe.wait_ge(raw_free[k], n // 16)
            pe.wait_ge(w_lo, C)
            with pe.Fori(0, NB // 2 - 1) as it:
                for s in range(2):
                    step(2 * it + s, s, True)
            for s in range(2):
                step(NB - 2 + s, s, s == 0)
            pe.wait_ge(acc_read, NACC + NB * NIT)
            for m in range(2, 6):
                mod_section(m, m - 2)


LAG = 3
CAP = (1, 2, 3, 3)
NEXT = 2
LEAD = 5
POOL_EVERY = 4


def attention_schedule():
    steps, first, last = [], [], []
    for head in range(2):
        for j in range(NB):
            first.append(len(steps))
            steps += [(head * NB + j, head, j, kt, max(0, kt - TPB * j))
                      for kt in range(TPB * (j + 1))]
            last.append(len(steps) - 1)

    def items(u):
        return ([("max", u, q, kb) for q in range(TPB) for kb in range(u % NB + 1)]
                + [("row", u)])

    units = len(first)
    todo = [(max(0, first[u] - LEAD), it) for u in range(NEXT, units) for it in items(u)]
    todo += [(len(steps) - 1, it) for u in range(units, units + NEXT) for it in items(u)]
    carried = [[] for _ in steps]
    for g in reversed(range(len(steps))):
        while todo and todo[-1][0] >= g and (len(carried[g]) < CAP[steps[g][4]] or g == 0):
            carried[g].insert(0, todo.pop()[1])
    return steps, first, last, [it for u in range(NEXT) for it in items(u)], carried


def attend_phase(nc, io, sh):
    STEPS, FIRST, LAST, AHEAD, CARRIED = attention_schedule()
    ORDER = AHEAD + [it for c in CARRIED for it in c]
    NG = len(STEPS)
    NU = len(FIRST)
    SR = 3
    NI = -(-(len(ORDER) - len(AHEAD)) // SR) * SR
    LEFT = NI - (len(ORDER) - len(AHEAD))
    with ExitStack() as ctx:
        def sb(name, shape, dt):
            return ctx.enter_context(nc.sbuf_tensor(name, shape, dt))

        def sem(name):
            return ctx.enter_context(nc.semaphore(name))

        kk, k1, qq, q1 = ([sb(f"{n}{i}", [P, S], F32R) for i in range(2)]
                          for n in ("kk", "k1_", "qq", "q1_"))
        v = [sb(f"v{i}", [P, KT, VW], BF16) for i in range(2)]
        PR = 6
        p32 = [sb(f"p32_{i}", [P, BLK], F32) for i in range(PR)]
        phi = [sb(f"phi{i}", [P, BLK], FP16) for i in range(PR)]
        plo = [sb(f"plo{i}", [P, BLK], FP16) for i in range(PR)]
        mpart = [sb(f"mpart{i}", [P, TPB, NB], F32) for i in range(2)]
        m4 = [sb(f"m4_{i}", [P, TPB], F32) for i in range(2)]
        zs = [sb(f"zs{i}", [P, TPB, VW], F32) for i in range(2)]
        rl = [sb(f"rl{i}", [P, TPB], F32) for i in range(2)]
        zt = [sb(f"zt{i}", [P, TPB, DH], F32) for i in range(2)]
        zo = [sb(f"zo{i}", [P, TPB, DH], F32) for i in range(2)]
        st = [ctx.enter_context(nc.psum_tensor(f"st{i}", [P, BLK], F32)) for i in range(SR)]
        zp = ctx.enter_context(nc.psum_tensor("zp", [P, TPB, 256], F32))
        sq = [ctx.enter_context(nc.psum_tensor(f"sq{i}", [P, BLK], F32)) for i in range(SR)]

        kqv_in = [sem(f"kqv_in{i}") for i in range(2)]
        fill_done = sem("fill_done")
        sq_done = sem("sq_done")
        sq_read = sem("sq_read")
        m4_done = sem("m4_done")
        st_done = sem("st_done")
        exp_done = sem("exp_done")
        plo_dve = sem("plo_dve")
        plo_pool = sem("plo_pool")
        pv_done = sem("pv_done")
        z_copied = sem("z_copied")
        r_done = sem("r_done")
        z_chain = sem("z_chain")
        z_ready = sem("z_ready")
        z_sent = [sem(f"z_sent{i}") for i in range(2)]
        LOADS = 7

        def width(g):
            return BLK - STEPS[g][4] * P

        def by_pool(g):
            return g % POOL_EVERY == 1 and width(g) == BLK

        def lows(g, pool):
            return sum(by_pool(x) == pool for x in range(g + 1))

        NPOOL = lows(NG - 1, True)
        NDVE = NG - NPOOL

        block = ctx.enter_context(nc.Block())

        @block.sync
        def _(sp):
            def load(pair, i):
                rows = slice(i * DH, (i + 1) * DH)
                for dst, lo, src, part in ((kk, 0, io.k_scr, 0), (kk, DH, io.k_scr, 1),
                                           (qq, 0, io.q_scr, 0), (qq, DH, io.q_scr, 0),
                                           (k1, 0, io.k_scr, 0), (q1, 0, io.q_scr, 1)):
                    sp.dma_start(dst[i][lo:lo + DH, :].bitcast(F32), src[part, pair, rows, :])\
                      .then_inc(kqv_in[i], 16)
                sp.dma_start(v[i][:, :, :], io.v_scr[:, 2 * pair + i, :, :])\
                  .then_inc(kqv_in[i], 16)

            def store(pair, u):
                i, j = divmod(u, NB)
                sp.wait_ge(z_ready, 2 + pair * NU + u + 1)
                sp.dma_start(io.z_scr[j, :, :, bass.ds((2 * pair + i) * DH, DH)],
                             zo[u % 2][:, :, :]).then_inc(z_sent[u % 2], 16)

            for i in range(2):
                load(0, i)
            with sp.Fori(0, PAIRS - 1) as pair:
                for i in range(2):
                    for j in range(NB):
                        store(pair, i * NB + j)
                    load(pair + 1, i)
            for u in range(NU):
                store(PAIRS - 1, u)
            for i in range(2):
                sp.wait_ge(z_sent[i], 16 + PAIRS * NU // 2 * 16)

        @block.gpsimd
        def _(pool):
            pool.sem_inc(z_ready, 2)
            for i in range(2):
                pool.sem_inc(z_sent[i], 16)
                pool.memset(k1[i][DH:P, :].bitcast(F32), 0.0).then_inc(fill_done, 1)
                pool.memset(q1[i][DH:P, :].bitcast(F32), 0.0).then_inc(fill_done, 1)
            pool.wait_ge(fill_done, 4)
            for i in range(2):
                pool.memset(k1[i][DH:DH + 1, :].bitcast(F32), 1.0).then_inc(fill_done, 1)

            with pool.Fori(0, PAIRS) as pair:
                def normalise(u):
                    k = u % 2
                    n = pair * NU + u
                    pool.wait_ge(z_copied, 2 + 2 * n + 2)
                    pool.tensor_tensor(zt[0][:, :, :], zs[k][:, :, VHI:VHI + DH],
                                       zs[k][:, :, VMID:VMID + DH], ALU.add).then_inc(z_chain, 1)
                    pool.wait_ge(z_chain, n * 2 + 1)
                    pool.tensor_tensor(zt[1][:, :, :], zt[0][:, :, :],
                                       zs[k][:, :, VLO:VLO + DH], ALU.add).then_inc(z_chain, 1)
                    pool.wait_ge(z_chain, n * 2 + 2)
                    pool.wait_ge(r_done, n + 1)
                    pool.wait_ge(z_sent[k], 16 * (pair * (NU // 2) + u // 2) + 16)
                    pool.tensor_tensor(zo[k][:, :, :], zt[1][:, :, :],
                                       rl[k][:, :].unsqueeze(2).broadcast_to([P, TPB, DH]),
                                       ALU.mult).then_inc(z_ready, 1)

                for g in range(NG):
                    if by_pool(g):
                        pool.wait_ge(exp_done, SR + pair * NG + g + 1)
                        pool.tensor_tensor(plo[g % PR][:, :], p32[g % PR][:, :],
                                           phi[g % PR][:, :], ALU.subtract)\
                            .then_inc(plo_pool, 1)
                    if g - LAG - 1 in LAST:
                        normalise(LAST.index(g - LAG - 1))
                normalise(NU - 1)

        @block.scalar
        def _(act):
            act.sem_inc(exp_done, SR)
            act.sem_inc(z_copied, 2)
            with act.Fori(0, PAIRS) as pair:
                def copy_z(u, half):
                    act.wait_ge(pv_done, PR + pair * NG + LAST[u] - (0 if half else 2) + 1)
                    if half == 0:
                        act.wait_ge(z_ready, pair * NU + u + 1)
                    q = slice(2 * half, 2 * half + 2)
                    act.activation(zs[u % 2][:, q, 0:VW - 1], zp[:, q, 0:VW - 1], ACT.Copy)\
                       .then_inc(z_copied, 1)

                for g in range(NG):
                    w = width(g)
                    scores = st[g % SR][:, 0:w] if w > P else st[g % SR][:, P:2 * P]
                    act.wait_ge(st_done, pair * NG + g + 1)
                    act.wait_ge(pv_done, pair * NG + g + 1)
                    act.activation(phi[g % PR][:, 0:w], scores, ACT.Exp, scale=SCALE)
                    act.activation(p32[g % PR][:, 0:w], scores, ACT.Exp, scale=SCALE)\
                       .then_inc(exp_done, 1)
                    for half in range(2):
                        if g - LAG + 2 - 2 * half in LAST:
                            copy_z(LAST.index(g - LAG + 2 - 2 * half), half)
                for half in range(LAG < 3, 2):
                    copy_z(NU - 1, half)

        @block.vector
        def _(dve):
            dve.sem_inc(sq_read, SR)
            dve.wait_ge(fill_done, 6)

            def item(pair, n):
                it = ORDER[n]
                u = it[1]
                head, j = divmod(u, NB)
                head %= 2
                dve.wait_ge(sq_done, pair * NI + n + 1)
                if it[0] == "max":
                    q, kb = it[2:]
                    dve.reduce_max(mpart[u % 2][:, q, kb:kb + 1],
                                   sq[n % SR][:, 0:BLK if kb < j else (q + 1) * P],
                                   AX.X).then_inc(sq_read, 1)
                    if (q, kb) == (TPB - 1, j):
                        dve.wait_ge(sq_read, SR + pair * NI + n + 1)
                        dve.reduce_max(m4[u % 2][:, :], mpart[u % 2][:, :, 0:j + 1], AX.X)\
                           .then_inc(m4_done, 1)
                else:
                    dve.tensor_scalar(q1[head][DH:DH + 1, j * BLK:(j + 1) * BLK],
                                      sq[n % SR][0:1, :], -1.0, P_SHIFT, ALU.mult, ALU.add)\
                       .then_inc(sq_read, 1)

            def low_p(pair, g):
                w = width(g)
                if not by_pool(g):
                    dve.wait_ge(exp_done, SR + pair * NG + g + 1)
                    dve.tensor_tensor(plo[g % PR][:, 0:w], p32[g % PR][:, 0:w],
                                      phi[g % PR][:, 0:w], ALU.subtract).then_inc(plo_dve, 1)

            def inverse_sums(pair, u):
                dve.wait_ge(z_copied, 2 + 2 * (pair * NU + u) + 2)
                dve.reciprocal(rl[u % 2][:, :], zs[u % 2][:, :, VONE]).then_inc(r_done, 1)

            def iteration(pair, final):
                n = len(AHEAD)
                for g in range(NG):
                    mine = [m for m in range(n, n + len(CARRIED[g]))
                            if not (final and ORDER[m][1] >= NU)]
                    n += len(CARRIED[g])
                    cut = (len(mine) + 1) // 2
                    for m in mine[:cut]:
                        item(pair, m)
                    if g > 0:
                        low_p(pair, g - 1)
                    for m in mine[cut:]:
                        item(pair, m)
                    if g - LAG - 1 in LAST:
                        inverse_sums(pair, LAST.index(g - LAG - 1))
                low_p(pair, NG - 1)
                inverse_sums(pair, NU - 1)
                if LEFT and not final:
                    dve.wait_ge(sq_read, SR + pair * NI + len(ORDER))
                    dve.sem_inc(sq_read, LEFT)

            for n in range(len(AHEAD)):
                item(0, n)
            with dve.Fori(0, PAIRS - 1) as pair:
                iteration(pair, False)
            iteration(PAIRS - 1, True)

        @block.tensor
        def _(pe):
            pe.sem_inc(pv_done, PR)
            pe.wait_ge(fill_done, 6)

            def item(pair, n):
                it = ORDER[n]
                u = it[1]
                head, j = divmod(u, NB)
                if it[0] == "max" and j == 0 and it[2:] == (0, 0):
                    pe.wait_ge(kqv_in[head % 2], (pair + 1 + head // 2) * (LOADS * 16))
                head %= 2
                pe.wait_ge(sq_read, pair * NI + n + 1)
                if it[0] == "max":
                    q, kb = it[2:]
                    w = BLK if kb < j else (q + 1) * P
                    wide = max(w, 2 * P)
                    last = pe.matmul(sq[n % SR][:, 0:wide],
                                     qq[head][:, j * BLK + q * P:j * BLK + (q + 1) * P],
                                     kk[head][:, kb * BLK:kb * BLK + wide],
                                     start=True, stop=kb < j)
                    if kb == j:
                        last = pe.matmul(sq[n % SR][:, w - P:w], sh.identb[:, :],
                                         sh.mask_qk[:, :], start=False, stop=True)
                else:
                    pe.wait_ge(m4_done, pair * NU + u + 1)
                    for q in range(TPB):
                        last = pe.transpose(sq[n % SR][0:1, q * P:(q + 1) * P],
                                            m4[u % 2][:, q:q + 1], sh.identf[:, :])
                last.then_inc(sq_done, 1)

            def scores(g):
                u, head, j, kt, q0 = STEPS[g]
                q1st = min(q0, TPB - 2)
                at = (q0 - q1st) * P
                out = st[g % SR][:, 0:at + width(g)]
                keys = slice(kt * P, (kt + 1) * P)
                queries = slice(j * BLK + q1st * P, (j + 1) * BLK)
                pe.matmul(out, kk[head][:, keys], qq[head][:, queries], start=True, stop=False)
                last = pe.matmul(out, k1[head][:, keys], q1[head][:, queries],
                                 start=False, stop=kt < TPB * j)
                if kt >= TPB * j:
                    last = pe.matmul(st[g % SR][:, at:at + P], sh.identb[:, :],
                                     sh.mask_kq[:, :], start=False, stop=True)
                last.then_inc(st_done, 1)

            def p_v_waits(pair, g):
                if by_pool(g):
                    pe.wait_ge(plo_pool, pair * NPOOL + lows(g, True))
                else:
                    pe.wait_ge(plo_dve, pair * NDVE + lows(g, False))

            def p_v(pair, g):
                u, head, j, kt, q0 = STEPS[g]
                for q in range(q0, TPB):
                    c = (q - q0) * P
                    if g == FIRST[u] and q % 2 == 0:
                        pe.wait_ge(z_copied, 2 * (pair * NU + u) + q // 2 + 1)
                    pe.matmul(zp[:, q, 0:VW - 1], phi[g % PR][:, c:c + P],
                              v[head][:, kt, 0:VW - 1], start=(kt == 0 and q % 2 == 0),
                              stop=False, skip_group_check=True)
                    last = pe.matmul(zp[:, q, 0:VONE + 1], plo[g % PR][:, c:c + P],
                                     v[head][:, kt, 0:VONE + 1], start=False,
                                     stop=(kt == TPB * j + q), skip_group_check=True)
                last.then_inc(pv_done, 1)

            def iteration(pair, final):
                n = len(AHEAD)
                for g in range(NG):
                    u = STEPS[g][0]
                    if g == FIRST[u]:
                        pe.wait_ge(sq_read, SR + pair * NI + ORDER.index(("row", u)) + 1)
                    if g >= LAG:
                        p_v_waits(pair, g - LAG)
                    else:
                        pe.wait_ge(exp_done, pair * NG + g + 1)
                    scores(g)
                    for m in range(n, n + len(CARRIED[g])):
                        if not (final and ORDER[m][1] >= NU):
                            item(pair, m)
                    n += len(CARRIED[g])
                    if g >= LAG:
                        p_v(pair, g - LAG)
                for g in range(NG - LAG, NG):
                    p_v_waits(pair, g)
                    p_v(pair, g)
                if LEFT and not final:
                    pe.sem_inc(sq_done, LEFT)

            for n in range(len(AHEAD)):
                item(0, n)
            with pe.Fori(0, PAIRS - 1) as pair:
                iteration(pair, False)
            iteration(PAIRS - 1, True)


def mix_phase(nc, io, sh):
    with ExitStack() as ctx:
        def sb(name, shape, dt):
            return ctx.enter_context(nc.sbuf_tensor(name, shape, dt))

        def sem(name):
            return ctx.enter_context(nc.semaphore(name))

        def bank(name, shape=(P, 512)):
            return ctx.enter_context(nc.psum_tensor(name, list(shape), F32))

        raw = sb("mraw", [P, C, 512], F32)
        woh, wol = (sb(n, [P, C, D], F32R) for n in ("woh", "wol"))
        rw = sb("rw", [P, C, E], F32)
        rwh, rwl = (sb(n, [P, C, E], F32R) for n in ("rwh", "rwl"))
        rb = sb("rb", [E, 1], F32)
        ob = sb("ob", [P, D], F32)
        obg = sb("obg", [P, D], F32)
        z = sb("z", [P, TPB, D], F32)
        zh, zl = (sb(n, [P, C, BLK], F32R) for n in ("zh", "zl"))
        xt = [sb(f"xt{i}", [P, TPB, D], F32) for i in range(2)]
        bst = sb("bst2", [P, TPB, 6], F32)
        mv = sb("mv2", [P, TPB, 2], F32)
        sd = sb("sd2", [P, TPB], F32)
        rstd = sb("rstd2", [P, TPB], F32)
        xhat = sb("xhat2", [P, TPB, D], F32)
        h = sb("h", [P, TPB, D], F32)
        hh, hl = (sb(n, [P, C, BLK], F32R) for n in ("hh2", "hl2"))
        tz = [bank(f"tz{i}") for i in range(2)]
        th = [bank(f"th{i}") for i in range(2)]
        acc = [bank(f"macc{i}") for i in range(2)]
        lgt = sb("lgt", [E, S], F32)
        lg = bank("lg")
        lt = bank("lt")

        w_in = [sem(f"mw_in{i}") for i in range(3)]
        small_in = sem("small_in")
        z_in = sem("z_in")
        x_in = [sem(f"mx_in{i}") for i in range(2)]
        we_in = sem("we_in")
        w_scaled = sem("w_scaled")
        w_hi = sem("mw_hi")
        w_lo = sem("mw_lo")
        obg_done = sem("obg_done")
        tz_done = sem("tz_done")
        z_high = sem("z_high")
        z_low = sem("z_low")
        acc_done = sem("macc_done")
        x1_done = sem("x1_done")
        bn_done = sem("bn_done2")
        bn_seen = sem("bn_seen2")
        mv_done = sem("mv_done2")
        sd_done = sem("sd_done2")
        rstd_done = sem("rstd_done2")
        xhat_done = sem("xhat_done2")
        h_done = sem("h_done")
        x1o_done = sem("x1o_done")
        x1_sent = sem("x1_sent")
        th_done = sem("th_done")
        h_high = sem("h_high2")
        h_low = sem("h_low2")
        h_sent = sem("h_sent")
        lg_done = sem("lg_done")
        lg_read = sem("lg_read")
        lt_done = sem("lt_done")

        block = ctx.enter_context(nc.Block())

        @block.sync
        def _(sp):
            sp.dma_start(raw[:, :, :], io.wo).then_inc(w_in[0], 16)
            sp.dma_start(z[:, :, :], io.z_scr[0]).then_inc(z_in, 16)
            sp.dma_start(xt[0][:, :, :], io.x[0]).then_inc(x_in[0], 16)
            sp.dma_start(rw[:, :, :], io.rw).then_inc(w_in[2], 16)
            sp.dma_start(rb[:, :], io.rb).then_inc(small_in, 16)
            sp.dma_start(ob[:, :], io.ob.broadcast_to([P, D])).then_inc(small_in, 16)
            sp.dma_start(xt[1][:, :, :], io.x[1]).then_inc(x_in[1], 16)
            sp.wait_ge(w_lo, 1)
            sp.dma_start(raw[:, :, :], io.ow).then_inc(w_in[1], 16)

            def step(b, s, ahead, ahead2):
                if ahead:
                    sp.wait_ge(tz_done, (b + 1) * C)
                    sp.dma_start(z[:, :, :], io.z_scr[b + 1]).then_inc(z_in, 16)
                sp.dma_start(sh.weraw[:, b, :, :], io.we[b]).then_inc(we_in, 16)
                sp.wait_ge(x1o_done, b + 1)
                sp.dma_start(io.x1_scr[b], xt[s][:, :, :]).then_inc(x1_sent, 16)
                if ahead2:
                    sp.wait_ge(x1_sent, (b + 1) * 16)
                    sp.dma_start(xt[s][:, :, :], io.x[b + 2]).then_inc(x_in[s], 16)
                sp.wait_ge(h_done, b + 1)
                sp.dma_start(io.h_scr[bass.ds(b * BLK, BLK), :].rearrange("(t p) d -> p t d", p=P),
                             h[:, :, :]).then_inc(h_sent, 16)

            with sp.Fori(0, NB // 2 - 1) as it:
                for s in range(2):
                    step(2 * it + s, s, True, True)
            for s in range(2):
                step(NB - 2 + s, s, s == 0, False)
            sp.wait_ge(we_in, NB * 16)
            sp.wait_ge(x1_sent, NB * 16)
            sp.wait_ge(h_sent, 16 + NB * 16)

        @block.gpsimd
        def _(pool):
            pool.wait_ge(small_in, 32)
            pool.tensor_tensor(obg[:, :], ob[:, :], sh.gb[:, :], ALU.mult).then_inc(obg_done, 1)
            pool.wait_ge(obg_done, 1)

            def residual(b, s):
                pool.wait_ge(xhat_done, (b + 1) * TPB)
                for t in range(TPB):
                    last = pool.tensor_tensor(xt[s][:, t, :], xt[s][:, t, :], obg[:, :], ALU.add)
                last.then_inc(x1o_done, 1)

            with pool.Fori(0, NB // 2) as it:
                for s in range(2):
                    residual(2 * it + s, s)

        @block.scalar
        def _(act):
            act.sem_inc(h_sent, 16)
            act.sem_inc(lg_read, 1)

            act.wait_ge(w_scaled, 1)
            act.activation(woh[:, :, :], raw[:, :, :], ACT.Copy).then_inc(w_hi, 1)

            def z_stage(b):
                for c in range(C):
                    act.wait_ge(tz_done, b * C + c + 1)
                    act.activation(zh[:, c, :], tz[c % 2][:, :], ACT.Copy).then_inc(z_high, 1)

            def o_stage(b):
                act.wait_ge(mv_done, b + 1)
                act.activation(sd[:, :], mv[:, :, 1], ACT.Sqrt, bias=sh.eps[:, 0:1])\
                   .then_inc(sd_done, 1)

            def h_stage(b):
                act.wait_ge(lg_done, b)
                for c in range(C):
                    act.wait_ge(th_done, b * C + c + 1)
                    act.activation(hh[:, c, :], th[c % 2][:, :], ACT.Copy).then_inc(h_high, 1)

            def r_stage(b):
                act.wait_ge(lg_done, b + 1)
                act.activation(lgt[:, bass.ds(b * BLK, BLK)], lg[0:E, :], ACT.Identity,
                               bias=rb[:, 0:1]).then_inc(lg_read, 1)

            z_stage(0)
            act.wait_ge(w_in[2], 16)
            act.activation(rwh[:, :, :], rw[:, :, :], ACT.Copy).then_inc(w_hi, 1)
            act.wait_ge(small_in, 32)
            o_stage(0)
            act.wait_ge(w_scaled, 2)
            act.activation(sh.owh[:, :, :], raw[:, :, :], ACT.Copy).then_inc(w_hi, 1)

            def step(b, ahead):
                if ahead:
                    z_stage(b + 1)
                h_stage(b)
                if ahead:
                    o_stage(b + 1)
                r_stage(b)

            with act.Fori(0, NB // 2 - 1) as it:
                for s in range(2):
                    step(2 * it + s, True)
            for s in range(2):
                step(NB - 2 + s, s == 0)
            act.wait_ge(lt_done, 1)
            act.activation(sh.logits[:, :, :], lt[:, 0:KT * E].rearrange("p (t e) -> p t e", e=E),
                           ACT.Copy)

        @block.vector
        def _(dve):
            dve.sem_inc(z_low, 2)
            dve.sem_inc(x1_done, 2)
            dve.sem_inc(h_low, 2)

            def scaled(k, g):
                dve.wait_ge(w_in[k], 16)
                for c in range(C):
                    last = dve.tensor_tensor(raw[:, c, :], raw[:, c, :], g[:, :], ALU.mult)
                last.then_inc(w_scaled, 1)

            def low(k, wl, wh, n):
                dve.wait_ge(w_hi, n)
                dve.tensor_tensor(wl[:, :, :], raw[:, :, :], wh[:, :, :].bitcast(F32),
                                  ALU.subtract).then_inc(w_lo, 1)

            def z_stage(b):
                for c in range(C):
                    dve.wait_ge(z_high, b * C + c + 1)
                    dve.tensor_tensor(zl[:, c, :], tz[c % 2][:, :], zh[:, c, :].bitcast(F32),
                                      ALU.subtract).then_inc(z_low, 1)

            def o_stage(b, s, x_count):
                dve.wait_ge(x_in[s], x_count)
                for t in range(TPB):
                    dve.wait_ge(acc_done, b * TPB + t + 1)
                    dve.tensor_tensor(xt[s][:, t, :], acc[t % 2][:, :], xt[s][:, t, :], ALU.add)\
                       .then_inc(x1_done, 1)
                    dve.wait_ge(x1_done, 2 + b * TPB + t + 1)
                    dve.bn_stats(bst[:, t, :], xt[s][:, t, :]).then_inc(bn_done, 1)
                dve.wait_ge(bn_done, b * TPB + TPB)
                dve.sem_inc(bn_seen, 1)
                for t in range(TPB):
                    last = dve.bn_aggr(mv[:, t, :], bst[:, t, :])
                last.then_inc(mv_done, 1)
                dve.wait_ge(mv_done, b + 1)
                for t in range(TPB):
                    dve.scalar_tensor_tensor(xhat[:, t, :], xt[s][:, t, :], mv[:, t, 0:1],
                                             sh.cb1[:, :], ALU.subtract, ALU.mult)\
                       .then_inc(xhat_done, 1)
                dve.wait_ge(sd_done, b + 1)
                dve.reciprocal(rstd[:, :], sd[:, :]).then_inc(rstd_done, 1)
                dve.wait_ge(rstd_done, b + 1)
                dve.wait_ge(xhat_done, b * TPB + TPB)
                if not isinstance(b, int) or b > 0:
                    dve.wait_ge(th_done, b * C)
                dve.wait_ge(h_sent, b * 16 + 16)
                for t in range(TPB):
                    last = dve.scalar_tensor_tensor(h[:, t, :], xhat[:, t, :], rstd[:, t:t + 1],
                                                    sh.sb[:, :], ALU.mult, ALU.add)
                last.then_inc(h_done, 1)

            def h_stage(b):
                for c in range(C):
                    dve.wait_ge(h_high, b * C + c + 1)
                    dve.tensor_tensor(hl[:, c, :], th[c % 2][:, :], hh[:, c, :].bitcast(F32),
                                      ALU.subtract).then_inc(h_low, 1)

            scaled(0, sh.ga)
            low(0, wol, woh, 1)
            z_stage(0)
            dve.wait_ge(w_hi, 2)
            dve.tensor_tensor(rwl[:, :, :], rw[:, :, :], rwh[:, :, :].bitcast(F32),
                              ALU.subtract).then_inc(w_lo, 1)
            o_stage(0, 0, 16)
            scaled(1, sh.gb)
            low(1, sh.owl, sh.owh, 3)

            def step(b, s, ahead, x_count):
                if ahead:
                    z_stage(b + 1)
                h_stage(b)
                if ahead:
                    o_stage(b + 1, 1 - s, x_count)

            with dve.Fori(0, NB // 2 - 1) as it:
                step(2 * it, 0, True, it * 16 + 16)
                step(2 * it + 1, 1, True, it * 16 + 32)
            step(NB - 2, 0, True, NB // 2 * 16)
            step(NB - 1, 1, False, 0)

        @block.tensor
        def _(pe):
            def z_stage(b):
                pe.wait_ge(z_in, b * 16 + 16)
                for c in range(C):
                    pe.wait_ge(z_low, b * C + c + 1)
                    for t in range(TPB):
                        last = pe.transpose(tz[c % 2][:, t * P:(t + 1) * P],
                                            z[:, t, c * P:(c + 1) * P], sh.identf[:, :])
                    last.then_inc(tz_done, 1)

            def h_stage(b):
                pe.wait_ge(h_done, b + 1)
                for c in range(C):
                    pe.wait_ge(h_low, b * C + c + 1)
                    for t in range(TPB):
                        last = pe.transpose(th[c % 2][:, t * P:(t + 1) * P],
                                            h[:, t, c * P:(c + 1) * P], sh.identf[:, :])
                    last.then_inc(th_done, 1)

            def o_stage(b):
                pe.wait_ge(z_low, 2 + (b + 1) * C)
                for t in range(TPB):
                    pe.wait_ge(x1_done, b * TPB + t + 1)
                    tok = slice(t * P, (t + 1) * P)
                    three_terms(pe, acc[t % 2][:, :], lambda c: zh[:, c, tok],
                                lambda c: zl[:, c, tok], lambda c: woh[:, c, :],
                                lambda c: wol[:, c, :]).then_inc(acc_done, 1)

            def r_stage(b):
                pe.wait_ge(h_low, 2 + (b + 1) * C)
                pe.wait_ge(lg_read, b + 1)
                three_terms(pe, lg[0:E, :], lambda c: rwh[:, c, :], lambda c: rwl[:, c, :],
                            lambda c: hh[:, c, :], lambda c: hl[:, c, :]).then_inc(lg_done, 1)

            def step(b, ahead):
                if ahead:
                    z_stage(b + 1)
                h_stage(b)
                if ahead:
                    o_stage(b + 1)
                r_stage(b)

            z_stage(0)
            pe.wait_ge(w_lo, 1)
            o_stage(0)
            pe.wait_ge(w_lo, 2)
            with pe.Fori(0, NB // 2 - 1) as it:
                for s in range(2):
                    step(2 * it + s, True)
            for s in range(2):
                step(NB - 2 + s, s == 0)
            pe.wait_ge(lg_read, 1 + NB)
            for t in range(KT):
                last = pe.transpose(lt[:, t * E:(t + 1) * E], lgt[:, t * P:(t + 1) * P],
                                    sh.identf[0:E, 0:E])
            last.then_inc(lt_done, 1)

def experts_phase(nc, io, sh):
    N2 = 2 * KT
    with ExitStack() as ctx:
        def sb(name, shape, dt=F32):
            return ctx.enter_context(nc.sbuf_tensor(name, shape, dt))

        def sem(name):
            return ctx.enter_context(nc.semaphore(name))

        wel = sb("wel", [P, E, C, D], F32R)
        weh = sb("weh", [P, E, C, D], F32R)
        eb = sb("eb", [P, E, D])
        rank = sb("rank", [P, E])
        ones = sb("ones", [P, P], BF16)
        before = sb("before", [P, P], BF16)
        count = sb("count", [P, P])
        token = sb("token", [P, N2])
        big = [sb(f"big{i}", [P, KT, E]) for i in range(6)]
        row = [sb(f"row{i}", [P, KT]) for i in range(6)]
        gate = sb("gate", [P, 2, KT])
        sel = sb("sel", [P, KT, E], BF16)
        PAD = KT // 2
        EPAD = E // 2
        escan = [sb(f"escan{i}", [P, EPAD + E]) for i in range(2)]
        load, tiles, start = (sb(n, [P, E]) for n in ("load", "tiles", "start"))
        texp = sb("texp", [P, NTILE])
        expert = sb("expert", [P, NTILE], I32)
        slot = sb("slot", [P, N2])
        sloti, slotr, slott = (sb(n, [P, N2], I32) for n in ("sloti", "slotr", "slott"))
        slotu = sb("slotu", [P, N2], U32)
        srow, stile = (sb(n, [P, N2]) for n in ("srow", "stile"))
        HOT = 4
        ids = sb("ids", [P, NTILE], U32)
        R4 = 4
        at = [sb(f"at{i}", [P, 1], U32) for i in range(R4)]
        at2 = [sb(f"at2_{i}", [P, 1], U32) for i in range(R4)]
        ya = [sh.ga, sh.gb, sh.sb, sh.cb1]
        yb = [sb(f"yb{i}", [P, D]) for i in range(R4)]
        rhot = [y[:, 0:P] for y in ya]
        thot = [y[:, P:P + NTILE] for y in ya]
        scan = [y[:, 0:(PAD + KT) * E].rearrange("p (t e) -> p t e", e=E) for y in yb[0:2]]
        over = yb[2][:, 0:E * KT].rearrange("p (e t) -> p e t", t=KT)
        past = yb[3][:, 0:NTILE * (E - 1)].rearrange("p (t e) -> p t e", e=E - 1)
        gl = [sb(f"gl{i}", [P, D]) for i in range(R4)]
        hh = [sb(f"hh3_{i}", [P, C, P], F32R) for i in range(2)]
        hl = [sb(f"hl3_{i}", [P, C, P], F32R) for i in range(2)]
        tps = [ctx.enter_context(nc.psum_tensor(f"tps{i}", [P, C, P], F32)) for i in range(2)]
        acc = [ctx.enter_context(nc.psum_tensor(f"eacc{i}", [P, 512], F32)) for i in range(R4)]

        eb_in = sem("eb_in")
        fill_done = sem("fill_done3")
        const_mm = sem("const_mm")
        before_done = sem("before_done")
        chain = sem("chain")
        g_exp = sem("g_exp")
        rank_mm = sem("rank_mm")
        hots = sem("hots")
        ids_mm = sem("ids_mm")
        ids_done = sem("ids_done")
        we_hi = sem("we_hi")
        we_lo = sem("we_lo")
        at_done = sem("at_done")
        at_seen = sem("at_seen")
        ya_in = [sem(f"ya_in{i}") for i in range(R4)]
        y_in = [sem(f"y_in{i}") for i in range(R4)]
        turned = sem("turned")
        high = sem("high")
        low = sem("low")
        acc_done = sem("eacc_done")
        acc_read = sem("eacc_read")
        gelu_done = sem("gelu_done")
        y_sent = [sem(f"y_sent{i}") for i in range(R4)]
        scaled = sem("scaled")
        combined = sem("combined")
        x1_in = [sem(f"x1_in{i}") for i in range(R4)]
        out_sent = [sem(f"out_sent{i}") for i in range(R4)]

        LINKS_SEL, LINKS_SLOT = 20, 51

        block = ctx.enter_context(nc.Block())

        def loop(eng, count, body):
            with eng.Fori(0, count // R4 - 1) as it:
                for k in range(R4):
                    body(it * R4 + k, it, k, True)
            for k in range(R4):
                body(count - R4 + k, count // R4 - 1, k, k < R4 - 1)

        @block.sync
        def _(sp):
            sp.dma_start(eb[:, :, :], io.eb.unsqueeze(0).broadcast_to([P, E, D]))\
              .then_inc(eb_in, 16)

            def y_store(n, it, k, ahead):
                sp.wait_ge(gelu_done, n + 1)
                sp.dma_start(io.y_scr[bass.ds(n * P, P), :], gl[k][:, :]).then_inc(y_sent[k], 16)

            loop(sp, NTILE, y_store)
            for k in range(R4):
                sp.wait_ge(y_sent[k], 16 + NTILE // R4 * 16)
                sp.dma_start(gl[k][:, :], io.x1_scr[k // TPB, :, k % TPB, :])\
                  .then_inc(x1_in[k], 16)

            def result(n, b, t, ahead):
                sp.wait_ge(acc_read, R4 + NTILE + n + 1)
                sp.dma_start(io.out[b, :, t, :], gl[t][:, :]).then_inc(out_sent[t], 16)

            def next_x1(b, t):
                sp.wait_ge(out_sent[t], (b + 1) * 16)
                sp.dma_start(gl[t][:, :], io.x1_scr[b + 1, :, t, :]).then_inc(x1_in[t], 16)

            with sp.Fori(0, NB - 1) as b:
                for t in range(TPB):
                    result(b * TPB + t, b, t, True)
                    next_x1(b, t)
            for t in range(TPB):
                result((NB - 1) * TPB + t, NB - 1, t, False)
            for t in range(TPB):
                sp.wait_ge(out_sent[t], NB * 16)

        @block.gpsimd
        def _(pool):
            pool.memset(ones[:, :], 1.0).then_inc(fill_done, 1)
            for e in range(E):
                pool.memset(rank[:, e:e + 1], float(E - e)).then_inc(fill_done, 1)
            for t in scan:
                pool.memset(t[:, 0:PAD, :], 0.0).then_inc(fill_done, 1)
            for t in escan:
                pool.memset(t[:, 0:EPAD], 0.0).then_inc(fill_done, 1)
            for e in range(E):
                pool.wait_ge(we_hi, e + 1)
                pool.tensor_tensor(wel[:, e, :, :], sh.weraw[:, e, :, :],
                                   weh[:, e, :, :].bitcast(F32), ALU.subtract)\
                    .then_inc(we_lo, 1)

            pool.wait_ge(ids_done, 1)

            def gather_h(n, it, k, ahead):
                pool.wait_ge(turned, n + 1)
                pool.tensor_copy(at[k][:, :], ids[:, bass.ds(n, 1)]).then_inc(at_done, 1)
                pool.wait_ge(at_done, n + 1)
                pool.sem_inc(at_seen, 1)
                pool.indirect_dma_start(ya[k][:, :], None, io.h_scr,
                                        bass.IndirectOffsetOnAxis(ap=at[k][:, 0:1], axis=0))\
                    .then_inc(ya_in[k], 16)

            loop(pool, NTILE, gather_h)
            for k in range(R4):
                pool.wait_ge(y_sent[k], 16 + NTILE // R4 * 16)

            def gather_y(n, it, k, ahead):
                pool.wait_ge(turned, NTILE + n + 1)
                pool.tensor_copy(at[k][:, :], slotu[:, bass.ds(n, 1)]).then_inc(at_done, 1)
                pool.tensor_copy(at2[k][:, :], slotu[:, bass.ds(n + KT, 1)]).then_inc(at_done, 1)
                pool.wait_ge(at_done, NTILE + 2 * n + 2)
                pool.sem_inc(at_seen, 1)
                for y, rows in ((ya, at), (yb, at2)):
                    pool.indirect_dma_start(y[k][:, :], None, io.y_scr,
                                            bass.IndirectOffsetOnAxis(ap=rows[k][:, 0:1], axis=0))\
                        .then_inc(y_in[k], 16)

            loop(pool, KT, gather_y)

        @block.scalar
        def _(act):
            for k in range(R4):
                act.sem_inc(y_sent[k], 16)

            act.wait_ge(chain, 2)
            act.activation(big[2][:, :, :], big[1][:, :, :], ACT.Exp).then_inc(g_exp, 1)
            for e in range(E):
                act.activation(weh[:, e, :, :], sh.weraw[:, e, :, :], ACT.Copy)\
                   .then_inc(we_hi, 1)

            def part(n, k):
                act.wait_ge(turned, R4 + n + 1)
                act.wait_ge(acc_done, n + 1)
                act.activation(hh[k % 2][:, :, :], tps[k % 2][:, :, :], ACT.Copy)\
                   .then_inc(high, 1)

            def expert_step(n, it, k, ahead):
                if ahead:
                    part(n + 1, k + 1)
                act.wait_ge(acc_read, R4 + n + 1)
                act.activation(gl[k][:, :], gl[k][:, :], ACT.Gelu_apprx_tanh)\
                   .then_inc(gelu_done, 1)

            def scale(n, it, k):
                act.wait_ge(y_in[k], it * 32 + 32)
                act.activation(ya[k][:, :], ya[k][:, :], ACT.Copy,
                               scale=gate[:, 0, bass.ds(n, 1)]).then_inc(scaled, 1)

            part(0, 0)
            loop(act, NTILE, expert_step)
            scale(0, 0, 0)
            scale(1, 0, 1)
            part(NTILE, 0)

            def out_step(n, it, k, last):
                if not last or k < 2:
                    scale(n + 2, it + (k + 2) // R4, (k + 2) % R4)
                if not last or k < 3:
                    part(NTILE + n + 1, k + 1)

            with act.Fori(0, KT // R4 - 1) as it:
                for k in range(R4):
                    out_step(it * R4 + k, it, k, False)
            for k in range(R4):
                out_step(KT - R4 + k, KT // R4 - 1, k, True)

        @block.vector
        def _(dve):
            dve.sem_inc(low, 2)
            dve.sem_inc(acc_read, R4)
            dve.tensor_scalar(before[:, :], sh.mask_qk[:, :], 0.0, None, ALU.is_lt)\
               .then_inc(before_done, 1)

            n = [0]

            def link(ins):
                n[0] += 1
                ins.then_inc(chain, 1)
                dve.wait_ge(chain, n[0])

            def wide(r):
                return r.unsqueeze(2).broadcast_to([P, KT, E])

            link(dve.reduce_max(row[0][:, :], sh.logits[:, :, :], AX.X))
            link(dve.tensor_tensor(big[1][:, :, :], sh.logits[:, :, :], wide(row[0][:, :]), ALU.subtract))
            dve.wait_ge(g_exp, 1)
            link(dve.reduce_sum(row[1][:, :], big[2][:, :, :], AX.X))
            link(dve.reciprocal(row[2][:, :], row[1][:, :]))
            link(dve.tensor_tensor(big[0][:, :, :], big[2][:, :, :], wide(row[2][:, :]),
                                   ALU.mult))
            ranks = rank[:, :].unsqueeze(1).broadcast_to([P, KT, E])
            dve.wait_ge(fill_done, 1 + E + 4)

            def best(probs, value, chosen):
                link(dve.reduce_max(value[:, :], probs, AX.X))
                link(dve.tensor_tensor(big[1][:, :, :], probs, wide(value[:, :]), ALU.is_equal))
                link(dve.tensor_tensor(big[2][:, :, :], big[1][:, :, :], ranks, ALU.mult))
                link(dve.reduce_max(row[5][:, :], big[2][:, :, :], AX.X))
                link(dve.tensor_tensor(chosen, big[2][:, :, :], wide(row[5][:, :]),
                                       ALU.is_equal))

            first, second = big[3], big[5]
            best(big[0][:, :, :], row[0], first[:, :, :])
            link(dve.scalar_tensor_tensor(big[4][:, :, :], first[:, :, :], -2.0,
                                          big[0][:, :, :], ALU.mult, ALU.add))
            best(big[4][:, :, :], row[1], second[:, :, :])
            link(dve.tensor_tensor(sel[:, :, :], first[:, :, :], second[:, :, :], ALU.add))
            link(dve.tensor_tensor(row[2][:, :], row[0][:, :], row[1][:, :], ALU.add))
            link(dve.reciprocal(row[3][:, :], row[2][:, :]))
            link(dve.tensor_tensor(gate[:, 0, :], row[0][:, :], row[3][:, :], ALU.mult))
            assert n[0] == LINKS_SEL, n[0]
            link(dve.tensor_tensor(gate[:, 1, :], row[1][:, :], row[3][:, :], ALU.mult))

            dve.wait_ge(const_mm, 1)
            link(dve.tensor_copy(count[:, :], acc[1][:, 0:P]))
            for i in range(2):
                link(dve.scalar_tensor_tensor(token[:, i * KT:(i + 1) * KT], count[:, 0:KT],
                                              float(P), acc[1][:, P:P + KT], ALU.mult, ALU.add))

            ahead_of, total = (acc[2][:, i * KT * E:(i + 1) * KT * E]
                               .rearrange("p (t e) -> p t e", e=E) for i in range(2))
            dve.wait_ge(rank_mm, 1)
            link(dve.tensor_copy(scan[0][:, PAD:, :], total))
            src, dst = scan
            shift = 1
            while shift < KT:
                link(dve.tensor_tensor(dst[:, PAD:, :], src[:, PAD:, :],
                                       src[:, PAD - shift:PAD + KT - shift, :], ALU.add))
                src, dst = dst, src
                shift *= 2
            upto = src
            link(dve.tensor_scalar(load[:, :], upto[:, PAD + KT - 1, :], 1.0 / P, None, ALU.mult))
            link(dve.tensor_tensor(over[:, :, :],
                                   count[:, 0:KT].unsqueeze(1).broadcast_to([P, E, KT]),
                                   load[:, :].unsqueeze(2).broadcast_to([P, E, KT]), ALU.is_lt))
            link(dve.reduce_sum(tiles[:, :], over[:, :, :], AX.X))
            link(dve.tensor_copy(escan[0][:, EPAD:], tiles[:, :]))
            esrc, edst = escan
            shift = 1
            while shift < E:
                link(dve.tensor_tensor(edst[:, EPAD:], esrc[:, EPAD:],
                                       esrc[:, EPAD - shift:EPAD + E - shift], ALU.add))
                esrc, edst = edst, esrc
                shift *= 2
            end = esrc[:, EPAD:]
            link(dve.tensor_tensor(start[:, :], end, tiles[:, :], ALU.subtract))
            link(dve.tensor_scalar(start[:, :], start[:, :], float(P), None, ALU.mult))
            link(dve.tensor_tensor(big[0][:, :, :], upto[:, PAD:, :], total, ALU.subtract))
            link(dve.tensor_tensor(big[1][:, :, :], big[0][:, :, :], ahead_of, ALU.add))
            link(dve.tensor_tensor(big[0][:, :, :], big[1][:, :, :],
                                   start[:, :].unsqueeze(1).broadcast_to([P, KT, E]), ALU.add))
            for i, chosen in enumerate((first, second)):
                link(dve.tensor_tensor(big[1][:, :, :], big[0][:, :, :], chosen[:, :, :],
                                       ALU.mult))
                link(dve.reduce_sum(slot[:, i * KT:(i + 1) * KT], big[1][:, :, :], AX.X))
            link(dve.tensor_copy(sloti[:, :], slot[:, :]))
            link(dve.tensor_scalar(slotr[:, :], sloti[:, :], P - 1, None, ALU.bitwise_and))
            link(dve.tensor_scalar(slott[:, :], sloti[:, :], P.bit_length() - 1, None,
                                   ALU.arith_shift_right))
            link(dve.tensor_copy(srow[:, :], slotr[:, :]))
            link(dve.tensor_copy(stile[:, :], slott[:, :]))
            assert n[0] == LINKS_SLOT, n[0]

            def one_hots(n, it, k, ahead):
                dve.wait_ge(ids_mm, n + 1)
                dve.tensor_scalar(rhot[k], count[:, :], srow[:, bass.ds(n, 1)], None,
                                  ALU.is_equal)
                dve.tensor_scalar(thot[k], count[:, 0:NTILE], stile[:, bass.ds(n, 1)],
                                  token[:, bass.ds(n, 1)], ALU.is_equal, ALU.mult)\
                   .then_inc(hots, 1)

            loop(dve, N2, one_hots)

            link(dve.tensor_copy(slotu[:, :], slot[:, :]))
            link(dve.tensor_tensor(past[:, :, :],
                                   end[:, 0:E - 1].unsqueeze(1).broadcast_to([P, NTILE, E - 1]),
                                   count[:, 0:NTILE].unsqueeze(2).broadcast_to([P, NTILE, E - 1]),
                                   ALU.is_le))
            link(dve.reduce_sum(texp[:, :], past[:, :, :], AX.X))
            link(dve.tensor_copy(expert[:, :], texp[:, :]))
            dve.wait_ge(ids_mm, HOT + N2)
            dve.tensor_copy(ids[:, :], acc[3][:, 0:NTILE]).then_inc(ids_done, 1)

            def part(n, k):
                dve.wait_ge(high, n + 1)
                dve.tensor_tensor(hl[k % 2][:, :, :], tps[k % 2][:, :, :],
                                  hh[k % 2][:, :, :].bitcast(F32), ALU.subtract).then_inc(low, 1)

            def expert_step(n, it, k, ahead):
                if ahead:
                    part(n + 1, k + 1)
                e = dve.value_load(expert[0:1, bass.ds(n, 1)], min_val=0, max_val=E - 1)
                dve.wait_ge(acc_done, 2 + n + 1)
                dve.wait_ge(y_sent[k], it * 16 + 16)
                dve.tensor_tensor(gl[k][:, :], acc[k][:, :], eb[:, bass.ds(e, 1), :]
                                  .rearrange("p a d -> p (a d)"), ALU.add).then_inc(acc_read, 1)

            def combine(n, k):
                dve.wait_ge(scaled, n + 1)
                dve.scalar_tensor_tensor(yb[k][:, :], yb[k][:, :], gate[:, 1, bass.ds(n, 1)],
                                         ya[k][:, :], ALU.mult, ALU.add).then_inc(combined, 1)

            part(0, 0)
            dve.wait_ge(eb_in, 16)
            loop(dve, NTILE, expert_step)
            combine(0, 0)
            combine(1, 1)
            part(NTILE, 0)

            def out_step(n, it, k, last):
                if not last or k < 2:
                    combine(n + 2, (k + 2) % R4)
                if not last or k < 3:
                    part(NTILE + n + 1, k + 1)
                dve.wait_ge(acc_done, 2 + NTILE + n + 1)
                dve.wait_ge(x1_in[k], it * 16 + 16)
                dve.tensor_tensor(gl[k][:, :], acc[k][:, :], gl[k][:, :], ALU.add)\
                   .then_inc(acc_read, 1)

            with dve.Fori(0, KT // R4 - 1) as it:
                for k in range(R4):
                    out_step(it * R4 + k, it, k, False)
            for k in range(R4):
                out_step(KT - R4 + k, KT // R4 - 1, k, True)

        @block.tensor
        def _(pe):
            pe.sem_inc(turned, R4)
            pe.sem_inc(acc_done, 2)
            pe.sem_inc(ids_mm, HOT)
            pe.wait_ge(fill_done, 1)
            pe.wait_ge(before_done, 1)
            pe.matmul(acc[1][:, 0:P], ones[:, :], before[:, :], start=True, stop=True)
            pe.matmul(acc[1][:, P:2 * P], before[:, :], ones[:, :], start=True, stop=True)\
              .then_inc(const_mm, 1)
            pe.wait_ge(chain, LINKS_SEL - 3)
            chosen = sel[:, :, :].rearrange("p t e -> p (t e)")
            pe.matmul(acc[2][:, 0:KT * E], before[:, :], chosen, start=True, stop=True)
            pe.matmul(acc[2][:, KT * E:2 * KT * E], ones[:, :], chosen, start=True, stop=True)\
              .then_inc(rank_mm, 1)

            def place(n, k, begin, end):
                pe.wait_ge(hots, n + 1)
                pe.matmul(acc[3][:, 0:NTILE], rhot[k], thot[k], start=begin,
                          stop=end).then_inc(ids_mm, 1)

            for k in range(HOT):
                place(k, k, k == 0, False)
            with pe.Fori(1, N2 // HOT - 1) as it:
                for k in range(HOT):
                    place(it * HOT + k, k, False, False)
            for k in range(HOT):
                place(N2 - HOT + k, k, False, k == HOT - 1)

            def turn(n, k, rows):
                pe.wait_ge(low, n + 1)
                for c in range(C):
                    last = pe.transpose(tps[k % 2][:, c, :], rows[k][:, c * P:(c + 1) * P],
                                        sh.identf[:, :])
                last.then_inc(turned, 1)

            def product(n, k, m_hi, m_lo):
                pe.wait_ge(low, 2 + n + 1)
                pe.wait_ge(acc_read, n + 1)
                three_terms(pe, acc[k][:, :], lambda c: hh[k % 2][:, c, :],
                            lambda c: hl[k % 2][:, c, :], m_hi, m_lo).then_inc(acc_done, 1)

            def gathered(it, k):
                pe.wait_ge(ya_in[k], it * 16 + 16)

            def expert_step(n, it, k, ahead):
                if ahead:
                    gathered(it + (k + 1) // R4, (k + 1) % R4)
                    turn(n + 1, (k + 1) % R4, ya)
                e = pe.value_load(expert[0:1, bass.ds(n, 1)], min_val=0, max_val=E - 1)
                product(n, k, lambda c: weh[:, bass.ds(e, 1), c, :],
                        lambda c: wel[:, bass.ds(e, 1), c, :])

            gathered(0, 0)
            turn(0, 0, ya)
            pe.wait_ge(we_lo, E)
            loop(pe, NTILE, expert_step)

            def out_step(n, it, k, ahead):
                if ahead:
                    pe.wait_ge(combined, n + 2)
                    turn(NTILE + n + 1, (k + 1) % R4, yb)
                product(NTILE + n, k, lambda c: sh.owh[:, c, :], lambda c: sh.owl[:, c, :])

            pe.wait_ge(combined, 1)
            turn(NTILE, 0, yb)
            loop(pe, KT, out_step)


class Holder:
    pass


def adaln_block(nc, arrays, out):
    io, sh = Holder(), Holder()

    def scratch(name, shape, dt=F32):
        return nc.dram_tensor(name, shape, dt, kind="Internal").ap()

    io.x = arrays["x"].rearrange("(b t p) d -> b p t d", t=TPB, p=P)
    io.out = out.rearrange("(b t p) d -> b p t d", t=TPB, p=P)
    io.c = arrays["c"]
    wide = "(c p) n -> p c n"
    io.wmod = [arrays["wmod"][:, m * D:(m + 1) * D].rearrange(wide, p=P) for m in range(6)]
    io.wk = [arrays["wk"].rearrange(wide, p=P)]
    io.wv = [arrays["wv"].rearrange(wide, p=P)]
    io.wq = [arrays["wq"][c * P:(c + 1) * P, :].rearrange("p (a n) -> p a n", a=C)
             for c in range(C)]
    io.wo = arrays["wo"].rearrange(wide, p=P)
    io.ow = arrays["ow"].rearrange(wide, p=P)
    io.we = arrays["we"].rearrange("e (c p) n -> e p c n", p=P)
    io.rw = arrays["rw"].rearrange(wide, p=P)
    io.rb, io.ob, io.eb = arrays["rb"], arrays["ob"], arrays["eb"]
    io.q_scr = scratch("q_scr", [2, PAIRS, P, S])
    io.k_scr = scratch("k_scr", [2, PAIRS, P, S])
    io.v_scr = scratch("v_scr", [P, HEADS, KT, VW], BF16)
    io.z_scr = scratch("z_scr", [NB, P, TPB, D])
    io.x1_scr = scratch("x1_scr", [NB, P, TPB, D])
    io.h_scr = scratch("h_scr", [S, D])
    io.y_scr = scratch("y_scr", [NTILE * P, D])

    with ExitStack() as ctx:
        def sb(name, shape, dt):
            return ctx.enter_context(nc.sbuf_tensor(name, shape, dt))

        sh.identf = sb("identf", [P, P], F32)
        sh.identb = sb("identb", [P, P], BF16)
        sh.mask_qk = sb("mask_qk", [P, P], BF16)
        sh.mask_kq = sb("mask_kq", [P, P], BF16)
        sh.eps = sb("eps", [P, 1], F32)
        sh.logits = sb("logits", [P, KT, E], F32)
        sh.ga, sh.gb, sh.sb, sh.cb1 = (sb(n, [P, D], F32) for n in ("ga", "gb", "sbv", "cb1"))
        project_phase(nc, io, sh)
        attend_phase(nc, io, sh)
        sh.owh, sh.owl = (sb(n, [P, C, D], F32R) for n in ("owh", "owl"))
        with nc.sbuf_tensor("weraw", [P, E, C, D], F32) as sh.weraw:
            mix_phase(nc, io, sh)
        experts_phase(nc, io, sh)


def kernel(**inputs):
    import numpy as np
    import concourse.bacc as bacc
    from concourse.bass_utils import run_bass_kernel_spmd

    f = {n.replace("L0_", ""): np.asarray(a) for n, a in inputs.items()}
    laid = {
        "x": f["attn_normalized_resid_pre"].reshape(S, D),
        "c": f["c"].reshape(C, P).T,
        "wmod": f["wmod"],
        "wq": f["attn_W_Q"].transpose(1, 0, 2).reshape(D, HEADS * GROUP * DH),
        "wk": f["attn_W_K"].transpose(1, 0, 2).reshape(D, HEADS * DH),
        "wv": f["attn_W_V"].transpose(1, 0, 2).reshape(D, HEADS * DH),
        "wo": f["attn_W_O"].reshape(HEADS * DH, D),
        "rw": f["ffn_router_w"],
        "rb": f["ffn_router_b"].reshape(E, 1),
        "we": f["ffn_expert_w"],
        "eb": f["ffn_expert_b"],
        "ow": f["ffn_out_w"],
        "ob": f["ffn_out_b"].reshape(1, D),
    }
    laid = {n: np.ascontiguousarray(a) for n, a in laid.items()}
    nc = bacc.Bacc("TRN2", target_bir_lowering=False, num_devices=1)
    aps = {n: nc.dram_tensor(f"in_{n}", a.shape, mybir.dt.from_np(a.dtype),
                             kind="ExternalInput").ap() for n, a in laid.items()}
    out = nc.dram_tensor("out", [S, D], F32, kind="ExternalOutput").ap()
    adaln_block(nc, aps, out)
    r = run_bass_kernel_spmd(nc, [{f"in_{n}": a for n, a in laid.items()}], core_ids=[0])
    return r.results[0]["out"].reshape(1, S, D)
```

```python
import math
from contextlib import ExitStack

import concourse.bass as bass
from concourse import mybir

F32 = mybir.dt.float32
F32R = mybir.dt.float32r
BF16 = mybir.dt.bfloat16
I32 = mybir.dt.int32
U32 = mybir.dt.uint32
FP16 = mybir.dt.float16
ALU = mybir.AluOpType
ACT = mybir.ActivationFunctionType
AX = mybir.AxisListType

P = 128
S = 4096
D = 512
C = D // P
BLK = 512
NB = S // BLK
TPB = BLK // P
HEADS = 8
GROUP = 4
DH = 64
PAIRS = HEADS // 2
KT = S // P
E = 8
NTILE = -(-((2 * S - E) // P + E) // 4) * 4
EPS = 1e-5
VHI, VMID, VONE, VLO = 0, DH, 2 * DH, 2 * DH + 1
VW = 3 * DH + 2
NEG = -1e30
SCALE = 1.0 / math.sqrt(DH)
P_SHIFT = 4 * math.log(2.0) / SCALE


def three_terms(pe, out, s_hi, s_lo, m_hi, m_lo):
    for c in range(C):
        for n, (s, m) in enumerate(((s_hi, m_hi), (s_hi, m_lo), (s_lo, m_hi))):
            last = pe.matmul(out, s(c), m(c), start=(c == 0 and n == 0),
                             stop=(c == C - 1 and n == 2))
    return last


def project_phase(nc, io, sh):
    with ExitStack() as ctx:
        def sb(name, shape, dt):
            return ctx.enter_context(nc.sbuf_tensor(name, shape, dt))

        def sem(name):
            return ctx.enter_context(nc.semaphore(name))

        RAW = 4
        raw = [sb(f"raw{i}", [P, C, 512], F32) for i in range(RAW)]
        wqh, wql, wkh, wkl, wvh, wvl = (sb(n, [P, C, 512], F32R)
                                        for n in ("wqh", "wql", "wkh", "wkl", "wvh", "wvl"))
        wsum = [sb(f"wsum{i}", [P, 512], F32) for i in range(4)]
        craw = sb("craw", [P, C], F32)
        cexp = sb("cexp", [P, C], F32)
        cden = sb("cden", [P, C], F32)
        cinv = sb("cinv", [P, C], F32)
        csilu = sb("csilu", [P, C], F32)
        cwide = sb("cwide", [P, C, P], F32)
        mrow = [sb(f"mrow{i}", [P, 512], F32) for i in range(4)]
        gneg, gabs, gsgn = (sb(n, [P, 512], F32) for n in ("gneg", "gabs", "gsgn"))
        sa = sb("sa", [P, C], F32)
        ca1 = sb("ca1", [P, C], F32)
        xb = [sb(f"xb{i}", [P, TPB, D], F32) for i in range(2)]
        bst = sb("bst", [P, TPB, 6], F32)
        mv = sb("mv", [P, TPB, 2], F32)
        sd = sb("sd", [P, TPB], F32)
        rstd = sb("rstd", [P, TPB], F32)
        xhat = sb("xhat", [P, TPB, D], F32)
        hf = [sb(f"hf{i}", [P, BLK], F32) for i in range(2)]
        hh = [sb(f"hh{i}", [P, C, BLK], F32R) for i in range(2)]
        hl = [sb(f"hl{i}", [P, C, BLK], F32R) for i in range(2)]
        QR = 4
        qh = [sb(f"qh{i}", [P, BLK], F32R) for i in range(QR)]
        ql = [sb(f"ql{i}", [P, BLK], F32R) for i in range(QR)]
        VR = 2
        vt = [sb(f"vt{i}", [P, HEADS, VW], BF16) for i in range(VR)]
        vr = [sb(f"vr{i}", [P, HEADS, DH], F32) for i in range(VR)]
        tp = [ctx.enter_context(nc.psum_tensor(f"tp{i}", [P, 512], F32)) for i in range(2)]
        NACC = 6
        acc = [ctx.enter_context(nc.psum_tensor(f"acc{i}", [P, 512], F32)) for i in range(NACC)]

        c_in = sem("c_in")
        x_in = [sem(f"x_in{i}") for i in range(2)]
        raw_in = [sem(f"raw_in{i}") for i in range(RAW)]
        raw_free = [sem(f"raw_free{i}") for i in range(RAW)]
        const_done = sem("const_done")
        c_exp = sem("c_exp")
        c_chain = sem("c_chain")
        cwide_done = sem("cwide_done")
        mod_mm = sem("mod_mm")
        mod_row = sem("mod_row")
        col_mm = sem("col_mm")
        col_done = sem("col_done")
        w_hi = sem("w_hi")
        w_lo = sem("w_lo")
        w_half = sem("w_half")
        w_sum = sem("w_sum")
        bn_done = sem("bn_done")
        bn_seen = sem("bn_seen")
        mv_done = sem("mv_done")
        sd_done = sem("sd_done")
        rstd_done = sem("rstd_done")
        xhat_done = sem("xhat_done")
        tp_done = sem("tp_done")
        h_high = sem("h_high")
        h_low = sem("h_low")
        acc_done = sem("acc_done")
        hi_out = sem("hi_out")
        acc_read = sem("acc_read")
        v_mid = sem("v_mid")
        v_ready = sem("v_ready")
        qk_sent = [sem(f"qk_sent{i}") for i in range(QR)]
        v_sent = [sem(f"v_sent{i}") for i in range(VR)]
        g_chain = sem("g_chain")

        NQK = 2 * PAIRS
        NIT = NQK + TPB
        HALF = NIT // 2
        X1_AFTER = 5
        PIECES = ([("mod", 0), ("mod", 1), ("wk", 0)] + [("wq", c) for c in range(C)]
                  + [("wv", 0)] + [("mod", m) for m in range(2, 6)])
        AT = {p: n for n, p in enumerate(PIECES)}

        def slot(kind, i=0):
            n = AT[kind, i]
            return n % RAW, 16 * (n // RAW + 1)

        block = ctx.enter_context(nc.Block())

        @block.sync
        def _(sp):
            sp.dma_start(craw[:, :], io.c).then_inc(c_in, 16)
            sp.dma_start(xb[0][:, :, :], io.x[0]).then_inc(x_in[0], 16)
            for n, (kind, i) in enumerate(PIECES):
                if n >= RAW:
                    sp.wait_ge(raw_free[n % RAW], n // RAW)
                src = {"mod": io.wmod, "wk": io.wk, "wv": io.wv, "wq": io.wq}[kind][i]
                sp.dma_start(raw[n % RAW][:, :, :], src).then_inc(raw_in[n % RAW], 16)
                if n == X1_AFTER:
                    sp.dma_start(xb[1][:, :, :], io.x[1]).then_inc(x_in[1], 16)

            def stores(b, s, ahead):
                if ahead:
                    sp.wait_ge(xhat_done, b + 1)
                    sp.dma_start(xb[s][:, :, :], io.x[b + 2]).then_inc(x_in[s], 16)
                for n in range(NQK):
                    dst = io.k_scr if n < PAIRS else io.q_scr
                    sp.wait_ge(acc_read, NACC + b * NIT + n + 1)
                    for part, t in enumerate((qh, ql)):
                        sp.dma_start(dst[part, n % PAIRS, :, bass.ds(b * BLK, BLK)],
                                     t[n % QR][:, :].bitcast(F32)).then_inc(qk_sent[n % QR], 16)
                for t in range(TPB):
                    sp.wait_ge(v_ready, b * TPB + t + 1)
                    sp.dma_start(io.v_scr[:, :, b * TPB + t, :], vt[t % VR][:, :, :])\
                      .then_inc(v_sent[t % VR], 16)

            with sp.Fori(0, NB // 2 - 1) as it:
                for s in range(2):
                    stores(2 * it + s, s, True)
            for s in range(2):
                stores(NB - 2 + s, s, False)
            for i in range(QR):
                sp.wait_ge(qk_sent[i], 32 + NB * (NQK // QR) * 32)
            for i in range(VR):
                sp.wait_ge(v_sent[i], 16 + NB * (TPB // VR) * 16)

        @block.gpsimd
        def _(pool):
            for m in (sh.identf, sh.identb, sh.mask_qk, sh.mask_kq):
                pool.memset(m[:, :], 0.0).then_inc(const_done, 1)
            pool.memset(sh.eps[:, :], EPS).then_inc(const_done, 1)
            for t in vt:
                pool.memset(t[:, :, :], 1.0).then_inc(const_done, 1)
            pool.wait_ge(const_done, 5 + VR)
            for m in (sh.identf, sh.identb):
                pool.affine_select(out=m[:, :], in_=m[:, :], compare_op=ALU.not_equal, fill=1.0,
                                   base=0, pattern=[[-1, P]], channel_multiplier=1)\
                    .then_inc(const_done, 1)
            pool.affine_select(out=sh.mask_qk[:, :], in_=sh.mask_qk[:, :], compare_op=ALU.is_ge,
                               fill=NEG, base=0, pattern=[[-1, P]], channel_multiplier=1)\
                .then_inc(const_done, 1)
            pool.affine_select(out=sh.mask_kq[:, :], in_=sh.mask_kq[:, :], compare_op=ALU.is_ge,
                               fill=NEG, base=0, pattern=[[1, P]], channel_multiplier=-1)\
                .then_inc(const_done, 1)

        CONST = 9 + VR

        @block.scalar
        def _(act):
            act.sem_inc(h_high, 2)
            for i in range(QR):
                act.sem_inc(qk_sent[i], 32)
            for i in range(VR):
                act.sem_inc(v_sent[i], 16)
            act.wait_ge(c_in, 16)
            act.activation(cexp[:, :], craw[:, :], ACT.Exp, scale=-1.0).then_inc(c_exp, 1)
            act.wait_ge(const_done, CONST)

            def std_dev(b):
                act.wait_ge(mv_done, b + 1)
                act.activation(sd[:, :], mv[:, :, 1], ACT.Sqrt, bias=sh.eps[:, 0:1])\
                   .then_inc(sd_done, 1)

            def modulate(b, s):
                for c in range(C):
                    act.wait_ge(tp_done, b * C + c + 1)
                    act.wait_ge(h_low, b * C + c + 1)
                    act.activation(hf[c % 2][:, :], tp[c % 2][:, :], ACT.Identity,
                                   scale=ca1[:, c:c + 1], bias=sa[:, c:c + 1])
                    act.activation(hh[s][:, c, :], tp[c % 2][:, :], ACT.Identity,
                                   scale=ca1[:, c:c + 1], bias=sa[:, c:c + 1]).then_inc(h_high, 1)

            def high_parts(b, lo, hi):
                for n in range(lo, hi):
                    act.wait_ge(acc_done, b * NIT + n + 1)
                    if n < NQK:
                        k = n % QR
                        act.wait_ge(qk_sent[k], (b * (NQK // QR) + n // QR) * 32 + 32)
                        act.activation(qh[k][:, :], acc[n % NACC][:, :], ACT.Copy)\
                           .then_inc(hi_out, 1)
                    else:
                        t = n - NQK
                        k = t % VR
                        act.wait_ge(v_sent[k], (b * (TPB // VR) + t // VR) * 16 + 16)
                        act.activation(vt[k][:, :, VHI:VHI + DH],
                                       acc[n % NACC][:, :].rearrange("p (h d) -> p h d", h=HEADS),
                                       ACT.Copy).then_inc(hi_out, 1)
                        act.wait_ge(acc_read, NACC + b * NIT + n + 1)
                        act.activation(vt[k][:, :, VMID:VMID + DH], vr[k][:, :, :], ACT.Copy)\
                           .then_inc(v_mid, 1)

            std_dev(0)
            act.wait_ge(col_done, 2)
            modulate(0, 0)

            def weights_high(w, kind):
                k, n = slot(kind)
                act.wait_ge(raw_in[k], n)
                act.activation(w[:, :, :], raw[k][:, :, :], ACT.Copy).then_inc(w_hi, 1)

            weights_high(wkh, "wk")
            for c in range(C):
                act.wait_ge(w_sum, c + 1)
                act.activation(wqh[:, c, :], wsum[2 + c % 2][:, :], ACT.Copy).then_inc(w_hi, 1)
            weights_high(wvh, "wv")

            def step(b, s, ahead):
                if ahead:
                    std_dev(b + 1)
                high_parts(b, 0, HALF)
                if ahead:
                    modulate(b + 1, 1 - s)
                high_parts(b, HALF, NIT)

            act.preload_act_table(ACT.Sqrt)
            with act.Fori(0, NB // 2 - 1) as it:
                for s in range(2):
                    step(2 * it + s, s, True)
            for s in range(2):
                step(NB - 2 + s, s, s == 0)

        @block.vector
        def _(dve):
            dve.sem_inc(acc_read, NACC)
            dve.sem_inc(h_low, 2)

            def layer_norm(b, s, x_count):
                dve.wait_ge(x_in[s], x_count)
                for t in range(TPB):
                    dve.bn_stats(bst[:, t, :], xb[s][:, t, :]).then_inc(bn_done, 1)
                dve.wait_ge(bn_done, b * TPB + TPB)
                dve.sem_inc(bn_seen, 1)
                for t in range(TPB):
                    last = dve.bn_aggr(mv[:, t, :], bst[:, t, :])
                last.then_inc(mv_done, 1)
                dve.wait_ge(sd_done, b + 1)
                dve.reciprocal(rstd[:, :], sd[:, :]).then_inc(rstd_done, 1)
                dve.wait_ge(rstd_done, b + 1)
                if not isinstance(b, int) or b > 0:
                    dve.wait_ge(tp_done, b * C)
                for t in range(TPB):
                    last = dve.tensor_scalar(xhat[:, t, :], xb[s][:, t, :], mv[:, t, 0:1],
                                             rstd[:, t:t + 1], ALU.subtract, ALU.mult)
                last.then_inc(xhat_done, 1)

            def low_h(b, s):
                for c in range(C):
                    dve.wait_ge(h_high, 2 + b * C + c + 1)
                    dve.tensor_tensor(hl[s][:, c, :], hf[c % 2][:, :],
                                      hh[s][:, c, :].bitcast(F32), ALU.subtract)\
                       .then_inc(h_low, 1)

            def low_parts(b, lo, hi):
                for n in range(lo, hi):
                    dve.wait_ge(hi_out, b * NIT + n + 1)
                    if n < NQK:
                        k = n % QR
                        dve.tensor_tensor(ql[k][:, :], acc[n % NACC][:, :],
                                          qh[k][:, :].bitcast(F32), ALU.subtract)\
                           .then_inc(acc_read, 1)
                    else:
                        t = n - NQK
                        k = t % VR
                        dve.tensor_tensor(vr[k][:, :, :],
                                          acc[n % NACC][:, :].rearrange("p (h d) -> p h d",
                                                                        h=HEADS),
                                          vt[k][:, :, VHI:VHI + DH], ALU.subtract)\
                           .then_inc(acc_read, 1)
                        dve.wait_ge(v_mid, b * TPB + t + 1)
                        dve.tensor_tensor(vt[k][:, :, VLO:VLO + DH], vr[k][:, :, :],
                                          vt[k][:, :, VMID:VMID + DH], ALU.subtract)\
                           .then_inc(v_ready, 1)

            dve.wait_ge(c_exp, 1)
            dve.tensor_scalar_add(cden[:, :], cexp[:, :], 1.0).then_inc(c_chain, 1)
            dve.wait_ge(c_chain, 1)
            dve.reciprocal(cinv[:, :], cden[:, :]).then_inc(c_chain, 1)
            dve.wait_ge(c_chain, 2)
            dve.tensor_tensor(csilu[:, :], craw[:, :], cinv[:, :], ALU.mult).then_inc(c_chain, 1)
            dve.wait_ge(c_chain, 3)
            for c in range(C):
                last = dve.tensor_copy(cwide[:, c, :], csilu[:, c:c + 1].broadcast_to([P, P]))
            last.then_inc(cwide_done, 1)
            layer_norm(0, 0, 16)

            def mod_sections(ms, bank0, cols):
                for i, m in enumerate(ms):
                    dve.wait_ge(mod_mm, m + 1)
                    dve.tensor_copy(mrow[i][:, :], acc[bank0 + i][:, :]).then_inc(mod_row, 1)
                for i, (col, dst, add) in enumerate(cols):
                    dve.wait_ge(col_mm, col + 1)
                    dve.tensor_scalar_add(dst[:, :], acc[bank0 + len(ms) + i][:, ::P], add)\
                       .then_inc(col_done, 1)

            mod_sections([0, 1], 0, [(0, sa, 0.0), (1, ca1, 1.0)])
            low_h(0, 0)

            def weights_low(w, wh, kind, high_parts_made):
                k, n = slot(kind)
                dve.wait_ge(raw_in[k], n)
                dve.wait_ge(w_hi, high_parts_made)
                dve.tensor_tensor(w[:, :, :], raw[k][:, :, :], wh[:, :, :].bitcast(F32),
                                  ALU.subtract).then_inc(raw_free[k], 1)

            weights_low(wkl, wkh, "wk", 1)
            for c in range(C):
                k, n = slot("wq", c)
                dve.wait_ge(raw_in[k], n)
                g = raw[k][:, :, :].rearrange("p a (b g d) -> p (a b) g d", g=GROUP, d=DH)

                def out(t):
                    return t[:, :].rearrange("p (n d) -> p n d", d=DH)

                dve.tensor_tensor(out(wsum[0]), g[:, :, 0, :], g[:, :, 1, :], ALU.add)\
                   .then_inc(w_half, 1)
                dve.tensor_tensor(out(wsum[1]), g[:, :, 2, :], g[:, :, 3, :], ALU.add)\
                   .then_inc(raw_free[k], 1)
                dve.wait_ge(w_half, c + 1)
                dve.wait_ge(raw_free[k], n // 16)
                dve.tensor_tensor(wsum[2 + c % 2][:, :], wsum[0][:, :], wsum[1][:, :], ALU.add)\
                   .then_inc(w_sum, 1)
                dve.wait_ge(w_sum, c + 1)
                dve.wait_ge(w_hi, 2 + c)
                dve.tensor_tensor(wql[:, c, :], wsum[2 + c % 2][:, :],
                                  wqh[:, c, :].bitcast(F32), ALU.subtract).then_inc(w_lo, 1)
            weights_low(wvl, wvh, "wv", C + 2)

            def step(b, s, ahead, x_count):
                if ahead:
                    layer_norm(b + 1, 1 - s, x_count)
                low_parts(b, 0, HALF)
                if ahead:
                    low_h(b + 1, 1 - s)
                low_parts(b, HALF, NIT)

            with dve.Fori(0, NB // 2 - 1) as it:
                step(2 * it, 0, True, it * 16 + 16)
                step(2 * it + 1, 1, True, it * 16 + 32)
            step(NB - 2, 0, True, NB // 2 * 16)
            step(NB - 1, 1, False, 0)

            def residual_gate(section, dst, n):
                g = acc[section - 2]
                dve.wait_ge(mod_mm, section + 1)
                dve.tensor_scalar(gneg[:, :], g[:, :], -1.0, None, ALU.mult).then_inc(g_chain, 1)
                dve.tensor_scalar(gsgn[:, :], g[:, :], 0.0, 2.0, ALU.is_ge, ALU.mult)\
                   .then_inc(g_chain, 1)
                dve.wait_ge(g_chain, n + 2)
                dve.tensor_tensor(gabs[:, :], g[:, :], gneg[:, :], ALU.max).then_inc(g_chain, 1)
                dve.wait_ge(g_chain, n + 3)
                dve.tensor_scalar(gneg[:, :], gabs[:, :], 0.25, None, ALU.max)\
                   .then_inc(g_chain, 1)
                dve.wait_ge(g_chain, n + 4)
                dve.scalar_tensor_tensor(dst[:, :], gsgn[:, :], -1.0, gneg[:, :], ALU.add,
                                         ALU.mult).then_inc(g_chain, 1)
                dve.wait_ge(g_chain, n + 5)

            residual_gate(2, sh.ga, 0)
            dve.wait_ge(mod_mm, 4)
            dve.tensor_copy(sh.sb[:, :], acc[1][:, :])
            dve.wait_ge(mod_mm, 5)
            dve.tensor_scalar_add(sh.cb1[:, :], acc[2][:, :], 1.0)
            residual_gate(5, sh.gb, 5)

        @block.tensor
        def _(pe):
            def mod_section(m, bank):
                k, n = slot("mod", m)
                pe.wait_ge(raw_in[k], n)
                for c in range(C):
                    last = pe.matmul(acc[bank][:, :], cwide[:, c, :], raw[k][:, c, :],
                                     start=(c == 0), stop=(c == C - 1))
                last.then_inc(mod_mm, 1)
                pe.wait_ge(mod_mm, m + 1)
                pe.sem_inc(raw_free[k], 1)

            def column(row, bank, row_count):
                pe.wait_ge(mod_row, row_count)
                for c in range(C):
                    last = pe.transpose(acc[bank][:, c * P:(c + 1) * P],
                                        mrow[row][:, c * P:(c + 1) * P], sh.identf[:, :])
                last.then_inc(col_mm, 1)

            def transposes(b):
                pe.wait_ge(xhat_done, b + 1)
                for c in range(C):
                    pe.wait_ge(h_high, b * C + c + 1)
                    for t in range(TPB):
                        last = pe.transpose(tp[c % 2][:, t * P:(t + 1) * P],
                                            xhat[:, t, c * P:(c + 1) * P], sh.identf[:, :])
                    last.then_inc(tp_done, 1)

            def wait_weights(kind):
                k, n = slot(kind)
                pe.wait_ge(raw_free[k], n // 16)

            def products(b, s, lo, hi):
                pe.wait_ge(h_low, 2 + (b + 1) * C)
                for n in range(lo, hi):
                    pe.wait_ge(acc_read, b * NIT + n + 1)
                    if n == PAIRS:
                        pe.wait_ge(w_lo, C)
                    if n == NQK:
                        wait_weights("wv")
                    if n < NQK:
                        wh, wl = (wkh, wkl) if n < PAIRS else (wqh, wql)
                        j = n % PAIRS * P
                        last = three_terms(pe, acc[n % NACC][:, :],
                                           lambda c: wh[:, c, j:j + P], lambda c: wl[:, c, j:j + P],
                                           lambda c: hh[s][:, c, :], lambda c: hl[s][:, c, :])
                    else:
                        j = (n - NQK) * P
                        last = three_terms(pe, acc[n % NACC][:, :],
                                           lambda c: hh[s][:, c, j:j + P],
                                           lambda c: hl[s][:, c, j:j + P],
                                           lambda c: wvh[:, c, :], lambda c: wvl[:, c, :])
                    last.then_inc(acc_done, 1)

            def step(b, s, ahead):
                products(b, s, 0, HALF)
                if ahead:
                    transposes(b + 1)
                products(b, s, HALF, NIT)

            pe.wait_ge(const_done, CONST)
            pe.wait_ge(cwide_done, 1)
            for m in range(2):
                mod_section(m, m)
            for m in range(2):
                column(m, 2 + m, m + 1)
            transposes(0)
            pe.wait_ge(col_done, 2)
            wait_weights("wk")
            with pe.Fori(0, NB // 2 - 1) as it:
                for s in range(2):
                    step(2 * it + s, s, True)
            for s in range(2):
                step(NB - 2 + s, s, s == 0)
            pe.wait_ge(acc_read, NACC + NB * NIT)
            for m in range(2, 6):
                mod_section(m, m - 2)


LAG = 4
CAP = (1, 2, 3, 2)
NEXT = 3
TAIL = 2
LEAD = 6
POOL_EVERY = 4


def attention_schedule():
    steps, first, last = [], [], []
    for head in range(2):
        for j in range(NB):
            first.append(len(steps))
            tiles = list(range(TPB * (j + 1)))
            if j > 0:
                full, short = tiles[:-TPB + 1], tiles[-TPB + 1:]
                tiles = full[:-1] + short[:-TAIL] + full[-1:] + short[-TAIL:]
            steps += [(head * NB + j, head, j, kt, max(0, kt - TPB * j)) for kt in tiles]
            last.append(len(steps) - 1)

    def items(u):
        return ([("max", u, q, kb) for q in range(TPB) for kb in range(u % NB + 1)]
                + [("row", u)])

    units = len(first)
    todo = [(max(0, first[u] - LEAD), it) for u in range(NEXT, units) for it in items(u)]
    todo += [(len(steps) - 1, it) for u in range(units, units + NEXT) for it in items(u)]
    carried = [[] for _ in steps]
    for g in reversed(range(len(steps))):
        while todo and todo[-1][0] >= g and (len(carried[g]) < CAP[steps[g][4]] or g == 0):
            carried[g].insert(0, todo.pop()[1])
    return steps, first, last, [it for u in range(NEXT) for it in items(u)], carried


def attend_phase(nc, io, sh):
    STEPS, FIRST, LAST, AHEAD, CARRIED = attention_schedule()
    ORDER = AHEAD + [it for c in CARRIED for it in c]
    NG = len(STEPS)
    NU = len(FIRST)
    ST, SQ = 3, 3
    NI = -(-(len(ORDER) - len(AHEAD)) // SQ) * SQ
    LEFT = NI - (len(ORDER) - len(AHEAD))
    with ExitStack() as ctx:
        def sb(name, shape, dt):
            return ctx.enter_context(nc.sbuf_tensor(name, shape, dt))

        def sem(name):
            return ctx.enter_context(nc.semaphore(name))

        kk, k1, qq, q1 = ([sb(f"{n}{i}", [P, S], F32R) for i in range(2)]
                          for n in ("kk", "k1_", "qq", "q1_"))
        v = [sb(f"v{i}", [P, KT, VW], BF16) for i in range(2)]
        PR = 6
        p32 = [sb(f"p32_{i}", [P, BLK], F32) for i in range(PR)]
        phi = [sb(f"phi{i}", [P, BLK], FP16) for i in range(PR)]
        plo = [sb(f"plo{i}", [P, BLK], FP16) for i in range(PR)]
        mpart = [sb(f"mpart{i}", [P, TPB, NB], F32) for i in range(2)]
        m4 = [sb(f"m4_{i}", [P, TPB], F32) for i in range(2)]
        zs = [sb(f"zs{i}", [P, TPB, VW], F32) for i in range(2)]
        rl = [sb(f"rl{i}", [P, TPB], F32) for i in range(2)]
        zt = [sb(f"zt{i}", [P, TPB, DH], F32) for i in range(2)]
        zo = [sb(f"zo{i}", [P, TPB, DH], F32) for i in range(2)]
        st = [ctx.enter_context(nc.psum_tensor(f"st{i}", [P, BLK], F32)) for i in range(ST)]
        zp = ctx.enter_context(nc.psum_tensor("zp", [P, TPB, 256], F32))
        sq = [ctx.enter_context(nc.psum_tensor(f"sq{i}", [P, BLK], F32)) for i in range(SQ)]

        early_in = sem("early_in")
        kqv_in = [sem(f"kqv_in{i}") for i in range(2)]
        k1_zero = sem("k1_zero")
        k1_fill = sem("k1_fill")
        q1_first = sem("q1_first")
        q1_fill = sem("q1_fill")
        sq_done = sem("sq_done")
        sq_read = sem("sq_read")
        m4_done = sem("m4_done")
        st_done = sem("st_done")
        exp_done = sem("exp_done")
        plo_dve = sem("plo_dve")
        plo_pool = sem("plo_pool")
        pv_done = sem("pv_done")
        z_copied = sem("z_copied")
        r_done = sem("r_done")
        z_chain = sem("z_chain")
        z_ready = sem("z_ready")
        z_sent = [sem(f"z_sent{i}") for i in range(2)]
        LOADS = 7
        PARTS = ((0, slice(0, NEXT * BLK)), (0, slice(NEXT * BLK, S)), (1, slice(0, S)))
        ROW_FILLS = {NEXT: 1, NB: 2}

        def width(g):
            return BLK - STEPS[g][4] * P

        def by_pool(g):
            return g % POOL_EVERY == 1 and width(g) == BLK

        def lows(g, pool):
            return sum(by_pool(x) == pool for x in range(g + 1))

        NPOOL = lows(NG - 1, True)
        NDVE = NG - NPOOL

        block = ctx.enter_context(nc.Block())

        @block.sync
        def _(sp):
            def load(pair, i, cols, landed):
                rows = slice(i * DH, (i + 1) * DH)
                tiles = slice(cols.start // P, cols.stop // P)
                for dst, lo, src, part in ((kk, 0, io.k_scr, 0), (kk, DH, io.k_scr, 1),
                                           (qq, 0, io.q_scr, 0), (qq, DH, io.q_scr, 0),
                                           (k1, 0, io.k_scr, 0), (q1, 0, io.q_scr, 1)):
                    sp.dma_start(dst[i][lo:lo + DH, cols].bitcast(F32),
                                 src[part, pair, rows, cols]).then_inc(landed, 16)
                sp.dma_start(v[i][:, tiles, :], io.v_scr[:, 2 * pair + i, tiles, :])\
                  .then_inc(landed, 16)

            def store(pair, u):
                i, j = divmod(u, NB)
                sp.wait_ge(z_ready, 2 + pair * NU + u + 1)
                sp.dma_start(io.z_scr[j, :, :, bass.ds((2 * pair + i) * DH, DH)],
                             zo[u % 2][:, :, :]).then_inc(z_sent[u % 2], 16)

            load(0, 0, PARTS[0][1], early_in)
            load(0, 0, PARTS[1][1], kqv_in[0])
            load(0, 1, PARTS[2][1], kqv_in[1])
            with sp.Fori(0, PAIRS - 1) as pair:
                for i in range(2):
                    for j in range(NB):
                        store(pair, i * NB + j)
                    load(pair + 1, i, slice(0, S), kqv_in[i])
            for u in range(NU):
                store(PAIRS - 1, u)
            for i in range(2):
                sp.wait_ge(z_sent[i], 16 + PAIRS * NU // 2 * 16)

        @block.gpsimd
        def _(pool):
            pool.sem_inc(z_ready, 2)
            for i in range(2):
                pool.sem_inc(z_sent[i], 16)
            for n, (i, cols) in enumerate(PARTS):
                pool.memset(k1[i][DH:P, cols].bitcast(F32), 0.0).then_inc(k1_zero, 1)
                if n > 0:
                    pool.memset(q1[i][DH:P, cols].bitcast(F32), 0.0).then_inc(q1_fill, 1)
                pool.wait_ge(k1_zero, n + 1)
                if n > 0:
                    pool.wait_ge(q1_fill, n)
                pool.memset(k1[i][DH:DH + 1, cols].bitcast(F32), 1.0).then_inc(k1_fill, 1)
            pool.wait_ge(k1_fill, len(PARTS))

            with pool.Fori(0, PAIRS) as pair:
                def normalise(u):
                    k = u % 2
                    n = pair * NU + u
                    pool.wait_ge(z_copied, 2 + 2 * n + 2)
                    pool.tensor_tensor(zt[0][:, :, :], zs[k][:, :, VHI:VHI + DH],
                                       zs[k][:, :, VMID:VMID + DH], ALU.add).then_inc(z_chain, 1)
                    pool.wait_ge(z_chain, n * 2 + 1)
                    pool.tensor_tensor(zt[1][:, :, :], zt[0][:, :, :],
                                       zs[k][:, :, VLO:VLO + DH], ALU.add).then_inc(z_chain, 1)
                    pool.wait_ge(z_chain, n * 2 + 2)
                    pool.wait_ge(r_done, n + 1)
                    pool.wait_ge(z_sent[k], 16 * (pair * (NU // 2) + u // 2) + 16)
                    pool.tensor_tensor(zo[k][:, :, :], zt[1][:, :, :],
                                       rl[k][:, :].unsqueeze(2).broadcast_to([P, TPB, DH]),
                                       ALU.mult).then_inc(z_ready, 1)

                for g in range(NG):
                    if by_pool(g):
                        pool.wait_ge(exp_done, ST + pair * NG + g + 1)
                        pool.tensor_tensor(plo[g % PR][:, :], p32[g % PR][:, :],
                                           phi[g % PR][:, :], ALU.subtract)\
                            .then_inc(plo_pool, 1)
                    if g - LAG - 1 in LAST:
                        normalise(LAST.index(g - LAG - 1))
                normalise(NU - 1)

        @block.scalar
        def _(act):
            act.sem_inc(exp_done, ST)
            act.sem_inc(z_copied, 2)
            act.preload_act_table(ACT.Exp)
            with act.Fori(0, PAIRS) as pair:
                def copy_z(u, half):
                    act.wait_ge(pv_done, PR + pair * NG + LAST[u] - (0 if half else TAIL) + 1)
                    if half == 0:
                        act.wait_ge(z_ready, pair * NU + u + 1)
                    q = slice(2 * half, 2 * half + 2)
                    act.activation(zs[u % 2][:, q, 0:VW - 1], zp[:, q, 0:VW - 1], ACT.Copy)\
                       .then_inc(z_copied, 1)

                for g in range(NG):
                    w = width(g)
                    scores = st[g % ST][:, 0:w] if w > P else st[g % ST][:, P:2 * P]
                    act.wait_ge(st_done, pair * NG + g + 1)
                    act.wait_ge(pv_done, pair * NG + g + 1)
                    act.activation(phi[g % PR][:, 0:w], scores, ACT.Exp, scale=SCALE)
                    act.activation(p32[g % PR][:, 0:w], scores, ACT.Exp, scale=SCALE)\
                       .then_inc(exp_done, 1)
                    for half in range(2):
                        back = LAG - TAIL * (1 - half)
                        if g - back in LAST:
                            copy_z(LAST.index(g - back), half)
                for half in range(LAG <= TAIL, 2):
                    copy_z(NU - 1, half)

        @block.vector
        def _(dve):
            dve.sem_inc(sq_read, SQ)
            i, cols = PARTS[0]
            dve.memset(q1[i][DH:P, cols].bitcast(F32), 0.0).then_inc(q1_first, 1)
            dve.wait_ge(q1_first, 1)

            def item(pair, n):
                it = ORDER[n]
                u = it[1]
                head, j = divmod(u, NB)
                head %= 2
                dve.wait_ge(sq_done, pair * NI + n + 1)
                if it[0] == "max":
                    q, kb = it[2:]
                    dve.reduce_max(mpart[u % 2][:, q, kb:kb + 1],
                                   sq[n % SQ][:, 0:BLK if kb < j else (q + 1) * P],
                                   AX.X).then_inc(sq_read, 1)
                    if (q, kb) == (TPB - 1, j):
                        dve.wait_ge(sq_read, SQ + pair * NI + n + 1)
                        dve.reduce_max(m4[u % 2][:, :], mpart[u % 2][:, :, 0:j + 1], AX.X)\
                           .then_inc(m4_done, 1)
                else:
                    if u in ROW_FILLS:
                        dve.wait_ge(q1_fill, ROW_FILLS[u])
                    dve.tensor_scalar(q1[head][DH:DH + 1, j * BLK:(j + 1) * BLK],
                                      sq[n % SQ][0:1, :], -1.0, P_SHIFT, ALU.mult, ALU.add)\
                       .then_inc(sq_read, 1)

            def low_p(pair, g):
                w = width(g)
                if not by_pool(g):
                    dve.wait_ge(exp_done, ST + pair * NG + g + 1)
                    dve.tensor_tensor(plo[g % PR][:, 0:w], p32[g % PR][:, 0:w],
                                      phi[g % PR][:, 0:w], ALU.subtract).then_inc(plo_dve, 1)

            def inverse_sums(pair, u):
                dve.wait_ge(z_copied, 2 + 2 * (pair * NU + u) + 2)
                dve.reciprocal(rl[u % 2][:, :], zs[u % 2][:, :, VONE]).then_inc(r_done, 1)

            def iteration(pair, final):
                n = len(AHEAD)
                for g in range(NG):
                    mine = [m for m in range(n, n + len(CARRIED[g]))
                            if not (final and ORDER[m][1] >= NU)]
                    n += len(CARRIED[g])
                    cut = (len(mine) + 1) // 2
                    for m in mine[:cut]:
                        item(pair, m)
                    if g > 0:
                        low_p(pair, g - 1)
                    for m in mine[cut:]:
                        item(pair, m)
                    if g - LAG - 1 in LAST:
                        inverse_sums(pair, LAST.index(g - LAG - 1))
                low_p(pair, NG - 1)
                inverse_sums(pair, NU - 1)
                if LEFT and not final:
                    dve.wait_ge(sq_read, SQ + pair * NI + len(ORDER))
                    dve.sem_inc(sq_read, LEFT)

            for n in range(len(AHEAD)):
                item(0, n)
            with dve.Fori(0, PAIRS - 1) as pair:
                iteration(pair, False)
            iteration(PAIRS - 1, True)

        @block.tensor
        def _(pe):
            pe.sem_inc(pv_done, PR)

            def item(pair, n):
                it = ORDER[n]
                u = it[1]
                head, j = divmod(u, NB)
                if n == 0:
                    pe.wait_ge(early_in, LOADS * 16)
                elif it == ("max", NEXT, 0, 0) or it[0] == "max" and j == 0 and it[2:] == (0, 0):
                    pe.wait_ge(kqv_in[head % 2], (pair + 1 + head // 2) * (LOADS * 16))
                if it[0] == "max" and it[2:] == (0, 0) and u in ROW_FILLS:
                    pe.wait_ge(k1_fill, ROW_FILLS[u] + 1)
                    pe.wait_ge(q1_fill, ROW_FILLS[u])
                head %= 2
                pe.wait_ge(sq_read, pair * NI + n + 1)
                if it[0] == "max":
                    q, kb = it[2:]
                    w = BLK if kb < j else (q + 1) * P
                    wide = max(w, 2 * P)
                    last = pe.matmul(sq[n % SQ][:, 0:wide],
                                     qq[head][:, j * BLK + q * P:j * BLK + (q + 1) * P],
                                     kk[head][:, kb * BLK:kb * BLK + wide],
                                     start=True, stop=kb < j)
                    if kb == j:
                        last = pe.matmul(sq[n % SQ][:, w - P:w], sh.identb[:, :],
                                         sh.mask_qk[:, :], start=False, stop=True)
                else:
                    pe.wait_ge(m4_done, pair * NU + u + 1)
                    for q in range(TPB):
                        last = pe.transpose(sq[n % SQ][0:1, q * P:(q + 1) * P],
                                            m4[u % 2][:, q:q + 1], sh.identf[:, :])
                last.then_inc(sq_done, 1)

            def scores(g):
                u, head, j, kt, q0 = STEPS[g]
                q1st = min(q0, TPB - 2)
                at = (q0 - q1st) * P
                out = st[g % ST][:, 0:at + width(g)]
                keys = slice(kt * P, (kt + 1) * P)
                queries = slice(j * BLK + q1st * P, (j + 1) * BLK)
                pe.matmul(out, kk[head][:, keys], qq[head][:, queries], start=True, stop=False)
                last = pe.matmul(out, k1[head][:, keys], q1[head][:, queries],
                                 start=False, stop=kt < TPB * j)
                if kt >= TPB * j:
                    last = pe.matmul(st[g % ST][:, at:at + P], sh.identb[:, :],
                                     sh.mask_kq[:, :], start=False, stop=True)
                last.then_inc(st_done, 1)

            def p_v_waits(pair, g):
                if by_pool(g):
                    pe.wait_ge(plo_pool, pair * NPOOL + lows(g, True))
                else:
                    pe.wait_ge(plo_dve, pair * NDVE + lows(g, False))

            def p_v(pair, g):
                u, head, j, kt, q0 = STEPS[g]
                for q in range(q0, TPB):
                    c = (q - q0) * P
                    if g == FIRST[u] and q % 2 == 0:
                        pe.wait_ge(z_copied, 2 * (pair * NU + u) + q // 2 + 1)
                    pe.matmul(zp[:, q, 0:VW - 1], phi[g % PR][:, c:c + P],
                              v[head][:, kt, 0:VW - 1], start=(kt == 0 and q % 2 == 0),
                              stop=False, skip_group_check=True)
                    last = pe.matmul(zp[:, q, 0:VONE + 1], plo[g % PR][:, c:c + P],
                                     v[head][:, kt, 0:VONE + 1], start=False,
                                     stop=(g == LAST[u]), skip_group_check=True)
                last.then_inc(pv_done, 1)

            def iteration(pair, final):
                n = len(AHEAD)
                for g in range(NG):
                    u = STEPS[g][0]
                    if g == FIRST[u]:
                        pe.wait_ge(sq_read, SQ + pair * NI + ORDER.index(("row", u)) + 1)
                    pe.wait_ge(exp_done, pair * NG + g + 1)
                    scores(g)
                    for m in range(n, n + len(CARRIED[g])):
                        if not (final and ORDER[m][1] >= NU):
                            item(pair, m)
                    n += len(CARRIED[g])
                    if g >= LAG:
                        p_v_waits(pair, g - LAG)
                        p_v(pair, g - LAG)
                for g in range(NG - LAG, NG):
                    p_v_waits(pair, g)
                    p_v(pair, g)
                if LEFT and not final:
                    pe.sem_inc(sq_done, LEFT)

            for n in range(len(AHEAD)):
                item(0, n)
            pe.wait_ge(k1_fill, 1)
            pe.wait_ge(q1_first, 1)
            with pe.Fori(0, PAIRS - 1) as pair:
                iteration(pair, False)
            iteration(PAIRS - 1, True)


def mix_phase(nc, io, sh):
    with ExitStack() as ctx:
        def sb(name, shape, dt):
            return ctx.enter_context(nc.sbuf_tensor(name, shape, dt))

        def sem(name):
            return ctx.enter_context(nc.semaphore(name))

        def bank(name, shape=(P, 512)):
            return ctx.enter_context(nc.psum_tensor(name, list(shape), F32))

        raw = sb("mraw", [P, C, 512], F32)
        woh, wol = (sb(n, [P, C, D], F32R) for n in ("woh", "wol"))
        rw = sb("rw", [P, C, E], F32)
        rwh, rwl = (sb(n, [P, C, E], F32R) for n in ("rwh", "rwl"))
        rb = sb("rb", [E, 1], F32)
        ob = sb("ob", [P, D], F32)
        z = sb("z", [P, TPB, D], F32)
        zh, zl = ([sb(f"{n}{i}", [P, C, BLK], F32R) for i in range(2)] for n in ("zh", "zl"))
        xt = [sb(f"xt{i}", [P, TPB, D], F32) for i in range(2)]
        bst = sb("bst2", [P, TPB, 6], F32)
        mv = sb("mv2", [P, TPB, 2], F32)
        sd = sb("sd2", [P, TPB], F32)
        rstd = sb("rstd2", [P, TPB], F32)
        xhat = sb("xhat2", [P, TPB, D], F32)
        h = sb("h", [P, TPB, D], F32)
        hh, hl = (sb(n, [P, C, BLK], F32R) for n in ("hh2", "hl2"))
        tz = [bank(f"tz{i}") for i in range(2)]
        th = [bank(f"th{i}") for i in range(2)]
        acc = [bank(f"macc{i}") for i in range(2)]
        lgt = sb("lgt", [E, BLK], F32)
        lg = bank("lg")
        lt = bank("lt", (P, TPB, E))

        w_in = [sem(f"mw_in{i}") for i in range(3)]
        small_in = sem("small_in")
        z_in = sem("z_in")
        x_in = [sem(f"mx_in{i}") for i in range(2)]
        we_in = sem("we_in")
        w_scaled = sem("w_scaled")
        ow_scaled = sem("ow_scaled")
        ow_hi = sem("ow_hi")
        ow_lo = sem("ow_lo")
        w_hi = sem("mw_hi")
        w_lo = sem("mw_lo")
        obg_done = sem("obg_done")
        tz_done = sem("tz_done")
        z_high = sem("z_high")
        z_low = sem("z_low")
        acc_done = sem("macc_done")
        x1_done = sem("x1_done")
        bn_done = sem("bn_done2")
        bn_seen = sem("bn_seen2")
        mv_done = sem("mv_done2")
        sd_done = sem("sd_done2")
        rstd_done = sem("rstd_done2")
        xhat_done = sem("xhat_done2")
        h_done = sem("h_done")
        x1o_done = sem("x1o_done")
        x1_sent = sem("x1_sent")
        th_done = sem("th_done")
        h_high = sem("h_high2")
        h_low = sem("h_low2")
        h_sent = sem("h_sent")
        lg_done = sem("lg_done")
        lg_read = sem("lg_read")
        lt_done = sem("lt_done")
        lt_seen = sem("lt_seen")
        lt_read = sem("lt_read")

        block = ctx.enter_context(nc.Block())

        @block.sync
        def _(sp):
            sp.dma_start(z[:, :, :], io.z_scr[0]).then_inc(z_in, 16)
            sp.dma_start(raw[:, :, :], io.wo).then_inc(w_in[0], 16)
            sp.dma_start(xt[0][:, :, :], io.x[0]).then_inc(x_in[0], 16)
            sp.dma_start(rw[:, :, :], io.rw).then_inc(w_in[2], 16)
            sp.dma_start(rb[:, :], io.rb).then_inc(small_in, 16)
            sp.dma_start(ob[:, :], io.ob.broadcast_to([P, D])).then_inc(small_in, 16)
            sp.dma_start(xt[1][:, :, :], io.x[1]).then_inc(x_in[1], 16)
            sp.wait_ge(tz_done, C)
            sp.dma_start(z[:, :, :], io.z_scr[1]).then_inc(z_in, 16)
            sp.wait_ge(w_lo, C)
            sp.dma_start(raw[:, :, :], io.ow).then_inc(w_in[1], 16)
            sp.wait_ge(tz_done, 2 * C)
            sp.dma_start(z[:, :, :], io.z_scr[2]).then_inc(z_in, 16)

            def step(b, s, e, more_x, more_z):
                sp.wait_ge(h_done, b + 1)
                sp.dma_start(io.h_scr[bass.ds(b * BLK, BLK), :].rearrange("(t p) d -> p t d", p=P),
                             h[:, :, :]).then_inc(h_sent, 16)
                sp.wait_ge(x1o_done, b + 1)
                sp.dma_start(io.x1_scr[b], xt[s][:, :, :]).then_inc(x1_sent, 16)
                if more_z:
                    sp.wait_ge(tz_done, (b + 3) * C)
                    sp.dma_start(z[:, :, :], io.z_scr[b + 3]).then_inc(z_in, 16)
                if more_x:
                    sp.wait_ge(x1_sent, (b + 1) * 16)
                    sp.dma_start(xt[s][:, :, :], io.x[b + 2]).then_inc(x_in[s], 16)
                if s == 0:
                    sp.dma_start(sh.weraw[:, e, :, :], io.we[e]).then_inc(we_in, 16)

            with sp.Fori(0, NB // 2 - 2) as it:
                for s in range(2):
                    step(2 * it + s, s, it, True, True)
            for b in range(NB - 4, NB):
                step(b, b % 2, b // 2, b + 2 < NB, b + 3 < NB)
            sp.wait_ge(we_in, NB // 2 * 16)
            sp.wait_ge(x1_sent, NB * 16)
            sp.wait_ge(h_sent, 16 + NB * 16)

        @block.gpsimd
        def _(pool):
            pool.wait_ge(small_in, 32)
            pool.tensor_tensor(ob[:, :], ob[:, :], sh.gb[:, :], ALU.mult).then_inc(obg_done, 1)
            pool.wait_ge(obg_done, 1)

            def residual(b, s):
                pool.wait_ge(xhat_done, (b + 1) * TPB)
                for t in range(TPB):
                    last = pool.tensor_tensor(xt[s][:, t, :], xt[s][:, t, :], ob[:, :], ALU.add)
                last.then_inc(x1o_done, 1)

            pool.wait_ge(w_in[1], 16)
            for c in range(C):
                last = pool.tensor_tensor(raw[:, c, :], raw[:, c, :], sh.gb[:, :], ALU.mult)
            last.then_inc(ow_scaled, 1)
            residual(0, 0)
            residual(1, 1)
            pool.wait_ge(ow_hi, 1)
            pool.tensor_tensor(sh.owl[:, :, :], raw[:, :, :], sh.owh[:, :, :].bitcast(F32),
                               ALU.subtract).then_inc(ow_lo, 1)
            with pool.Fori(1, NB // 2) as it:
                for s in range(2):
                    residual(2 * it + s, s)

        @block.scalar
        def _(act):
            act.sem_inc(h_sent, 16)
            act.sem_inc(lg_read, 1)
            act.sem_inc(lt_read, 1)

            def z_high_part(b, s, c):
                if c == 0 and not (isinstance(b, int) and b < 2):
                    act.wait_ge(acc_done, (b - 1) * TPB)
                act.wait_ge(tz_done, b * C + c + 1)
                act.activation(zh[s][:, c, :], tz[c % 2][:, :], ACT.Copy).then_inc(z_high, 1)

            def deviation(b):
                act.wait_ge(mv_done, b + 1)
                act.activation(sd[:, :], mv[:, :, 1], ACT.Sqrt, bias=sh.eps[:, 0:1])\
                   .then_inc(sd_done, 1)

            def h_high_part(b, c):
                if c == 0 and not (isinstance(b, int) and b == 0):
                    act.wait_ge(lg_done, b)
                act.wait_ge(th_done, b * C + c + 1)
                act.activation(hh[:, c, :], th[c % 2][:, :], ACT.Copy).then_inc(h_high, 1)

            def logits_by_token(b):
                act.wait_ge(lt_done, b + 1)
                act.activation(sh.logits[:, bass.ds(b * TPB, TPB), :], lt[:, :, :], ACT.Copy)\
                   .then_inc(lt_read, 1)

            def logits(b):
                act.wait_ge(lg_done, b + 1)
                act.activation(lgt[:, :], lg[0:E, :], ACT.Identity, bias=rb[:, 0:1])\
                   .then_inc(lg_read, 1)

            def step(b, s, z, h, r):
                if h:
                    deviation(b - 1)
                if z:
                    z_high_part(b + 1, 1 - s, 0)
                    z_high_part(b + 1, 1 - s, 1)
                if r:
                    logits(b - 2)
                if h:
                    h_high_part(b - 1, 0)
                if z:
                    z_high_part(b + 1, 1 - s, 2)
                if h:
                    h_high_part(b - 1, 1)
                if z:
                    z_high_part(b + 1, 1 - s, 3)
                if h:
                    h_high_part(b - 1, 2)
                    h_high_part(b - 1, 3)
                if r:
                    logits_by_token(b - 2)

            for c in range(C):
                z_high_part(0, 0, c)
            for c in range(C):
                act.wait_ge(w_scaled, c + 1)
                act.activation(woh[:, c, :], raw[:, c, :], ACT.Copy).then_inc(w_hi, 1)
            act.wait_ge(w_in[2], 16)
            act.activation(rwh[:, :, :], rw[:, :, :], ACT.Copy).then_inc(w_hi, 1)
            act.wait_ge(small_in, 32)
            step(0, 0, True, False, False)
            step(1, 1, True, True, False)
            act.wait_ge(ow_scaled, 1)
            act.activation(sh.owh[:, :, :], raw[:, :, :], ACT.Copy).then_inc(ow_hi, 1)
            act.preload_act_table(ACT.Sqrt)
            with act.Fori(1, NB // 2 - 1) as it:
                for s in range(2):
                    step(2 * it + s, s, True, True, True)
            for s in range(2):
                step(NB - 2 + s, s, s == 0, True, True)
            step(NB, 0, False, True, True)
            logits(NB - 1)
            logits_by_token(NB - 1)

        @block.vector
        def _(dve):
            dve.sem_inc(z_low, 2)
            dve.sem_inc(x1_done, 2)
            dve.sem_inc(h_low, 2)

            def z_low_part(b, s, c):
                dve.wait_ge(z_high, b * C + c + 1)
                dve.tensor_tensor(zl[s][:, c, :], tz[c % 2][:, :], zh[s][:, c, :].bitcast(F32),
                                  ALU.subtract).then_inc(z_low, 1)

            def residual(b, s, t):
                dve.wait_ge(acc_done, b * TPB + t + 1)
                dve.tensor_tensor(xt[s][:, t, :], acc[t % 2][:, :], xt[s][:, t, :], ALU.add)\
                   .then_inc(x1_done, 1)
                dve.wait_ge(x1_done, 2 + b * TPB + t + 1)
                dve.bn_stats(bst[:, t, :], xt[s][:, t, :]).then_inc(bn_done, 1)

            def layer_norm(b, s):
                dve.wait_ge(bn_done, b * TPB + TPB)
                dve.sem_inc(bn_seen, 1)
                for t in range(TPB):
                    last = dve.bn_aggr(mv[:, t, :], bst[:, t, :])
                last.then_inc(mv_done, 1)
                dve.wait_ge(mv_done, b + 1)
                for t in range(TPB):
                    dve.scalar_tensor_tensor(xhat[:, t, :], xt[s][:, t, :], mv[:, t, 0:1],
                                             sh.cb1[:, :], ALU.subtract, ALU.mult)\
                       .then_inc(xhat_done, 1)
                dve.wait_ge(sd_done, b + 1)
                dve.reciprocal(rstd[:, :], sd[:, :]).then_inc(rstd_done, 1)
                dve.wait_ge(rstd_done, b + 1)
                dve.wait_ge(xhat_done, b * TPB + TPB)
                if not isinstance(b, int) or b > 0:
                    dve.wait_ge(th_done, b * C)
                dve.wait_ge(h_sent, b * 16 + 16)
                for t in range(TPB):
                    last = dve.scalar_tensor_tensor(h[:, t, :], xhat[:, t, :], rstd[:, t:t + 1],
                                                    sh.sb[:, :], ALU.mult, ALU.add)
                last.then_inc(h_done, 1)

            def h_low_part(b, c):
                dve.wait_ge(h_high, b * C + c + 1)
                dve.tensor_tensor(hl[:, c, :], th[c % 2][:, :], hh[:, c, :].bitcast(F32),
                                  ALU.subtract).then_inc(h_low, 1)

            def step(b, s, z, o, h, x_count):
                if h:
                    layer_norm(b - 1, 1 - s)
                if o:
                    dve.wait_ge(x_in[s], x_count)
                for t in range(TPB):
                    if z:
                        z_low_part(b + 1, 1 - s, t)
                    if o:
                        residual(b, s, t)
                    if h and t > 0:
                        h_low_part(b - 1, t - 1)
                if h:
                    h_low_part(b - 1, C - 1)

            for c in range(C):
                z_low_part(0, 0, c)
            dve.wait_ge(w_in[0], 16)
            for c in range(C):
                dve.tensor_tensor(raw[:, c, :], raw[:, c, :], sh.ga[:, :], ALU.mult)\
                   .then_inc(w_scaled, 1)
            for c in range(C):
                dve.wait_ge(w_hi, c + 1)
                dve.tensor_tensor(wol[:, c, :], raw[:, c, :], woh[:, c, :].bitcast(F32),
                                  ALU.subtract).then_inc(w_lo, 1)
            dve.wait_ge(w_hi, C + 1)
            dve.tensor_tensor(rwl[:, :, :], rw[:, :, :], rwh[:, :, :].bitcast(F32),
                              ALU.subtract).then_inc(w_lo, 1)
            step(0, 0, True, True, False, 16)
            step(1, 1, True, True, True, 16)
            with dve.Fori(1, NB // 2 - 1) as it:
                for s in range(2):
                    step(2 * it + s, s, True, True, True, it * 16 + 16)
            for s in range(2):
                step(NB - 2 + s, s, s == 0, True, True, NB // 2 * 16)
            step(NB, 0, False, False, True, 0)

        @block.tensor
        def _(pe):
            def z_turn(b, c):
                if c == 0:
                    pe.wait_ge(z_in, b * 16 + 16)
                pe.wait_ge(z_low, b * C + c + 1)
                for t in range(TPB):
                    last = pe.transpose(tz[c % 2][:, t * P:(t + 1) * P],
                                        z[:, t, c * P:(c + 1) * P], sh.identf[:, :])
                last.then_inc(tz_done, 1)

            def h_turn(b, c):
                if c == 0:
                    pe.wait_ge(h_done, b + 1)
                pe.wait_ge(h_low, b * C + c + 1)
                for t in range(TPB):
                    last = pe.transpose(th[c % 2][:, t * P:(t + 1) * P],
                                        h[:, t, c * P:(c + 1) * P], sh.identf[:, :])
                last.then_inc(th_done, 1)

            def attention_out(b, s, t):
                if t == 0:
                    pe.wait_ge(z_low, 2 + (b + 1) * C)
                pe.wait_ge(x1_done, b * TPB + t + 1)
                tok = slice(t * P, (t + 1) * P)
                three_terms(pe, acc[t % 2][:, :], lambda c: zh[s][:, c, tok],
                            lambda c: zl[s][:, c, tok], lambda c: woh[:, c, :],
                            lambda c: wol[:, c, :]).then_inc(acc_done, 1)

            def logits_turn(b):
                pe.wait_ge(lg_read, b + 2)
                pe.wait_ge(lt_read, b + 1)
                pe.sem_inc(lt_seen, 1)
                for t in range(TPB):
                    last = pe.transpose(lt[:, t, :], lgt[:, t * P:(t + 1) * P],
                                        sh.identf[0:E, 0:E])
                last.then_inc(lt_done, 1)

            def router(b):
                pe.wait_ge(h_low, 2 + (b + 1) * C)
                pe.wait_ge(lg_read, b + 1)
                three_terms(pe, lg[0:E, :], lambda c: rwh[:, c, :], lambda c: rwl[:, c, :],
                            lambda c: hh[:, c, :], lambda c: hl[:, c, :]).then_inc(lg_done, 1)

            def step(b, s, z, o, h, r):
                for t in range(TPB):
                    if z:
                        z_turn(b + 1, t)
                    if o:
                        attention_out(b, s, t)
                    if r and t == 0:
                        router(b - 2)
                    if h and t > 0:
                        h_turn(b - 1, t - 1)
                if r:
                    logits_turn(b - 2)
                if h:
                    h_turn(b - 1, C - 1)

            for c in range(C):
                z_turn(0, c)
            pe.wait_ge(w_lo, C)
            step(0, 0, True, True, False, False)
            pe.wait_ge(w_lo, C + 1)
            step(1, 1, True, True, True, False)
            with pe.Fori(1, NB // 2 - 1) as it:
                for s in range(2):
                    step(2 * it + s, s, True, True, True, True)
            for s in range(2):
                step(NB - 2 + s, s, s == 0, True, True, True)
            step(NB, 0, False, False, True, True)
            router(NB - 1)
            logits_turn(NB - 1)

def experts_phase(nc, io, sh):
    N2 = 2 * KT
    with ExitStack() as ctx:
        def sb(name, shape, dt=F32):
            return ctx.enter_context(nc.sbuf_tensor(name, shape, dt))

        def sem(name):
            return ctx.enter_context(nc.semaphore(name))

        wel = sb("wel", [P, E, C, D], F32R)
        weh = sb("weh", [P, E, C, D], F32R)
        eb = sb("eb", [P, E, D])
        rank = sb("rank", [P, E])
        ones = sb("ones", [P, P], BF16)
        before = sb("before", [P, P], BF16)
        count = sb("count", [P, P])
        token = sb("token", [P, N2])
        big = [sb(f"big{i}", [P, KT, E]) for i in range(6)]
        row = [sb(f"row{i}", [P, KT]) for i in range(6)]
        gate = sb("gate", [P, 2, KT])
        sel = sb("sel", [P, KT, E], BF16)
        PAD = KT // 2
        EPAD = E // 2
        escan = [sb(f"escan{i}", [P, EPAD + E]) for i in range(2)]
        load, tiles, start = (sb(n, [P, E]) for n in ("load", "tiles", "start"))
        texp = sb("texp", [P, NTILE])
        expert = sb("expert", [P, NTILE], I32)
        slot = sb("slot", [P, N2])
        sloti, slotr, slott = (sb(n, [P, N2], I32) for n in ("sloti", "slotr", "slott"))
        slotu = sb("slotu", [P, N2], U32)
        srow, stile = (sb(n, [P, N2]) for n in ("srow", "stile"))
        HOT = 4
        ids = sb("ids", [P, NTILE], U32)
        R4 = 4
        at = [sb(f"at{i}", [P, 1], U32) for i in range(R4)]
        at2 = [sb(f"at2_{i}", [P, 1], U32) for i in range(R4)]
        gl = [sb(f"gl{i}", [P, D]) for i in range(R4)]
        ya = [sh.ga, sh.gb, sh.sb, sh.cb1]
        yb = [sb(f"yb{i}", [P, D]) for i in range(R4)]
        rhot = [y[:, :].rearrange("p (n r) -> p n r", r=P) for y in ya]
        thot = [y[:, 0:HOT * NTILE].rearrange("p (n r) -> p n r", r=NTILE) for y in gl]
        scan = [y[:, 0:(PAD + KT) * E].rearrange("p (t e) -> p t e", e=E) for y in yb[0:2]]
        over = yb[2][:, 0:E * KT].rearrange("p (e t) -> p e t", t=KT)
        past = yb[3][:, 0:NTILE * (E - 1)].rearrange("p (t e) -> p t e", e=E - 1)
        hh = [sb(f"hh3_{i}", [P, C, P], F32R) for i in range(2)]
        hl = [sb(f"hl3_{i}", [P, C, P], F32R) for i in range(2)]
        tps = [ctx.enter_context(nc.psum_tensor(f"tps{i}", [P, C, P], F32)) for i in range(2)]
        acc = [ctx.enter_context(nc.psum_tensor(f"eacc{i}", [P, 512], F32)) for i in range(R4)]

        eb_in = sem("eb_in")
        fill_done = sem("fill_done3")
        const_mm = sem("const_mm")
        before_done = sem("before_done")
        chain = sem("chain")
        g_exp = sem("g_exp")
        rank_mm = sem("rank_mm")
        hot_tile = sem("hot_tile")
        hots = sem("hots")
        ids_mm = sem("ids_mm")
        ids_done = sem("ids_done")
        we_in = sem("we_in3")
        we_hi = sem("we_hi")
        we_lo = sem("we_lo")
        at_done = sem("at_done")
        at_seen = sem("at_seen")
        ya_in = [sem(f"ya_in{i}") for i in range(R4)]
        y_in = [sem(f"y_in{i}") for i in range(R4)]
        turned = sem("turned")
        high = sem("high")
        low = sem("low")
        acc_done = sem("eacc_done")
        acc_read = sem("eacc_read")
        gelu_done = sem("gelu_done")
        y_sent = [sem(f"y_sent{i}") for i in range(R4)]
        scaled = sem("scaled")
        combined = sem("combined")
        x1_in = [sem(f"x1_in{i}") for i in range(R4)]
        out_sent = [sem(f"out_sent{i}") for i in range(R4)]

        SEL_LINK = 17

        block = ctx.enter_context(nc.Block())

        def loop(eng, count, body):
            with eng.Fori(0, count // R4 - 1) as it:
                for k in range(R4):
                    body(it * R4 + k, it, k, True)
            for k in range(R4):
                body(count - R4 + k, count // R4 - 1, k, k < R4 - 1)

        @block.sync
        def _(sp):
            for e in range(NB // 2, E):
                sp.dma_start(sh.weraw[:, e, :, :], io.we[e]).then_inc(we_in, 16)
            sp.dma_start(eb[:, :, :], io.eb.unsqueeze(0).broadcast_to([P, E, D]))\
              .then_inc(eb_in, 16)

            def y_store(n, it, k, ahead):
                sp.wait_ge(gelu_done, n + 1)
                sp.dma_start(io.y_scr[bass.ds(n * P, P), :], gl[k][:, :]).then_inc(y_sent[k], 16)

            loop(sp, NTILE, y_store)
            for k in range(R4):
                sp.wait_ge(y_sent[k], 16 + NTILE // R4 * 16)
                sp.dma_start(gl[k][:, :], io.x1_scr[k // TPB, :, k % TPB, :])\
                  .then_inc(x1_in[k], 16)

            def result(n, b, t):
                sp.wait_ge(acc_read, R4 + NTILE + n + 1)
                sp.dma_start(io.out[b, :, t, :], gl[t][:, :]).then_inc(out_sent[t], 16)

            def next_x1(b, t):
                sp.wait_ge(out_sent[t], (b + 1) * 16)
                sp.dma_start(gl[t][:, :], io.x1_scr[b + 1, :, t, :]).then_inc(x1_in[t], 16)

            with sp.Fori(0, NB - 1) as b:
                result(b * TPB, b, 0)
                for t in range(1, TPB):
                    result(b * TPB + t, b, t)
                    next_x1(b, t - 1)
                next_x1(b, TPB - 1)
            for t in range(TPB):
                result((NB - 1) * TPB + t, NB - 1, t)
            for t in range(TPB):
                sp.wait_ge(out_sent[t], NB * 16)

        @block.gpsimd
        def _(pool):
            pool.memset(ones[:, :], 1.0).then_inc(fill_done, 1)
            for e in range(E):
                pool.memset(rank[:, e:e + 1], float(E - e)).then_inc(fill_done, 1)
            for t in scan:
                pool.memset(t[:, 0:PAD, :], 0.0).then_inc(fill_done, 1)
            for t in escan:
                pool.memset(t[:, 0:EPAD], 0.0).then_inc(fill_done, 1)
            for e in range(E):
                pool.wait_ge(we_hi, e + 1)
                pool.tensor_tensor(wel[:, e, :, :], sh.weraw[:, e, :, :],
                                   weh[:, e, :, :].bitcast(F32), ALU.subtract)\
                    .then_inc(we_lo, 1)

            pool.wait_ge(ids_done, 1)

            def gather_h(n, it, k, ahead):
                pool.wait_ge(turned, n + 1)
                pool.tensor_copy(at[k][:, :], ids[:, bass.ds(n, 1)]).then_inc(at_done, 1)
                pool.wait_ge(at_done, n + 1)
                pool.sem_inc(at_seen, 1)
                pool.indirect_dma_start(ya[k][:, :], None, io.h_scr,
                                        bass.IndirectOffsetOnAxis(ap=at[k][:, 0:1], axis=0))\
                    .then_inc(ya_in[k], 16)

            loop(pool, NTILE, gather_h)
            for k in range(R4):
                pool.wait_ge(y_sent[k], 16 + NTILE // R4 * 16)

            def gather_y(n, it, k, ahead):
                pool.wait_ge(turned, NTILE + n + 1)
                pool.tensor_copy(at[k][:, :], slotu[:, bass.ds(n, 1)]).then_inc(at_done, 1)
                pool.tensor_copy(at2[k][:, :], slotu[:, bass.ds(n + KT, 1)]).then_inc(at_done, 1)
                pool.wait_ge(at_done, NTILE + 2 * n + 2)
                pool.sem_inc(at_seen, 1)
                for y, rows in ((ya, at), (yb, at2)):
                    pool.indirect_dma_start(y[k][:, :], None, io.y_scr,
                                            bass.IndirectOffsetOnAxis(ap=rows[k][:, 0:1], axis=0))\
                        .then_inc(y_in[k], 16)

            loop(pool, KT, gather_y)

        @block.scalar
        def _(act):
            for k in range(R4):
                act.sem_inc(y_sent[k], 16)

            act.wait_ge(chain, 2)
            act.activation(big[2][:, :, :], big[1][:, :, :], ACT.Exp).then_inc(g_exp, 1)
            for e in range(E):
                if e >= NB // 2:
                    act.wait_ge(we_in, (E - NB // 2) * 16)
                act.activation(weh[:, e, :, :], sh.weraw[:, e, :, :], ACT.Copy)\
                   .then_inc(we_hi, 1)

            def part(n, k):
                act.wait_ge(turned, R4 + n + 1)
                act.wait_ge(acc_done, n + 1)
                act.activation(hh[k % 2][:, :, :], tps[k % 2][:, :, :], ACT.Copy)\
                   .then_inc(high, 1)

            def expert_step(n, it, k, ahead):
                if ahead:
                    part(n + 1, k + 1)
                act.wait_ge(acc_read, R4 + n + 1)
                act.activation(gl[k][:, :], gl[k][:, :], ACT.Gelu_apprx_tanh)\
                   .then_inc(gelu_done, 1)

            def scale(n, it, k):
                act.wait_ge(y_in[k], it * 32 + 32)
                act.activation(ya[k][:, :], ya[k][:, :], ACT.Copy,
                               scale=gate[:, 0, bass.ds(n, 1)]).then_inc(scaled, 1)

            act.preload_act_table(ACT.Gelu_apprx_tanh)
            part(0, 0)
            loop(act, NTILE, expert_step)
            scale(0, 0, 0)
            scale(1, 0, 1)
            part(NTILE, 0)

            def out_step(n, it, k, last):
                if not last or k < 2:
                    scale(n + 2, it + (k + 2) // R4, (k + 2) % R4)
                if not last or k < 3:
                    part(NTILE + n + 1, k + 1)

            with act.Fori(0, KT // R4 - 1) as it:
                for k in range(R4):
                    out_step(it * R4 + k, it, k, False)
            for k in range(R4):
                out_step(KT - R4 + k, KT // R4 - 1, k, True)

        @block.vector
        def _(dve):
            dve.sem_inc(low, 2)
            dve.sem_inc(acc_read, R4)
            dve.tensor_scalar(before[:, :], sh.mask_qk[:, :], 0.0, None, ALU.is_lt)\
               .then_inc(before_done, 1)

            n = [0]

            def link(ins):
                n[0] += 1
                ins.then_inc(chain, 1)
                dve.wait_ge(chain, n[0])

            def wide(r):
                return r.unsqueeze(2).broadcast_to([P, KT, E])

            link(dve.reduce_max(row[0][:, :], sh.logits[:, :, :], AX.X))
            link(dve.tensor_tensor(big[1][:, :, :], sh.logits[:, :, :], wide(row[0][:, :]),
                                   ALU.subtract))
            dve.wait_ge(g_exp, 1)
            link(dve.reduce_sum(row[1][:, :], big[2][:, :, :], AX.X))
            link(dve.reciprocal(row[2][:, :], row[1][:, :]))
            link(dve.tensor_tensor(big[0][:, :, :], big[2][:, :, :], wide(row[2][:, :]),
                                   ALU.mult))
            ranks = rank[:, :].unsqueeze(1).broadcast_to([P, KT, E])
            dve.wait_ge(fill_done, 1 + E + 4)

            def best(probs, value, chosen):
                link(dve.reduce_max(value[:, :], probs, AX.X))
                link(dve.tensor_tensor(big[1][:, :, :], probs, wide(value[:, :]), ALU.is_equal))
                link(dve.tensor_tensor(big[2][:, :, :], big[1][:, :, :], ranks, ALU.mult))
                link(dve.reduce_max(row[5][:, :], big[2][:, :, :], AX.X))
                link(dve.tensor_tensor(chosen, big[2][:, :, :], wide(row[5][:, :]),
                                       ALU.is_equal))

            first, second = big[3], big[5]
            best(big[0][:, :, :], row[0], first[:, :, :])
            link(dve.scalar_tensor_tensor(big[4][:, :, :], first[:, :, :], -2.0,
                                          big[0][:, :, :], ALU.mult, ALU.add))
            best(big[4][:, :, :], row[1], second[:, :, :])
            link(dve.tensor_tensor(sel[:, :, :], first[:, :, :], second[:, :, :], ALU.add))
            assert n[0] == SEL_LINK, n[0]
            link(dve.tensor_tensor(row[2][:, :], row[0][:, :], row[1][:, :], ALU.add))
            link(dve.reciprocal(row[3][:, :], row[2][:, :]))
            link(dve.tensor_tensor(gate[:, 0, :], row[0][:, :], row[3][:, :], ALU.mult))
            link(dve.tensor_tensor(gate[:, 1, :], row[1][:, :], row[3][:, :], ALU.mult))

            dve.wait_ge(const_mm, 1)
            link(dve.tensor_copy(count[:, :], acc[1][:, 0:P]))
            for i in range(2):
                link(dve.scalar_tensor_tensor(token[:, i * KT:(i + 1) * KT], count[:, 0:KT],
                                              float(P), acc[1][:, P:P + KT], ALU.mult, ALU.add))

            ahead_of, total = (acc[2][:, i * KT * E:(i + 1) * KT * E]
                               .rearrange("p (t e) -> p t e", e=E) for i in range(2))
            dve.wait_ge(rank_mm, 1)
            link(dve.tensor_copy(scan[0][:, PAD:, :], total))
            src, dst = scan
            shift = 1
            while shift < KT:
                link(dve.tensor_tensor(dst[:, PAD:, :], src[:, PAD:, :],
                                       src[:, PAD - shift:PAD + KT - shift, :], ALU.add))
                src, dst = dst, src
                shift *= 2
            upto = src
            link(dve.tensor_scalar(load[:, :], upto[:, PAD + KT - 1, :], 1.0 / P, None, ALU.mult))
            link(dve.tensor_tensor(over[:, :, :],
                                   count[:, 0:KT].unsqueeze(1).broadcast_to([P, E, KT]),
                                   load[:, :].unsqueeze(2).broadcast_to([P, E, KT]), ALU.is_lt))
            link(dve.reduce_sum(tiles[:, :], over[:, :, :], AX.X))
            link(dve.tensor_copy(escan[0][:, EPAD:], tiles[:, :]))
            esrc, edst = escan
            shift = 1
            while shift < E:
                link(dve.tensor_tensor(edst[:, EPAD:], esrc[:, EPAD:],
                                       esrc[:, EPAD - shift:EPAD + E - shift], ALU.add))
                esrc, edst = edst, esrc
                shift *= 2
            end = esrc[:, EPAD:]
            link(dve.tensor_tensor(start[:, :], end, tiles[:, :], ALU.subtract))
            link(dve.tensor_scalar(start[:, :], start[:, :], float(P), None, ALU.mult))
            link(dve.tensor_tensor(big[0][:, :, :], upto[:, PAD:, :], total, ALU.subtract))
            link(dve.tensor_tensor(big[1][:, :, :], big[0][:, :, :], ahead_of, ALU.add))
            link(dve.tensor_tensor(big[0][:, :, :], big[1][:, :, :],
                                   start[:, :].unsqueeze(1).broadcast_to([P, KT, E]), ALU.add))
            for i, chosen in enumerate((first, second)):
                link(dve.tensor_tensor(big[1][:, :, :], big[0][:, :, :], chosen[:, :, :],
                                       ALU.mult))
                link(dve.reduce_sum(slot[:, i * KT:(i + 1) * KT], big[1][:, :, :], AX.X))
            link(dve.tensor_copy(sloti[:, :], slot[:, :]))
            link(dve.tensor_scalar(slotr[:, :], sloti[:, :], P - 1, None, ALU.bitwise_and))
            link(dve.tensor_scalar(slott[:, :], sloti[:, :], P.bit_length() - 1, None,
                                   ALU.arith_shift_right))
            link(dve.tensor_copy(srow[:, :], slotr[:, :]))
            link(dve.tensor_copy(stile[:, :], slott[:, :]))

            def spread(column, width):
                return column.unsqueeze(2).broadcast_to([P, HOT, width])

            def numbers(width):
                return count[:, 0:width].unsqueeze(1).broadcast_to([P, HOT, width])

            def one_hots(g, k):
                n = bass.ds(g * HOT, HOT)
                dve.wait_ge(ids_mm, g + 1)
                dve.tensor_tensor(thot[k], numbers(NTILE), spread(stile[:, n], NTILE),
                                  ALU.is_equal).then_inc(hot_tile, 1)
                dve.tensor_tensor(rhot[k], numbers(P), spread(srow[:, n], P), ALU.is_equal)
                dve.wait_ge(hot_tile, g + 1)
                dve.tensor_tensor(thot[k], thot[k], spread(token[:, n], NTILE), ALU.mult)\
                   .then_inc(hots, 1)

            with dve.Fori(0, N2 // HOT // R4) as it:
                for k in range(R4):
                    one_hots(it * R4 + k, k)

            link(dve.tensor_copy(slotu[:, :], slot[:, :]))
            link(dve.tensor_tensor(past[:, :, :],
                                   end[:, 0:E - 1].unsqueeze(1).broadcast_to([P, NTILE, E - 1]),
                                   count[:, 0:NTILE].unsqueeze(2).broadcast_to([P, NTILE, E - 1]),
                                   ALU.is_le))
            link(dve.reduce_sum(texp[:, :], past[:, :, :], AX.X))
            link(dve.tensor_copy(expert[:, :], texp[:, :]))
            dve.wait_ge(ids_mm, R4 + N2 // HOT)
            dve.tensor_copy(ids[:, :], acc[3][:, 0:NTILE]).then_inc(ids_done, 1)

            def part(n, k):
                dve.wait_ge(high, n + 1)
                dve.tensor_tensor(hl[k % 2][:, :, :], tps[k % 2][:, :, :],
                                  hh[k % 2][:, :, :].bitcast(F32), ALU.subtract).then_inc(low, 1)

            def expert_step(n, it, k, ahead):
                if ahead:
                    part(n + 1, k + 1)
                e = dve.value_load(expert[0:1, bass.ds(n, 1)], min_val=0, max_val=E - 1)
                dve.wait_ge(acc_done, 2 + n + 1)
                dve.wait_ge(y_sent[k], it * 16 + 16)
                dve.tensor_tensor(gl[k][:, :], acc[k][:, :], eb[:, bass.ds(e, 1), :]
                                  .rearrange("p a d -> p (a d)"), ALU.add).then_inc(acc_read, 1)

            def combine(n, k):
                dve.wait_ge(scaled, n + 1)
                dve.scalar_tensor_tensor(yb[k][:, :], yb[k][:, :], gate[:, 1, bass.ds(n, 1)],
                                         ya[k][:, :], ALU.mult, ALU.add).then_inc(combined, 1)

            part(0, 0)
            dve.wait_ge(eb_in, 16)
            loop(dve, NTILE, expert_step)
            combine(0, 0)
            combine(1, 1)
            part(NTILE, 0)

            def out_step(n, it, k, last):
                if not last or k < 2:
                    combine(n + 2, (k + 2) % R4)
                if not last or k < 3:
                    part(NTILE + n + 1, k + 1)
                dve.wait_ge(acc_done, 2 + NTILE + n + 1)
                dve.wait_ge(x1_in[k], it * 16 + 16)
                dve.tensor_tensor(gl[k][:, :], acc[k][:, :], gl[k][:, :], ALU.add)\
                   .then_inc(acc_read, 1)

            with dve.Fori(0, KT // R4 - 1) as it:
                for k in range(R4):
                    out_step(it * R4 + k, it, k, False)
            for k in range(R4):
                out_step(KT - R4 + k, KT // R4 - 1, k, True)

        @block.tensor
        def _(pe):
            pe.sem_inc(turned, R4)
            pe.sem_inc(acc_done, 2)
            pe.sem_inc(ids_mm, R4)
            pe.wait_ge(fill_done, 1)
            pe.wait_ge(before_done, 1)
            pe.matmul(acc[1][:, 0:P], ones[:, :], before[:, :], start=True, stop=True)
            pe.matmul(acc[1][:, P:2 * P], before[:, :], ones[:, :], start=True, stop=True)\
              .then_inc(const_mm, 1)
            pe.wait_ge(chain, SEL_LINK)
            chosen = sel[:, :, :].rearrange("p t e -> p (t e)")
            pe.matmul(acc[2][:, 0:KT * E], before[:, :], chosen, start=True, stop=True)
            pe.matmul(acc[2][:, KT * E:2 * KT * E], ones[:, :], chosen, start=True, stop=True)\
              .then_inc(rank_mm, 1)

            def place(g, k, begin, end):
                pe.wait_ge(hots, g + 1)
                for n in range(HOT):
                    last = pe.matmul(acc[3][:, 0:NTILE], rhot[k][:, n, :], thot[k][:, n, :],
                                     start=begin and n == 0, stop=end and n == HOT - 1)
                last.then_inc(ids_mm, 1)

            groups = N2 // HOT
            for g in range(R4):
                place(g, g, g == 0, False)
            with pe.Fori(1, groups // R4 - 1) as it:
                for k in range(R4):
                    place(it * R4 + k, k, False, False)
            for k in range(R4):
                place(groups - R4 + k, k, False, k == R4 - 1)

            def turn(n, k, rows):
                pe.wait_ge(low, n + 1)
                for c in range(C):
                    last = pe.transpose(tps[k % 2][:, c, :], rows[k][:, c * P:(c + 1) * P],
                                        sh.identf[:, :])
                last.then_inc(turned, 1)

            def product(n, k, m_hi, m_lo):
                pe.wait_ge(low, 2 + n + 1)
                pe.wait_ge(acc_read, n + 1)
                three_terms(pe, acc[k][:, :], lambda c: hh[k % 2][:, c, :],
                            lambda c: hl[k % 2][:, c, :], m_hi, m_lo).then_inc(acc_done, 1)

            def gathered(it, k):
                pe.wait_ge(ya_in[k], it * 16 + 16)

            def expert_step(n, it, k, ahead):
                if ahead:
                    gathered(it + (k + 1) // R4, (k + 1) % R4)
                    turn(n + 1, (k + 1) % R4, ya)
                e = pe.value_load(expert[0:1, bass.ds(n, 1)], min_val=0, max_val=E - 1)
                product(n, k, lambda c: weh[:, bass.ds(e, 1), c, :],
                        lambda c: wel[:, bass.ds(e, 1), c, :])

            gathered(0, 0)
            turn(0, 0, ya)
            pe.wait_ge(we_lo, E)
            loop(pe, NTILE, expert_step)

            def out_step(n, it, k, ahead):
                if ahead:
                    pe.wait_ge(combined, n + 2)
                    turn(NTILE + n + 1, (k + 1) % R4, yb)
                product(NTILE + n, k, lambda c: sh.owh[:, c, :], lambda c: sh.owl[:, c, :])

            pe.wait_ge(combined, 1)
            turn(NTILE, 0, yb)
            loop(pe, KT, out_step)


class Holder:
    pass


def adaln_block(nc, arrays, out):
    io, sh = Holder(), Holder()

    def scratch(name, shape, dt=F32):
        return nc.dram_tensor(name, shape, dt, kind="Internal").ap()

    io.x = arrays["x"].rearrange("(b t p) d -> b p t d", t=TPB, p=P)
    io.out = out.rearrange("(b t p) d -> b p t d", t=TPB, p=P)
    io.c = arrays["c"]
    wide = "(c p) n -> p c n"
    io.wmod = [arrays["wmod"][:, m * D:(m + 1) * D].rearrange(wide, p=P) for m in range(6)]
    io.wk = [arrays["wk"].rearrange(wide, p=P)]
    io.wv = [arrays["wv"].rearrange(wide, p=P)]
    io.wq = [arrays["wq"][c * P:(c + 1) * P, :].rearrange("p (a n) -> p a n", a=C)
             for c in range(C)]
    io.wo = arrays["wo"].rearrange(wide, p=P)
    io.ow = arrays["ow"].rearrange(wide, p=P)
    io.we = arrays["we"].rearrange("e (c p) n -> e p c n", p=P)
    io.rw = arrays["rw"].rearrange(wide, p=P)
    io.rb, io.ob, io.eb = arrays["rb"], arrays["ob"], arrays["eb"]
    io.q_scr = scratch("q_scr", [2, PAIRS, P, S])
    io.k_scr = scratch("k_scr", [2, PAIRS, P, S])
    io.v_scr = scratch("v_scr", [P, HEADS, KT, VW], BF16)
    io.z_scr = scratch("z_scr", [NB, P, TPB, D])
    io.x1_scr = scratch("x1_scr", [NB, P, TPB, D])
    io.h_scr = scratch("h_scr", [S, D])
    io.y_scr = scratch("y_scr", [NTILE * P, D])

    with ExitStack() as ctx:
        def sb(name, shape, dt):
            return ctx.enter_context(nc.sbuf_tensor(name, shape, dt))

        sh.identf = sb("identf", [P, P], F32)
        sh.identb = sb("identb", [P, P], BF16)
        sh.mask_qk = sb("mask_qk", [P, P], BF16)
        sh.mask_kq = sb("mask_kq", [P, P], BF16)
        sh.eps = sb("eps", [P, 1], F32)
        sh.logits = sb("logits", [P, KT, E], F32)
        sh.ga, sh.gb, sh.sb, sh.cb1 = (sb(n, [P, D], F32) for n in ("ga", "gb", "sbv", "cb1"))
        project_phase(nc, io, sh)
        attend_phase(nc, io, sh)
        sh.owh, sh.owl = (sb(n, [P, C, D], F32R) for n in ("owh", "owl"))
        with nc.sbuf_tensor("weraw", [P, E, C, D], F32) as sh.weraw:
            mix_phase(nc, io, sh)
        experts_phase(nc, io, sh)


def kernel(**inputs):
    import numpy as np
    import concourse.bacc as bacc
    from concourse.bass_utils import run_bass_kernel_spmd

    f = {n.replace("L0_", ""): np.asarray(a) for n, a in inputs.items()}
    laid = {
        "x": f["attn_normalized_resid_pre"].reshape(S, D),
        "c": f["c"].reshape(C, P).T,
        "wmod": f["wmod"],
        "wq": f["attn_W_Q"].transpose(1, 0, 2).reshape(D, HEADS * GROUP * DH),
        "wk": f["attn_W_K"].transpose(1, 0, 2).reshape(D, HEADS * DH),
        "wv": f["attn_W_V"].transpose(1, 0, 2).reshape(D, HEADS * DH),
        "wo": f["attn_W_O"].reshape(HEADS * DH, D),
        "rw": f["ffn_router_w"],
        "rb": f["ffn_router_b"].reshape(E, 1),
        "we": f["ffn_expert_w"],
        "eb": f["ffn_expert_b"],
        "ow": f["ffn_out_w"],
        "ob": f["ffn_out_b"].reshape(1, D),
    }
    laid = {n: np.ascontiguousarray(a) for n, a in laid.items()}
    nc = bacc.Bacc("TRN2", target_bir_lowering=False, num_devices=1)
    aps = {n: nc.dram_tensor(f"in_{n}", a.shape, mybir.dt.from_np(a.dtype),
                             kind="ExternalInput").ap() for n, a in laid.items()}
    out = nc.dram_tensor("out", [S, D], F32, kind="ExternalOutput").ap()
    adaln_block(nc, aps, out)
    r = run_bass_kernel_spmd(nc, [{f"in_{n}": a for n, a in laid.items()}], core_ids=[0])
    return r.results[0]["out"].reshape(1, S, D)
```
